# Optimizing a Trainium2 kernel written in Bass

```python
import numpy as np
import jax
import jax.numpy as jnp

def _softmax(x, axis=-1):
    return jax.nn.softmax(x, axis=axis)

def _gelu(x):
    return jax.nn.gelu(x, approximate=True)

def _silu(x):
    return jax.nn.silu(x)

def _sigmoid(x):
    return jax.nn.sigmoid(x)

def _layernorm(x, axis=-1, eps=1e-05):
    m = jnp.mean(x, axis=axis, keepdims=True)
    v = jnp.var(x, axis=axis, keepdims=True)
    return (x - m) / jnp.sqrt(v + eps)

def _scatter_add(tgt, idx, src, axis=0):
    return tgt.at[idx].add(src)

def _segment_sum(src, seg, n):
    return jax.ops.segment_sum(src, seg, n)
kernel_name = 'mk_xattn_ffn_d4_seqx_r8_0e4c9c'

def setup_inputs(seed: int=0):
    np.random.seed(seed)
    _w = jnp.asarray

    def _rec_inputs():
        import jax
        import jax.numpy as jnp
        _rk = jax.random.key(seed)
        x = -0.0002928 + 1 * jax.random.normal(jax.random.fold_in(_rk, 1), (4, 256, 128), jnp.float32)
        _lenS = 256 - jax.random.randint(jax.random.fold_in(_rk, 7), (4,), 0, max(1, 256 // 4) + 1, jnp.int32)
        _lenS2 = 64 - jax.random.randint(jax.random.fold_in(_rk, 8), (4,), 0, max(1, 64 // 4) + 1, jnp.int32)
        _ctx_1024P = jax.random.normal(jax.random.fold_in(_rk, 11), (4, 16, 128), jnp.float32)
        _ctx_1024c = jax.random.dirichlet(jax.random.fold_in(_rk, 511), 0.3 * jnp.ones((16,), jnp.float32), (4, 64))
        _ctx_1024t = jnp.einsum('bsk,bkd->bsd', _ctx_1024c, _ctx_1024P)
        _ctx_1024t = _ctx_1024t * jax.lax.rsqrt(jnp.mean(jnp.square(_ctx_1024t)) + 1e-12) * 0.953939
        ctx_1024 = -1.39393e-06 + 0.999914 * (_ctx_1024t + 0.3 * jax.random.normal(jax.random.fold_in(_rk, 611), (4, 64, 128), jnp.float32))
        _validS = jnp.arange(256)[None, :] < _lenS[:, None]
        _validS2 = jnp.arange(64)[None, :] < _lenS2[:, None]
        _causal = jnp.tril(jnp.ones((256, 256), dtype=bool))
        mask_BxS2_bk0 = jnp.logical_not(jnp.broadcast_to(_validS2[:, :], (4, 64)))
        return (x, ctx_1024, mask_BxS2_bk0)
    x, ctx_1024, mask_BxS2_bk0 = _rec_inputs()

    def _L0_xattn_setup():
        import jax, jax.numpy as jnp
        import numpy as np
        import math
        D_MODEL = 128
        N_HEADS = 16
        HEAD_DIM = D_MODEL // N_HEADS
        TOP_K = 32
        SCALE = math.sqrt(HEAD_DIM)

        def _split_heads(t, n):
            B, L, _ = t.shape
            return t.reshape(B, L, N_HEADS, HEAD_DIM).transpose(0, 2, 1, 3)
        key = jax.random.key(seed)
        ks = jax.random.split(key, 12)
        B, S, N = (2, 256, 256)
        std = 1.0 / math.sqrt(D_MODEL)
        inp = {'x': jax.random.normal(ks[0], (B, S, D_MODEL), dtype=jnp.float32), 'knowledge_embeddings': jax.random.normal(ks[1], (B, N, D_MODEL), dtype=jnp.float32), 'Wq': jax.random.normal(ks[2], (D_MODEL, D_MODEL), dtype=jnp.float32) * std, 'bq': jnp.zeros((D_MODEL,), dtype=jnp.float32), 'Wk': jax.random.normal(ks[3], (D_MODEL, D_MODEL), dtype=jnp.float32) * std, 'bk': jnp.zeros((D_MODEL,), dtype=jnp.float32), 'Wv': jax.random.normal(ks[4], (D_MODEL, D_MODEL), dtype=jnp.float32) * std, 'bv': jnp.zeros((D_MODEL,), dtype=jnp.float32), 'Wo': jax.random.normal(ks[5], (D_MODEL, D_MODEL), dtype=jnp.float32) * std, 'bo': jnp.zeros((D_MODEL,), dtype=jnp.float32)}
        return inp
    _L0_xattn_all = _L0_xattn_setup()
    _L0_xattn_in = {k: v for k, v in _L0_xattn_all.items() if k in ('Wq', 'bq', 'Wk', 'bk', 'Wv', 'bv', 'Wo', 'bo')}
    del _L0_xattn_all

    def _L0_ffn_setup():
        import jax, jax.numpy as jnp
        import numpy as np
        D_MODEL = 128
        N_EXPERTS = 8
        TOP_K = 2
        key = jax.random.key(seed)
        k1, k2, k3, k4 = jax.random.split(key, 4)
        B, S, D, E = (4, 256, D_MODEL, N_EXPERTS)
        dff = 4 * D
        lim = float(np.sqrt(6.0 / (D + dff)))
        return {'x': jax.random.normal(k1, (B, S, D), dtype=jnp.float32), 'router_w': jax.random.normal(k2, (D, E), dtype=jnp.float32) * (1.0 / np.sqrt(D)), 'router_b': jnp.zeros((E,), dtype=jnp.float32), 'expert_up': jax.random.uniform(k3, (E, dff, D), dtype=jnp.float32, minval=-lim, maxval=lim), 'expert_down': jax.random.uniform(k4, (E, D, dff), dtype=jnp.float32, minval=-lim, maxval=lim)}
    _L0_ffn_all = _L0_ffn_setup()
    _L0_ffn_in = {k: v for k, v in _L0_ffn_all.items() if k in ('router_w', 'router_b', 'expert_up', 'expert_down')}
    del _L0_ffn_all

    def _L1_xattn_setup():
        import jax, jax.numpy as jnp
        import numpy as np
        DIM = 128
        HEAD_DIM = 64
        NUM_HEADS = 8
        INNER = HEAD_DIM * NUM_HEADS
        ROT_DIM = HEAD_DIM
        ROPE_BASE = 10000.0
        EPS = 1e-05

        def layer_norm(x, g, b):
            mu = jnp.mean(x, axis=-1, keepdims=True)
            var = jnp.var(x, axis=-1, keepdims=True)
            return (x - mu) * jax.lax.rsqrt(var + EPS) * g + b

        def rope_rotate_k(k):
            n = k.shape[1]
            half = ROT_DIM // 2
            inv_freq = 1.0 / ROPE_BASE ** (jnp.arange(0, ROT_DIM, 2, dtype=jnp.float32) / ROT_DIM)
            theta = jnp.arange(n, dtype=jnp.float32)[:, None] * inv_freq[None, :]
            angles = jnp.concatenate([theta, theta], axis=-1)
            cos = jnp.cos(angles)[None, :, None, :].astype(k.dtype)
            sin = jnp.sin(angles)[None, :, None, :].astype(k.dtype)
            k_rope, k_pass = (k[..., :ROT_DIM], k[..., ROT_DIM:])
            neg_half = jnp.concatenate([-k_rope[..., half:], k_rope[..., :half]], axis=-1)
            k_rope = k_rope * cos + neg_half * sin
            return jnp.concatenate([k_rope, k_pass], axis=-1)
        key = jax.random.key(seed)
        ks = jax.random.split(key, 5)
        b, n, m = (8, 1024, 64)
        s = 1.0 / np.sqrt(DIM)
        return {'x': jax.random.normal(ks[0], (b, n, DIM), jnp.float32), 'latents': jax.random.normal(ks[1], (b, m, DIM), jnp.float32), 'gamma_x': jnp.ones((DIM,), jnp.float32), 'beta_x': jnp.zeros((DIM,), jnp.float32), 'gamma_l': jnp.ones((DIM,), jnp.float32), 'beta_l': jnp.zeros((DIM,), jnp.float32), 'Wq': jax.random.normal(ks[2], (DIM, INNER), jnp.float32) * s, 'Wkv': jax.random.normal(ks[3], (DIM, 2 * INNER), jnp.float32) * s, 'Wo': jax.random.normal(ks[4], (INNER, DIM), jnp.float32) * (1.0 / np.sqrt(INNER))}
    _L1_xattn_all = _L1_xattn_setup()
    _L1_xattn_in = {k: v for k, v in _L1_xattn_all.items() if k in ('gamma_x', 'beta_x', 'gamma_l', 'beta_l', 'Wq', 'Wkv', 'Wo')}
    del _L1_xattn_all

    def _L1_ffn_setup():
        import jax, jax.numpy as jnp
        import numpy as np
        D_MODEL, D_FF, N_EXP = (128, 512, 8)
        key = jax.random.key(seed)
        ks = jax.random.split(key, 8)
        s = lambda fan_in: 1.0 / np.sqrt(fan_in)
        x = jax.random.normal(ks[0], (4, 256, D_MODEL), dtype=jnp.float32)
        Wr = jax.random.uniform(ks[1], (N_EXP, D_MODEL), jnp.float32, -s(D_MODEL), s(D_MODEL))
        br = jax.random.uniform(ks[2], (N_EXP,), jnp.float32, -s(D_MODEL), s(D_MODEL))
        W1 = jax.random.uniform(ks[3], (N_EXP, D_FF, D_MODEL), jnp.float32, -s(D_MODEL), s(D_MODEL))
        b1 = jax.random.uniform(ks[4], (N_EXP, D_FF), jnp.float32, -s(D_MODEL), s(D_MODEL))
        W2 = jax.random.uniform(ks[5], (N_EXP, D_MODEL, D_FF), jnp.float32, -s(D_FF), s(D_FF))
        b2 = jax.random.uniform(ks[6], (N_EXP, D_MODEL), jnp.float32, -s(D_FF), s(D_FF))
        return {'x': x, 'Wr': Wr, 'br': br, 'W1': W1, 'b1': b1, 'W2': W2, 'b2': b2}
    _L1_ffn_all = _L1_ffn_setup()
    _L1_ffn_in = {k: v for k, v in _L1_ffn_all.items() if k in ('Wr', 'br', 'W1', 'b1', 'W2', 'b2')}
    del _L1_ffn_all

    def _L2_xattn_setup():
        import jax, jax.numpy as jnp
        import numpy as np
        EPS = 1e-05

        def layer_norm(x, g, b):
            mu = jnp.mean(x, axis=-1, keepdims=True)
            var = jnp.mean((x - mu) ** 2, axis=-1, keepdims=True)
            return (x - mu) * jax.lax.rsqrt(var + EPS) * g + b
        key = jax.random.key(seed)
        ks = jax.random.split(key, 8)
        b, n, l, D = (8, 512, 64, 128)
        heads, dim_head = (16, 64)
        inner = heads * dim_head
        x = jax.random.normal(ks[0], (b, n, D), dtype=jnp.float32)
        latents = jax.random.normal(ks[1], (b, l, D), dtype=jnp.float32)
        mask = jax.random.randint(ks[2], (b, n), 0, 2) > 0
        Wq = jax.random.normal(ks[3], (D, inner), dtype=jnp.float32) * D ** (-0.5)
        Wkv = jax.random.normal(ks[4], (D, 2 * inner), dtype=jnp.float32) * D ** (-0.5)
        Wout = jax.random.normal(ks[5], (inner, D), dtype=jnp.float32) * inner ** (-0.5)
        g1 = jnp.ones((D,), jnp.float32)
        b1 = jnp.zeros((D,), jnp.float32)
        g2 = jnp.ones((D,), jnp.float32)
        b2 = jnp.zeros((D,), jnp.float32)
        return {'x': x, 'latents': latents, 'mask': mask, 'g1': g1, 'b1': b1, 'g2': g2, 'b2': b2, 'Wq': Wq, 'Wkv': Wkv, 'Wout': Wout}
    _L2_xattn_all = _L2_xattn_setup()
    _L2_xattn_in = {k: v for k, v in _L2_xattn_all.items() if k in ('g1', 'b1', 'g2', 'b2', 'Wq', 'Wkv', 'Wout')}
    del _L2_xattn_all

    def _L2_ffn_setup():
        import jax, jax.numpy as jnp
        import numpy as np
        B, S, H, F, E, K = (2, 256, 128, 512, 8, 2)

        def _ln(x, g, b, eps=1e-05):
            m = jnp.mean(x, axis=-1, keepdims=True)
            v = jnp.var(x, axis=-1, keepdims=True)
            return (x - m) / jnp.sqrt(v + eps) * g + b

        def _gelu(x):
            return jax.nn.gelu(x, approximate=False)
        key = jax.random.key(seed)
        ks = jax.random.split(key, 12)
        F2 = F // 2
        return {'hidden_states': jax.random.normal(ks[0], (B, S, H), jnp.float32), 'ln_g': jnp.ones((H,), jnp.float32), 'ln_b': jnp.zeros((H,), jnp.float32), 'router_w': jax.random.normal(ks[1], (H, E), jnp.float32) * 0.01, 'up_W': jax.random.normal(ks[2], (E, H, F), jnp.float32) * 0.02, 'up_b': jnp.zeros((E, F), jnp.float32), 'down_W': jax.random.normal(ks[3], (E, F, H), jnp.float32) * 0.02, 'down_b': jnp.zeros((E, H), jnp.float32), 'spec0_W': jax.random.normal(ks[4], (2, F, F), jnp.float32) * 0.02, 'spec0_b': jnp.zeros((2, F), jnp.float32), 'ln0_g': jnp.ones((2, F), jnp.float32), 'ln0_b': jnp.zeros((2, F), jnp.float32), 'spec1a_W': jax.random.normal(ks[5], (2, F, F2), jnp.float32) * 0.02, 'spec1a_b': jnp.zeros((2, F2), jnp.float32), 'spec1b_W': jax.random.normal(ks[6], (2, F2, F), jnp.float32) * 0.02, 'spec1b_b': jnp.zeros((2, F), jnp.float32), 'ln1_g': jnp.ones((2, F), jnp.float32), 'ln1_b': jnp.zeros((2, F), jnp.float32), 'spec2_W': jax.random.normal(ks[7], (2, F, F), jnp.float32) * 0.02, 'spec2_b': jnp.zeros((2, F), jnp.float32)}
    _L2_ffn_all = _L2_ffn_setup()
    _L2_ffn_in = {k: v for k, v in _L2_ffn_all.items() if k in ('ln_g', 'ln_b', 'router_w', 'up_W', 'up_b', 'down_W', 'down_b', 'spec0_W', 'spec0_b', 'ln0_g', 'ln0_b', 'spec1a_W', 'spec1a_b', 'spec1b_W', 'spec1b_b', 'ln1_g', 'ln1_b', 'spec2_W', 'spec2_b')}
    del _L2_ffn_all

    def _L3_xattn_setup():
        import jax, jax.numpy as jnp
        import numpy as np
        NUM_HEADS, NUM_KV, HEAD_DIM, WIDTH = (4, 1, 32, 128)
        MASK_FILL = -2.3819763e+38

        def _apply_rope(x, positions, max_wavelength=10000.0):
            d = x.shape[-1]
            freq_exp = 2.0 / d * jnp.arange(d // 2, dtype=jnp.float32)
            timescale = max_wavelength ** freq_exp
            radians = positions[..., None].astype(jnp.float32) / timescale
            radians = radians[..., None, :]
            sin, cos = (jnp.sin(radians), jnp.cos(radians))
            x1, x2 = jnp.split(x, 2, axis=-1)
            out = jnp.concatenate([x1 * cos - x2 * sin, x2 * cos + x1 * sin], axis=-1)
            return out.astype(x.dtype)

        def _rmsnorm(x, scale):
            var = jnp.mean(jnp.square(x.astype(jnp.float32)), axis=-1, keepdims=True)
            normed = x * jax.lax.rsqrt(var + 1e-06)
            return (normed * (1 + scale)).astype(x.dtype)
        key = jax.random.key(seed)
        ks = jax.random.split(key, 7)
        B, T, S = (8, 64, 256)
        return {'x': jax.random.normal(ks[0], (B, T, WIDTH), jnp.float32), 'mem_seq': jax.random.normal(ks[1], (B, S, WIDTH), jnp.float32), 'mem_mask': jax.random.randint(ks[2], (B, S), 0, 2).astype(bool), 'rms_scale': jax.random.normal(ks[3], (WIDTH,), jnp.float32) * 0.02, 'q_w': jax.random.normal(ks[4], (NUM_HEADS, WIDTH, HEAD_DIM), jnp.float32) / np.sqrt(WIDTH), 'kv_w': jax.random.normal(ks[5], (2, NUM_KV, WIDTH, HEAD_DIM), jnp.float32) / np.sqrt(WIDTH), 'out_w': jax.random.normal(ks[6], (NUM_HEADS, HEAD_DIM, WIDTH), jnp.float32) / np.sqrt(NUM_HEADS * HEAD_DIM)}
    _L3_xattn_all = _L3_xattn_setup()
    _L3_xattn_in = {k: v for k, v in _L3_xattn_all.items() if k in ('rms_scale', 'q_w', 'kv_w', 'out_w')}
    del _L3_xattn_all

    def _L3_ffn_setup():
        import jax, jax.numpy as jnp
        import numpy as np
        DIM = 128
        HID = 512
        NUM_EXPERTS = 8
        TOP_K = 2
        ALPHA = 2.0
        B, S = (4, 256)

        def _swiglu(x, wu, wg, wd):
            up = x @ wu
            g = x @ wg
            gate = jax.nn.sigmoid(g) * g
            return up * gate @ wd
        key = jax.random.key(seed)
        ks = jax.random.split(key, 8)
        x = jax.random.normal(ks[0], (B, S, DIM), dtype=jnp.float32)
        Wr = jax.random.normal(ks[1], (DIM, NUM_EXPERTS), dtype=jnp.float32) * 0.02
        Wu = jax.random.normal(ks[2], (NUM_EXPERTS - 1, DIM, HID), dtype=jnp.float32) * 0.02
        Wg = jax.random.normal(ks[3], (NUM_EXPERTS - 1, DIM, HID), dtype=jnp.float32) * 0.02
        Wd = jax.random.normal(ks[4], (NUM_EXPERTS - 1, HID, DIM), dtype=jnp.float32) * 0.002
        Wu_s = jax.random.normal(ks[5], (DIM, HID), dtype=jnp.float32) * 0.02
        Wg_s = jax.random.normal(ks[6], (DIM, HID), dtype=jnp.float32) * 0.02
        Wd_s = jax.random.normal(ks[7], (HID, DIM), dtype=jnp.float32) * 0.002
        return {'x': x, 'Wr': Wr, 'Wu': Wu, 'Wg': Wg, 'Wd': Wd, 'Wu_s': Wu_s, 'Wg_s': Wg_s, 'Wd_s': Wd_s}
    _L3_ffn_all = _L3_ffn_setup()
    _L3_ffn_in = {k: v for k, v in _L3_ffn_all.items() if k in ('Wr', 'Wu', 'Wg', 'Wd', 'Wu_s', 'Wg_s', 'Wd_s')}
    del _L3_ffn_all
    return {'x': x, 'ctx_1024': ctx_1024, 'mask_BxS2_bk0': mask_BxS2_bk0, 'L0_xattn_Wq': _L0_xattn_in['Wq'], 'L0_xattn_bq': _L0_xattn_in['bq'], 'L0_xattn_Wk': _L0_xattn_in['Wk'], 'L0_xattn_bk': _L0_xattn_in['bk'], 'L0_xattn_Wv': _L0_xattn_in['Wv'], 'L0_xattn_bv': _L0_xattn_in['bv'], 'L0_xattn_Wo': _L0_xattn_in['Wo'], 'L0_xattn_bo': _L0_xattn_in['bo'], 'L0_ffn_router_w': _L0_ffn_in['router_w'], 'L0_ffn_router_b': _L0_ffn_in['router_b'], 'L0_ffn_expert_up': _L0_ffn_in['expert_up'], 'L0_ffn_expert_down': _L0_ffn_in['expert_down'], 'L1_xattn_gamma_x': _L1_xattn_in['gamma_x'], 'L1_xattn_beta_x': _L1_xattn_in['beta_x'], 'L1_xattn_gamma_l': _L1_xattn_in['gamma_l'], 'L1_xattn_beta_l': _L1_xattn_in['beta_l'], 'L1_xattn_Wq': _L1_xattn_in['Wq'], 'L1_xattn_Wkv': _L1_xattn_in['Wkv'], 'L1_xattn_Wo': _L1_xattn_in['Wo'], 'L1_ffn_Wr': _L1_ffn_in['Wr'], 'L1_ffn_br': _L1_ffn_in['br'], 'L1_ffn_W1': _L1_ffn_in['W1'], 'L1_ffn_b1': _L1_ffn_in['b1'], 'L1_ffn_W2': _L1_ffn_in['W2'], 'L1_ffn_b2': _L1_ffn_in['b2'], 'L2_xattn_g1': _L2_xattn_in['g1'], 'L2_xattn_b1': _L2_xattn_in['b1'], 'L2_xattn_g2': _L2_xattn_in['g2'], 'L2_xattn_b2': _L2_xattn_in['b2'], 'L2_xattn_Wq': _L2_xattn_in['Wq'], 'L2_xattn_Wkv': _L2_xattn_in['Wkv'], 'L2_xattn_Wout': _L2_xattn_in['Wout'], 'L2_ffn_ln_g': _L2_ffn_in['ln_g'], 'L2_ffn_ln_b': _L2_ffn_in['ln_b'], 'L2_ffn_router_w': _L2_ffn_in['router_w'], 'L2_ffn_up_W': _L2_ffn_in['up_W'], 'L2_ffn_up_b': _L2_ffn_in['up_b'], 'L2_ffn_down_W': _L2_ffn_in['down_W'], 'L2_ffn_down_b': _L2_ffn_in['down_b'], 'L2_ffn_spec0_W': _L2_ffn_in['spec0_W'], 'L2_ffn_spec0_b': _L2_ffn_in['spec0_b'], 'L2_ffn_ln0_g': _L2_ffn_in['ln0_g'], 'L2_ffn_ln0_b': _L2_ffn_in['ln0_b'], 'L2_ffn_spec1a_W': _L2_ffn_in['spec1a_W'], 'L2_ffn_spec1a_b': _L2_ffn_in['spec1a_b'], 'L2_ffn_spec1b_W': _L2_ffn_in['spec1b_W'], 'L2_ffn_spec1b_b': _L2_ffn_in['spec1b_b'], 'L2_ffn_ln1_g': _L2_ffn_in['ln1_g'], 'L2_ffn_ln1_b': _L2_ffn_in['ln1_b'], 'L2_ffn_spec2_W': _L2_ffn_in['spec2_W'], 'L2_ffn_spec2_b': _L2_ffn_in['spec2_b'], 'L3_xattn_rms_scale': _L3_xattn_in['rms_scale'], 'L3_xattn_q_w': _L3_xattn_in['q_w'], 'L3_xattn_kv_w': _L3_xattn_in['kv_w'], 'L3_xattn_out_w': _L3_xattn_in['out_w'], 'L3_ffn_Wr': _L3_ffn_in['Wr'], 'L3_ffn_Wu': _L3_ffn_in['Wu'], 'L3_ffn_Wg': _L3_ffn_in['Wg'], 'L3_ffn_Wd': _L3_ffn_in['Wd'], 'L3_ffn_Wu_s': _L3_ffn_in['Wu_s'], 'L3_ffn_Wg_s': _L3_ffn_in['Wg_s'], 'L3_ffn_Wd_s': _L3_ffn_in['Wd_s']}

def reference(x, ctx_1024, mask_BxS2_bk0, L0_xattn_Wq, L0_xattn_bq, L0_xattn_Wk, L0_xattn_bk, L0_xattn_Wv, L0_xattn_bv, L0_xattn_Wo, L0_xattn_bo, L0_ffn_router_w, L0_ffn_router_b, L0_ffn_expert_up, L0_ffn_expert_down, L1_xattn_gamma_x, L1_xattn_beta_x, L1_xattn_gamma_l, L1_xattn_beta_l, L1_xattn_Wq, L1_xattn_Wkv, L1_xattn_Wo, L1_ffn_Wr, L1_ffn_br, L1_ffn_W1, L1_ffn_b1, L1_ffn_W2, L1_ffn_b2, L2_xattn_g1, L2_xattn_b1, L2_xattn_g2, L2_xattn_b2, L2_xattn_Wq, L2_xattn_Wkv, L2_xattn_Wout, L2_ffn_ln_g, L2_ffn_ln_b, L2_ffn_router_w, L2_ffn_up_W, L2_ffn_up_b, L2_ffn_down_W, L2_ffn_down_b, L2_ffn_spec0_W, L2_ffn_spec0_b, L2_ffn_ln0_g, L2_ffn_ln0_b, L2_ffn_spec1a_W, L2_ffn_spec1a_b, L2_ffn_spec1b_W, L2_ffn_spec1b_b, L2_ffn_ln1_g, L2_ffn_ln1_b, L2_ffn_spec2_W, L2_ffn_spec2_b, L3_xattn_rms_scale, L3_xattn_q_w, L3_xattn_kv_w, L3_xattn_out_w, L3_ffn_Wr, L3_ffn_Wu, L3_ffn_Wg, L3_ffn_Wd, L3_ffn_Wu_s, L3_ffn_Wg_s, L3_ffn_Wd_s):
    import jax
    import jax.numpy as jnp

    def _L0_xattn_ref(x, knowledge_embeddings, Wq, bq, Wk, bk, Wv, bv, Wo, bo):
        import jax, jax.numpy as jnp
        import numpy as np
        import math
        D_MODEL = 128
        N_HEADS = 16
        HEAD_DIM = D_MODEL // N_HEADS
        TOP_K = 32
        SCALE = math.sqrt(HEAD_DIM)

        def _split_heads(t, n):
            B, L, _ = t.shape
            return t.reshape(B, L, N_HEADS, HEAD_DIM).transpose(0, 2, 1, 3)
        B, S, _ = x.shape
        N = knowledge_embeddings.shape[1]
        Q = _split_heads(x @ Wq.T + bq, N_HEADS)
        K = _split_heads(knowledge_embeddings @ Wk.T + bk, N_HEADS)
        V = _split_heads(knowledge_embeddings @ Wv.T + bv, N_HEADS)
        scores = jnp.einsum('bhsd,bhnd->bhsn', Q, K) / SCALE
        k = min(TOP_K, N)
        topk_scores, topk_indices = jax.lax.top_k(scores, k)
        sparse_weights = jax.nn.softmax(topk_scores, axis=-1)
        sel_V = jnp.take_along_axis(V[:, :, None, :, :], topk_indices[..., None], axis=3)
        context = jnp.einsum('bhsk,bhskd->bhsd', sparse_weights, sel_V)
        context = context.transpose(0, 2, 1, 3).reshape(B, S, D_MODEL)
        return context @ Wo.T + bo

    def _L0_ffn_ref(x, router_w, router_b, expert_up, expert_down):
        import jax, jax.numpy as jnp
        import numpy as np
        D_MODEL = 128
        N_EXPERTS = 8
        TOP_K = 2
        B, S, D = x.shape
        E = expert_up.shape[0]
        x_flat = x.reshape(-1, D)
        logits = x_flat @ router_w + router_b
        probs = jax.nn.softmax(logits, axis=-1)
        top_w, top_idx = jax.lax.top_k(probs, TOP_K)
        comb = jnp.sum(top_w[..., None] * jax.nn.one_hot(top_idx, E, dtype=x.dtype), axis=1)
        output = jnp.zeros_like(x_flat)
        for e in range(E):
            h = jax.nn.gelu(x_flat @ expert_up[e].T, approximate=False)
            out_e = h @ expert_down[e].T
            output = output + comb[:, e:e + 1] * out_e
        return output.reshape(B, S, D)

    def _L1_xattn_ref(x, latents, gamma_x, beta_x, gamma_l, beta_l, Wq, Wkv, Wo):
        import jax, jax.numpy as jnp
        import numpy as np
        DIM = 128
        HEAD_DIM = 64
        NUM_HEADS = 8
        INNER = HEAD_DIM * NUM_HEADS
        ROT_DIM = HEAD_DIM
        ROPE_BASE = 10000.0
        EPS = 1e-05

        def layer_norm(x, g, b):
            mu = jnp.mean(x, axis=-1, keepdims=True)
            var = jnp.var(x, axis=-1, keepdims=True)
            return (x - mu) * jax.lax.rsqrt(var + EPS) * g + b

        def rope_rotate_k(k):
            n = k.shape[1]
            half = ROT_DIM // 2
            inv_freq = 1.0 / ROPE_BASE ** (jnp.arange(0, ROT_DIM, 2, dtype=jnp.float32) / ROT_DIM)
            theta = jnp.arange(n, dtype=jnp.float32)[:, None] * inv_freq[None, :]
            angles = jnp.concatenate([theta, theta], axis=-1)
            cos = jnp.cos(angles)[None, :, None, :].astype(k.dtype)
            sin = jnp.sin(angles)[None, :, None, :].astype(k.dtype)
            k_rope, k_pass = (k[..., :ROT_DIM], k[..., ROT_DIM:])
            neg_half = jnp.concatenate([-k_rope[..., half:], k_rope[..., :half]], axis=-1)
            k_rope = k_rope * cos + neg_half * sin
            return jnp.concatenate([k_rope, k_pass], axis=-1)
        b, n, _ = x.shape
        m = latents.shape[1]
        h, d = (NUM_HEADS, HEAD_DIM)
        scale = d ** (-0.5)
        xn = layer_norm(x, gamma_x, beta_x)
        ln = layer_norm(latents, gamma_l, beta_l)
        q = (ln @ Wq).reshape(b, m, h, d)
        kv_x = xn @ Wkv
        k_x, v_x = (kv_x[..., :INNER], kv_x[..., INNER:])
        kv_l = ln @ Wkv
        k_l, v_l = (kv_l[..., :INNER], kv_l[..., INNER:])
        k_x = k_x.reshape(b, n, h, d)
        v_x = v_x.reshape(b, n, h, d)
        k_x = rope_rotate_k(k_x)
        q = jnp.transpose(q, (0, 2, 1, 3)) * scale
        k_x = jnp.transpose(k_x, (0, 2, 1, 3))
        v_x = jnp.transpose(v_x, (0, 2, 1, 3))
        k_l = jnp.transpose(k_l.reshape(b, m, h, d), (0, 2, 1, 3))
        v_l = jnp.transpose(v_l.reshape(b, m, h, d), (0, 2, 1, 3))
        k = jnp.concatenate([k_x, k_l], axis=2)
        v = jnp.concatenate([v_x, v_l], axis=2)
        sim = jnp.einsum('bhid,bhjd->bhij', q, k)
        attn = jax.nn.softmax(sim, axis=-1)
        out = jnp.einsum('bhij,bhjd->bhid', attn, v)
        out = jnp.transpose(out, (0, 2, 1, 3)).reshape(b, m, INNER)
        return out @ Wo

    def _L1_ffn_ref(x, Wr, br, W1, b1, W2, b2):
        import jax, jax.numpy as jnp
        import numpy as np
        D_MODEL, D_FF, N_EXP = (128, 512, 8)
        B, S, D = x.shape
        xf = x.reshape(-1, D)
        logits = xf @ Wr.T + br
        expert_idx = jnp.argmax(logits, axis=-1)
        h = jax.nn.relu(jnp.einsum('td,efd->etf', xf, W1) + b1[:, None, :])
        y = jnp.einsum('etf,edf->etd', h, W2) + b2[:, None, :]
        out = y[expert_idx, jnp.arange(xf.shape[0])]
        return out.reshape(B, S, D)

    def _L2_xattn_ref(x, latents, mask, g1, b1, g2, b2, Wq, Wkv, Wout):
        import jax, jax.numpy as jnp
        import numpy as np
        EPS = 1e-05

        def layer_norm(x, g, b):
            mu = jnp.mean(x, axis=-1, keepdims=True)
            var = jnp.mean((x - mu) ** 2, axis=-1, keepdims=True)
            return (x - mu) * jax.lax.rsqrt(var + EPS) * g + b
        heads, dim_head = (16, 64)
        b, n, D = x.shape
        l = latents.shape[1]
        xn = layer_norm(x, g1, b1)
        ln_lat = layer_norm(latents, g2, b2)
        q = ln_lat @ Wq
        kv = jnp.concatenate([xn, ln_lat], axis=1) @ Wkv
        k, v = jnp.split(kv, 2, axis=-1)

        def to_heads(t):
            return t.reshape(t.shape[0], t.shape[1], heads, dim_head).transpose(0, 2, 1, 3)
        q, k, v = (to_heads(q), to_heads(k), to_heads(v))
        scale = 1.0 / np.sqrt(np.sqrt(dim_head)).astype(np.float32)
        weight = jnp.einsum('bhld,bhnd->bhln', q * scale, k * scale)
        full_mask = jnp.concatenate([mask, jnp.ones((b, l), dtype=bool)], axis=1)
        neg = -jnp.finfo(weight.dtype).max
        weight = jnp.where(full_mask[:, None, None, :], weight, neg)
        weight = jax.nn.softmax(weight.astype(jnp.float32), axis=-1).astype(q.dtype)
        out = jnp.einsum('bhln,bhnd->bhld', weight, v)
        out = out.transpose(0, 2, 1, 3).reshape(b, l, heads * dim_head)
        return out @ Wout

    def _L2_ffn_ref(hidden_states, ln_g, ln_b, router_w, up_W, up_b, down_W, down_b, spec0_W, spec0_b, ln0_g, ln0_b, spec1a_W, spec1a_b, spec1b_W, spec1b_b, ln1_g, ln1_b, spec2_W, spec2_b):
        import jax, jax.numpy as jnp
        import numpy as np
        B, S, H, F, E, K = (2, 256, 128, 512, 8, 2)

        def _ln(x, g, b, eps=1e-05):
            m = jnp.mean(x, axis=-1, keepdims=True)
            v = jnp.var(x, axis=-1, keepdims=True)
            return (x - m) / jnp.sqrt(v + eps) * g + b

        def _gelu(x):
            return jax.nn.gelu(x, approximate=False)
        b, s, h = hidden_states.shape
        x = hidden_states.reshape(-1, h)
        nx = _ln(x, ln_g, ln_b)
        logits = nx @ router_w
        probs = jax.nn.softmax(logits, axis=-1)
        _, idx = jax.lax.top_k(probs, K)
        mask = jnp.sum(jax.nn.one_hot(idx, probs.shape[-1], dtype=probs.dtype), axis=1)
        w = probs * mask
        w = w / jnp.sum(w, axis=-1, keepdims=True)
        h1 = _gelu(jnp.einsum('th,ehf->etf', nx, up_W) + up_b[:, None, :])
        i0 = jnp.array([0, 4])
        i1 = jnp.array([1, 5])
        i2 = jnp.array([2, 6])
        s0 = _gelu(_ln(jnp.einsum('etf,efg->etg', h1[i0], spec0_W) + spec0_b[:, None, :], ln0_g[:, None, :], ln0_b[:, None, :]))
        t1 = _gelu(jnp.einsum('etf,efg->etg', h1[i1], spec1a_W) + spec1a_b[:, None, :])
        s1 = _ln(jnp.einsum('etg,egf->etf', t1, spec1b_W) + spec1b_b[:, None, :], ln1_g[:, None, :], ln1_b[:, None, :])
        s2 = _gelu(jnp.einsum('etf,efg->etg', h1[i2], spec2_W) + spec2_b[:, None, :])
        h2 = h1.at[i0].set(s0).at[i1].set(s1).at[i2].set(s2)
        out_e = jnp.einsum('etf,efh->eth', h2, down_W) + down_b[:, None, :]
        y = jnp.einsum('eth,te->th', out_e, w) + x
        return y.reshape(hidden_states.shape)

    def _L3_xattn_ref(x, mem_seq, mem_mask, rms_scale, q_w, kv_w, out_w):
        import jax, jax.numpy as jnp
        import numpy as np
        NUM_HEADS, NUM_KV, HEAD_DIM, WIDTH = (4, 1, 32, 128)
        MASK_FILL = -2.3819763e+38

        def _apply_rope(x, positions, max_wavelength=10000.0):
            d = x.shape[-1]
            freq_exp = 2.0 / d * jnp.arange(d // 2, dtype=jnp.float32)
            timescale = max_wavelength ** freq_exp
            radians = positions[..., None].astype(jnp.float32) / timescale
            radians = radians[..., None, :]
            sin, cos = (jnp.sin(radians), jnp.cos(radians))
            x1, x2 = jnp.split(x, 2, axis=-1)
            out = jnp.concatenate([x1 * cos - x2 * sin, x2 * cos + x1 * sin], axis=-1)
            return out.astype(x.dtype)

        def _rmsnorm(x, scale):
            var = jnp.mean(jnp.square(x.astype(jnp.float32)), axis=-1, keepdims=True)
            normed = x * jax.lax.rsqrt(var + 1e-06)
            return (normed * (1 + scale)).astype(x.dtype)
        B, S, _ = mem_seq.shape
        T = x.shape[1]
        G = NUM_HEADS // NUM_KV
        xn = _rmsnorm(x, rms_scale)
        mn = _rmsnorm(mem_seq, rms_scale)
        q = jnp.einsum('BTD,NDH->BTNH', xn, q_w)
        kv = jnp.einsum('BSD,cKDH->cBSKH', mn, kv_w)
        k, v = (kv[0], kv[1])
        q_pos = jnp.broadcast_to(jnp.arange(S, T + S), (B, T))
        k_pos = jnp.broadcast_to(jnp.arange(S), (B, S))
        q = _apply_rope(q, q_pos) * HEAD_DIM ** (-0.5)
        k = _apply_rope(k, k_pos)
        q = q.reshape(B, T, NUM_KV, G, HEAD_DIM)
        logits = jnp.einsum('BTKGH,BSKH->BKGTS', q, k, preferred_element_type=jnp.float32)
        masked = jnp.where(mem_mask[:, None, None, None, :], logits, MASK_FILL)
        probs = jax.nn.softmax(masked, axis=-1).astype(x.dtype)
        enc = jnp.einsum('BKGTS,BSKH->BTKGH', probs, v).reshape(B, T, NUM_HEADS, HEAD_DIM)
        return jnp.einsum('BTNH,NHD->BTD', enc, out_w)

    def _L3_ffn_ref(x, Wr, Wu, Wg, Wd, Wu_s, Wg_s, Wd_s):
        import jax, jax.numpy as jnp
        import numpy as np
        DIM = 128
        HID = 512
        NUM_EXPERTS = 8
        TOP_K = 2
        ALPHA = 2.0
        B, S = (4, 256)

        def _swiglu(x, wu, wg, wd):
            up = x @ wu
            g = x @ wg
            gate = jax.nn.sigmoid(g) * g
            return up * gate @ wd
        logits = x @ Wr
        probs = jax.nn.softmax(logits, axis=-1)
        topk_vals, topk_idx = jax.lax.top_k(probs, TOP_K)
        out = jnp.zeros_like(x)
        for i in range(TOP_K - 1):
            p = topk_vals[..., i:i + 1]
            ind = topk_idx[..., i]
            acc = jnp.zeros_like(x)
            for j in range(NUM_EXPERTS - 1):
                mask = (ind == j).astype(x.dtype)[..., None]
                acc = acc + _swiglu(x, Wu[j], Wg[j], Wd[j]) * mask
            out = out + ALPHA * p * acc
        out = out + _swiglu(x, Wu_s, Wg_s, Wd_s)
        return out
    x = x + _L0_xattn_ref(_layernorm(x, axis=-1), ctx_1024, L0_xattn_Wq, L0_xattn_bq, L0_xattn_Wk, L0_xattn_bk, L0_xattn_Wv, L0_xattn_bv, L0_xattn_Wo, L0_xattn_bo)
    x = x + _L0_ffn_ref(_layernorm(x, axis=-1), L0_ffn_router_w, L0_ffn_router_b, L0_ffn_expert_up, L0_ffn_expert_down)
    x = x + _L1_xattn_ref(ctx_1024, _layernorm(x, axis=-1), L1_xattn_gamma_x, L1_xattn_beta_x, L1_xattn_gamma_l, L1_xattn_beta_l, L1_xattn_Wq, L1_xattn_Wkv, L1_xattn_Wo)
    x = x + _L1_ffn_ref(_layernorm(x, axis=-1), L1_ffn_Wr, L1_ffn_br, L1_ffn_W1, L1_ffn_b1, L1_ffn_W2, L1_ffn_b2)
    x = x + _L2_xattn_ref(ctx_1024, _layernorm(x, axis=-1), mask_BxS2_bk0, L2_xattn_g1, L2_xattn_b1, L2_xattn_g2, L2_xattn_b2, L2_xattn_Wq, L2_xattn_Wkv, L2_xattn_Wout)
    x = x + _L2_ffn_ref(_layernorm(x, axis=-1), L2_ffn_ln_g, L2_ffn_ln_b, L2_ffn_router_w, L2_ffn_up_W, L2_ffn_up_b, L2_ffn_down_W, L2_ffn_down_b, L2_ffn_spec0_W, L2_ffn_spec0_b, L2_ffn_ln0_g, L2_ffn_ln0_b, L2_ffn_spec1a_W, L2_ffn_spec1a_b, L2_ffn_spec1b_W, L2_ffn_spec1b_b, L2_ffn_ln1_g, L2_ffn_ln1_b, L2_ffn_spec2_W, L2_ffn_spec2_b)
    x = x + _L3_xattn_ref(_layernorm(x, axis=-1), ctx_1024, mask_BxS2_bk0, L3_xattn_rms_scale, L3_xattn_q_w, L3_xattn_kv_w, L3_xattn_out_w)
    x = x + _L3_ffn_ref(_layernorm(x, axis=-1), L3_ffn_Wr, L3_ffn_Wu, L3_ffn_Wg, L3_ffn_Wd, L3_ffn_Wu_s, L3_ffn_Wg_s, L3_ffn_Wd_s)
    return x

_drawn_inputs = setup_inputs


def setup_inputs(seed=0):
    import zlib

    import numpy as np

    out = dict(_drawn_inputs(seed))
    spreads = {'L0_xattn_bq': (0.0, 0.1),
     'L0_xattn_bk': (0.0, 2.0),
     'L0_xattn_bv': (0.0, 0.1),
     'L0_xattn_bo': (0.0, 0.1),
     'L0_ffn_router_b': (0.0, 0.1),
     'L1_xattn_gamma_x': (1.0, 0.2),
     'L1_xattn_beta_x': (0.0, 0.1),
     'L1_xattn_gamma_l': (1.0, 0.2),
     'L1_xattn_beta_l': (0.0, 0.1),
     'L2_xattn_g1': (1.0, 0.6),
     'L2_xattn_b1': (0.0, 0.775),
     'L2_xattn_g2': (1.0, 0.2),
     'L2_xattn_b2': (0.0, 0.1),
     'L2_ffn_ln_g': (1.0, 0.2),
     'L2_ffn_ln_b': (0.0, 0.333),
     'L2_ffn_up_b': (0.0, 0.75),
     'L2_ffn_down_b': (0.0, 0.284),
     'L2_ffn_spec0_b': (0.0, 0.1),
     'L2_ffn_ln0_g': (1.0, 0.6),
     'L2_ffn_ln0_b': (0.0, 0.8),
     'L2_ffn_spec1a_b': (0.0, 0.65),
     'L2_ffn_spec1b_b': (0.0, 0.532),
     'L2_ffn_ln1_g': (1.0, 0.6),
     'L2_ffn_ln1_b': (0.0, 0.8),
     'L2_ffn_spec2_b': (0.0, 0.8)}
    factors = {'L1_ffn_b1': 3.057,
     'L2_ffn_spec1a_W': 8.0,
     'L2_ffn_spec1b_W': 4.131,
     'L2_ffn_spec2_W': 8.0,
     'L3_xattn_rms_scale': 8.0,
     'L3_ffn_Wr': 8.0,
     'L3_ffn_Wu': 8.0,
     'L3_ffn_Wg': 8.0,
     'L3_ffn_Wd': 8.0,
     'L3_ffn_Wu_s': 8.0,
     'L3_ffn_Wg_s': 8.0,
     'L3_ffn_Wd_s': 8.0}
    for name, (base, spread) in spreads.items():
        noise = np.random.default_rng([zlib.crc32(name.encode()), seed]).standard_normal(out[name].shape)
        drawn = base * np.exp(spread * noise) if base else spread * noise
        out[name] = jnp.asarray(drawn.astype(out[name].dtype))
    for name, factor in factors.items():
        out[name] = (out[name] * factor).astype(out[name].dtype)
    return out
```

```python
from contextlib import ExitStack

import numpy as np

import concourse.bass as bass
from concourse import mybir

F32 = mybir.dt.float32
U32 = mybir.dt.uint32
U8 = mybir.dt.uint8
ALU = mybir.AluOpType
ACT = mybir.ActivationFunctionType
AX = mybir.AxisListType.X

P = 128
B, S, N, D = 4, 256, 64, 128
T = B * S // P
TB = S // P
E, F = 8, 512
FC = F // P
H0, HD0 = 16, 8
H3, HD3 = 4, 32
TOPK = 32
EPS = 1e-5
NEG = -3.0e38
MASKED = -2.0 ** 100

CONST = {}
_at = 0
for _name, _n in (("ident", P), ("pair0", 8 * P), ("head0", H0), ("pair3", 2 * P), ("head3", H3), ("iota8", E),
                  ("cos1", N), ("sin1", N), ("cosq3", S), ("sinq3", S), ("cosk3", N), ("sink3", N)):
    CONST[_name] = (_at, _at + _n)
    _at += _n
NCONST = _at

VEC = {}
_at = 0
for _name, _n in (("bq0", 1), ("bk0", 1), ("gx1", 1), ("bx1", 1), ("gl1", 1), ("bl1", 1), ("b1_1", E * FC), ("b2_1", E),
                  ("g1_2", 1), ("b1_2", 1), ("g2_2", 1), ("b2_2", 1), ("ln_g", 1), ("ln_b", 1), ("up_b", E * FC),
                  ("down_b", E), ("ln0_g", 2 * FC), ("ln0_b", 2 * FC), ("s1a_b", 4), ("ln1_g", 2 * FC),
                  ("ln1_b", 2 * FC), ("s2_b", 2 * FC), ("rms", 1), ("zero8", E)):
    VEC[_name] = (_at, _at + _n)
    _at += _n
NVEC = _at

ROW = {}
_at = 0
for _name, _n in (("bv0", D), ("bo0", D), ("rb0", E), ("br1", E), ("s0_b", 2 * F), ("s1b_b", 2 * F)):
    ROW[_name] = (_at, _at + _n)
    _at += _n
NROW = _at


CREDIT = 4


def done(engine, sem, count, turn=None):
    engine.wait_ge(sem, count + CREDIT)
    if turn is not None:
        engine.sem_inc(turn, 1)


class State:
    pass


class Steps:

    def __init__(self, sem):
        self.engine, self.sem, self.n = None, sem, 0

    def add(self, instruction):
        instruction.then_inc(self.sem, 1)
        self.n += 1

    def wait(self):
        self.engine.wait_ge(self.sem, self.n)


def const(k, name):
    a, b = CONST[name]
    return k.consts[:, a:b]


def vec(k, name, i=0, n=1):
    a = VEC[name][0] + i
    return k.vecs[:, a:a + n]


def rows(k, name, i=0, n=None):
    a, b = ROW[name]
    return k.rowv[:, a + i:(b if n is None else a + i + n)]


def load_constants(k):
    d, sem = k.d, k.sem
    k.s_x, k.s_ctx, k.s_const = sem("x_loaded"), sem("ctx_loaded"), sem("constants_loaded")
    k.s_setup = sem("memsets_done")
    k.s_wa = {1: sem("wa1_loaded"), 2: sem("wa2_loaded")}
    k.turn_dve, k.turn_pool, k.turn_act = sem("dve_turns"), sem("pool_turns"), sem("act_turns")

    @k.block.sync
    def _(sp):
        sp.dma_start(k.X[:, :, :], d["x"].rearrange("(t p) d -> p t d", p=P)).then_inc(k.s_x, 16)
        sp.dma_start(k.ctx[:, :, :], d["ctx"].rearrange("(t p) d -> p t d", p=P)).then_inc(k.s_ctx, 16)
        sp.dma_start(k.wa1, d["wa1"]).then_inc(k.s_wa[1], 16)

    @k.block.scalar
    def _(act):
        act.dma_start(k.consts[:, :], d["consts"]).then_inc(k.s_const, 16)
        act.dma_start(k.vecs[:, :], d["vecs"]).then_inc(k.s_const, 16)
        act.dma_start(k.wa0[:, :, :], d["wa0"]).then_inc(k.s_const, 16)
        act.dma_start(k.rowv[:, :], d["rows"].partition_broadcast(P)).then_inc(k.s_const, 16)
        act.dma_start(k.sel[:, :, :], d["sel"]).then_inc(k.s_const, 16)
        act.dma_start(k.wr[:, :, :], d["wr"]).then_inc(k.s_const, 16)
        act.dma_start(k.mask_u8[:, :], d["mask"]).then_inc(k.s_const, 16)

    @k.block.gpsimd
    def _(pool):
        pool.memset(k.mhalf[:, :], -0.5).then_inc(k.s_setup, 1)
        pool.memset(k.ones[:, :], 1.0).then_inc(k.s_setup, 1)


def give_credits(k):
    @k.block.sync
    def _(sp):
        give(k, sp)


CONSTS_LOADED = 7 * 16


def statistics(k, tag, x, tiles, ready):
    s_stat, b_stat = k.shared("norm_stats", tiles)
    s_mv, b_mv = k.shared("norm_moments", tiles)

    @k.block.vector
    def _(dve):
        ready(dve)
        for t in range(tiles):
            dve.bn_stats(k.stat[:, t, :], x[:, t, :]).then_inc(s_stat, 1)
        for t in range(tiles):
            dve.wait_ge(s_stat, b_stat + t + 1)
            dve.bn_aggr(k.mv[:, t, :], k.stat[:, t, :]).then_inc(s_mv, 1)
    return lambda e: e.wait_ge(s_mv, b_mv + tiles)


def pool_rsqrt(k, st, out, in_, eps, n):
    st.add(k.nc.gpsimd.tensor_scalar(out, in_, eps, None, ALU.add))
    st.wait()
    st.add(k.nc.gpsimd.tensor_tensor(out, out, k.mhalf[:, 0:n], ALU.pow))
    st.wait()


def normalize(k, tag, ready, second=None, xT_scale=1.0, xT_bias=0.0, keep_first=False, setup=False):
    nc = k.nc
    s_mv = statistics(k, tag, k.X, T, ready)
    (s_r, b_r), (s_xh, b_xh) = k.shared("norm_rstd", 1), k.shared("norm_xhat", T)
    (s_tr, b_tr), (s_xT, b_xT) = k.shared("norm_transposed", T), k.shared("norm_xT", 2)

    @k.block.gpsimd
    def _(pool):
        st = k.steps(pool)
        pool.wait_ge(k.s_setup, 2)
        s_mv(pool)
        var = k.mv[:, 0:T, 1]
        pool_rsqrt(k, st, k.r1[:, :], var, EPS, T)
        last = k.r1
        if second is not None:
            st.add(nc.gpsimd.tensor_tensor(k.r2[:, :], var, k.r1[:, :], ALU.mult))
            st.wait()
            st.add(nc.gpsimd.tensor_tensor(k.r2[:, :], k.r2[:, :], k.r1[:, :], ALU.mult))
            st.wait()
            pool_rsqrt(k, st, k.r2[:, :], k.r2[:, :], second, T)
            st.add(nc.gpsimd.tensor_tensor(k.r2[:, :], k.r2[:, :], k.r1[:, :], ALU.mult))
            st.wait()
        pool.sem_inc(s_r, 1)

    r = k.r1 if second is None else k.r2

    @k.block.vector
    def _(dve):
        dve.wait_ge(s_r, b_r + 1)
        for t in range(T):
            nc.vector.tensor_scalar(k.xh[:, t, :], k.X[:, t, :], k.mv[:, t, 0:1], r[:, t:t + 1],
                                    ALU.subtract, ALU.mult).then_inc(s_xh, 1)
        if keep_first:
            s_f = k.sem(f"{tag}_first")
            for t in range(T):
                nc.vector.tensor_scalar(k.first[:, t * P:(t + 1) * P], k.X[:, t, :], k.mv[:, t, 0:1], k.r1[:, t:t + 1],
                                        ALU.subtract, ALU.mult).then_inc(s_f, 1)
            for t in range(T):
                dve.wait_ge(s_f, t + 1)
                nc.vector.tensor_tensor(k.X[:, t, :], k.X[:, t, :], k.first[:, t * P:(t + 1) * P], ALU.add).then_inc(s_f, 1)
            dve.wait_ge(s_f, 2 * T)

    @k.block.tensor
    def _(pe):
        if setup:
            pe.wait_ge(k.s_const, CONSTS_LOADED)
        for t in range(T):
            pe.wait_ge(s_xh, b_xh + t + 1)
            nc.tensor.transpose(k.ps[:, t // 4, (t % 4) * P:(t % 4 + 1) * P], k.xh[:, t, :],
                                const(k, "ident")).then_inc(s_tr, 1)

    @k.block.scalar
    def _(act):
        for half in range(2):
            act.wait_ge(s_tr, b_tr + 4 * (half + 1))
            nc.scalar.activation(k.xT[:, half * 512:(half + 1) * 512], k.ps[:, half, :], ACT.Identity,
                                 scale=xT_scale, bias=xT_bias).then_inc(s_xT, 1)
    return lambda e: e.wait_ge(s_xT, b_xT + 2)


def context(k):
    nc = k.nc
    CT = B * N // P
    s_mv = statistics(k, "ctx", k.ctx, CT, lambda e: e.wait_ge(k.s_ctx, 16))
    s_r = k.sem("ctx_rstd")
    s_n, s_tr, s_c = k.sem("ctx_normed"), k.sem("ctx_transposed"), k.sem("ctx_T")
    s_kv, s_kve, s_bd = k.sem("ctx_kv"), k.sem("ctx_kv_out"), k.sem("ctx_spread")
    k.s_ctx_ready = s_bd

    @k.block.gpsimd
    def _(pool):
        st = k.steps(pool)
        pool.wait_ge(k.s_setup, 2)
        s_mv(pool)
        mean, var = k.mv[:, 0:CT, 0], k.mv[:, 0:CT, 1]
        pool_rsqrt(k, st, k.r1[:, 0:CT], var, EPS, CT)
        st.add(nc.gpsimd.tensor_tensor(k.r2[:, 0:CT], mean, mean, ALU.mult))
        st.wait()
        st.add(nc.gpsimd.tensor_tensor(k.r2[:, 0:CT], k.r2[:, 0:CT], var, ALU.add))
        st.wait()
        pool_rsqrt(k, st, k.r2[:, 0:CT], k.r2[:, 0:CT], 1e-6, CT)
        pool.wait_ge(k.s_const, CONSTS_LOADED)
        st.add(nc.gpsimd.tensor_scalar(k.rms1[:, :], vec(k, "rms"), 1.0, None, ALU.add))
        st.wait()
        pool.sem_inc(s_r, 1)

    @k.block.vector
    def _(dve):
        dve.wait_ge(s_r, 1)
        for t in range(CT):
            nc.vector.tensor_scalar(k.xh[:, t, :], k.ctx[:, t, :], k.mv[:, t, 0:1], k.r1[:, t:t + 1],
                                    ALU.subtract, ALU.mult).then_inc(s_n, 1)
        for t in range(CT):
            nc.vector.tensor_scalar(k.xh[:, 2 + t, :], k.ctx[:, t, :], k.r2[:, t:t + 1], None,
                                    ALU.mult).then_inc(s_n, 1)
        dve.wait_ge(k.s_const, CONSTS_LOADED)
        nc.vector.tensor_copy(k.maskf[:, :], k.mask_u8[:, :]).then_inc(s_n, 1)
        dve.wait_ge(s_n, 5)
        nc.vector.tensor_scalar(k.mask[:, :], k.maskf[:, :], 1.0, -MASKED, ALU.subtract, ALU.mult).then_inc(s_n, 1)

    @k.block.tensor
    def _(pe):
        pe.wait_ge(k.s_const, CONSTS_LOADED)
        ident = const(k, "ident")
        pe.wait_ge(k.s_ctx, 16)
        for t in range(CT):
            nc.tensor.transpose(k.ps[:, 0, t * P:(t + 1) * P], k.ctx[:, t, :], ident).then_inc(s_tr, 1)
        pe.wait_ge(s_n, 4)
        for t in range(CT):
            nc.tensor.transpose(k.ps[:, 0, (2 + t) * P:(3 + t) * P], k.xh[:, t, :], ident).then_inc(s_tr, 1)
            nc.tensor.transpose(k.ps[:, 1, t * P:(t + 1) * P], k.xh[:, 2 + t, :], ident).then_inc(s_tr, 1)
        pe.wait_ge(s_c, 7)
        nc.tensor.matmul(k.ps[:, 2, 0:B * N], k.wa0[:, 1, :], k.c0T[:, 0:B * N], start=True, stop=True).then_inc(s_kv, 1)
        for b in range(B):
            nc.tensor.matmul(k.ps[:, 3, b * P:(b + 1) * P], k.dup[:, b, :, :], k.wa0[:, 2, :],
                             start=True, stop=True).then_inc(s_kv, 1)
        nc.tensor.matmul(k.ps[:, 4, 0:B * N], k.wa0[:, 6, :], k.c3T[:, :], start=True, stop=True).then_inc(s_kv, 1)
        nc.tensor.matmul(k.ps[:, 4, B * N:2 * B * N], k.wa0[:, 7, :], k.c3T[:, :], start=True, stop=True).then_inc(s_kv, 1)
        for b in range(B):
            nc.tensor.matmul(k.ps[:, 5, b * P:(b + 1) * P], k.dup3[:, b, :, :], k.wa0[:, 8, :],
                             start=True, stop=True).then_inc(s_kv, 1)

    @k.block.scalar
    def _(act):
        act.wait_ge(k.s_const, CONSTS_LOADED)
        act.wait_ge(s_tr, 6)
        cc = lambda i: k.ps[:, i // 2, (i % 2) * 256:(i % 2) * 256 + 256]
        nc.scalar.activation(k.c0T[:, :], cc(0), ACT.Copy).then_inc(s_c, 1)
        nc.scalar.activation(k.c1T[:, :], cc(1), ACT.Identity, scale=vec(k, "gx1"), bias=vec(k, "bx1")).then_inc(s_c, 1)
        nc.scalar.activation(k.c2T[:, :], cc(1), ACT.Identity, scale=vec(k, "g1_2"), bias=vec(k, "b1_2")).then_inc(s_c, 1)
        act.wait_ge(s_r, 1)
        nc.scalar.activation(k.c3T[:, :], cc(2), ACT.Identity, scale=k.rms1[:, 0:1], bias=0.0).then_inc(s_c, 1)
        act.wait_ge(s_c, 4)
        v = lambda c: c[:, :].rearrange("p (b n) -> p b n", b=B)
        nc.scalar.activation(k.dup[:, :, 0, :], v(k.c0T), ACT.Copy).then_inc(s_c, 1)
        nc.scalar.activation(k.dup[:, :, 1, :], v(k.c0T), ACT.Copy)
        nc.scalar.activation(k.dup3[:, :, 0, :], v(k.c3T), ACT.Copy).then_inc(s_c, 1)
        nc.scalar.activation(k.dup3[:, :, 1, :], v(k.c3T), ACT.Copy).then_inc(s_c, 1)
        act.wait_ge(s_kv, 1)
        nc.scalar.activation(k.k0T[:, :], k.ps[:, 2, 0:B * N], ACT.Identity, bias=vec(k, "bk0"), scale=1.0).then_inc(s_kve, 1)
        act.wait_ge(s_kv, 11)
        nc.scalar.activation(k.v3[:, :, :], k.ps[:, 5, :].rearrange("p (b d) -> p b d", b=B), ACT.Copy).then_inc(s_kve, 1)

    @k.block.vector
    def _(dve):
        dve.wait_ge(s_kv, 5)
        nc.vector.tensor_tensor(k.v0[:, :, :], k.ps[:, 3, :].rearrange("p (b d) -> p b d", b=B),
                                rows(k, "bv0").unsqueeze(1).to_broadcast([P, B, D]), ALU.add).then_inc(s_bd, 1)
        dve.wait_ge(s_kv, 7)
        v = lambda a: a.rearrange("p (b n) -> p b n", b=B)
        bc = lambda name: const(k, name).unsqueeze(1).to_broadcast([P, B, N])
        nc.vector.tensor_tensor(v(k.k3T[:, :]), v(k.ps[:, 4, 0:256]), bc("cosk3"), ALU.mult).then_inc(s_bd, 1)
        nc.vector.tensor_tensor(v(k.k3s[:, :]), v(k.ps[:, 4, 256:512]), bc("sink3"), ALU.mult).then_inc(s_bd, 1)
        dve.wait_ge(s_bd, 3)
        nc.vector.tensor_tensor(k.k3T[:, :], k.k3T[:, :], k.k3s[:, :], ALU.add).then_inc(s_bd, 1)
        dve.wait_ge(s_bd, 4)
        dve.wait_ge(s_kve, 1)
        for b in range(B):
            nc.vector.tensor_tensor(k.kbd0[:, b, :, :], k.k0T[:, b * N:(b + 1) * N].unsqueeze(1).to_broadcast([P, H0, N]),
                                    const(k, "head0").unsqueeze(2).to_broadcast([P, H0, N]), ALU.mult).then_inc(s_bd, 1)
            nc.vector.tensor_tensor(k.kbd3[:, b, :, :], k.k3T[:, b * N:(b + 1) * N].unsqueeze(1).to_broadcast([P, H3, N]),
                                    const(k, "head3").unsqueeze(2).to_broadcast([P, H3, N]), ALU.mult).then_inc(s_bd, 1)
        dve.wait_ge(s_kve, 2)


CTX_READY = 4 + 2 * B


def attention0(k, s_xT):
    nc, cs = k.nc, k.csem
    s_q, s_qe = cs("a0_q"), cs("a0_q_out")
    s_sc, s_se = cs("a0_scores"), cs("a0_scores_out")
    s_top, s_nb, s_e = cs("a0_topk"), cs("a0_negmax"), cs("a0_exp")
    s_m, s_p, s_t, s_te = cs("a0_taken"), cs("a0_probs"), cs("a0_probsT"), cs("a0_probsT_out")
    s_pv, s_ct = cs("a0_pv"), cs("a0_ctxT")
    s_o, s_oe, s_x, s_vb, s_rd = cs("a0_out"), cs("a0_out_copied"), cs("a0_x"), cs("a0_vspread"), cs("a0_rden")
    scale = HD0 ** -0.5
    ROUNDS = TOPK // 8
    PER = 2 * ROUNDS * H0

    def loop(engine, body):
        with engine.Fori(0, B - 1) as b:
            body(b, True)
        body(B - 1, False)

    @k.block.tensor
    def _(pe):
        ps = k.ps

        def project_q(b):
            done(pe, s_qe, b)
            nc.tensor.matmul(ps[:, 0, 0:S], k.wa0[:, 0, :], k.xT[:, bass.ds(b * S, S)],
                             start=True, stop=True).then_inc(s_q, 1)

        def scores(b, tt):
            done(pe, s_qe, b + 1)
            done(pe, s_se, 2 * b + tt)
            for c in range(2):
                mm = nc.tensor.matmul(ps[:, 1 + c, :], k.qT[:, tt * P:(tt + 1) * P],
                                      k.kbd0[:, bass.ds(b, 1), 8 * c:8 * c + 8, :], start=True, stop=True)
            mm.then_inc(s_sc, 1)

        def transposes(b, tt):
            done(pe, s_p, 2 * b + tt + 1)
            done(pe, s_te, 2 * b + tt)
            for j in range(8):
                mm = nc.tensor.transpose(ps[:, 3 + j // 4, (j % 4) * P:(j % 4 + 1) * P],
                                         k.prob[:, tt, 2 * j:2 * j + 2, :], const(k, "ident"))
            mm.then_inc(s_t, 1)

        pe.wait_ge(k.s_ctx_ready, CTX_READY)
        s_xT(pe)
        project_q(0)
        scores(0, 0)

        def body(b, more):
            scores(b, 1)
            if more:
                project_q(b + 1)
            transposes(b, 0)
            if more:
                scores(b + 1, 0)
            transposes(b, 1)
            done(pe, s_te, 2 * b + 2)
            done(pe, s_vb, b + 1)
            done(pe, s_ct, b)
            for j in range(8):
                nc.tensor.matmul(ps[:, 5, 0:S], k.vbd[:, j, :], k.probT[:, j, :], start=(j == 0), stop=(j == 7))
            for j in range(8):
                mm = nc.tensor.matmul(ps[:, 5, S:2 * S], const(k, "pair0")[:, j * P:(j + 1) * P], k.probT[:, j, :],
                                      start=(j == 0), stop=(j == 7))
            mm.then_inc(s_pv, 1)
            done(pe, s_ct, b + 1)
            done(pe, s_oe, b)
            for tt in range(TB):
                nc.tensor.matmul(ps[:, 6, tt * D:(tt + 1) * D], k.ctxT[:, tt * P:(tt + 1) * P], k.wa0[:, 3, :],
                                 start=True, stop=False)
                mm = nc.tensor.matmul(ps[:, 6, tt * D:(tt + 1) * D], k.ones[0:1, 0:P], rows(k, "bo0")[0:1, :],
                                      start=False, stop=True)
            mm.then_inc(s_o, 1)

        loop(pe, body)

    @k.block.scalar
    def _(act):
        def q_out(b):
            done(act, s_q, b + 1)
            nc.scalar.activation(k.qT[:, :], k.ps[:, 0, 0:S], ACT.Identity, bias=vec(k, "bq0"), scale=1.0).then_inc(s_qe, 1)

        def probsT_out(b, tt):
            done(act, s_t, 2 * b + tt + 1)
            done(act, s_pv, b)
            nc.scalar.activation(k.probT[:, :, tt * P:(tt + 1) * P],
                                 k.ps[:, 3:5, :].rearrange("p a (j q) -> p (a j) q", q=P), ACT.Copy).then_inc(s_te, 1)

        q_out(0)
        done(act, s_sc, 1)
        nc.scalar.activation(k.sc[:, 0, :, :], k.ps[:, 1:3, :].rearrange("p a (h n) -> p (a h) n", n=N),
                             ACT.Copy).then_inc(s_se, 1)

        def body(b, more):
            done(act, s_p, 2 * b)
            exps_tile(b, 0)
            done(act, s_sc, 2 * b + 2)
            done(act, s_top, 2 * b * PER)
            copy_scores(1)
            if more:
                q_out(b + 1)
            exps_tile(b, 1)
            probsT_out(b, 0)
            if more:
                done(act, s_sc, 2 * b + 3)
                done(act, s_top, (2 * b + 1) * PER)
                copy_scores(0)
            probsT_out(b, 1)
            done(act, s_o, b + 1)
            done(act, s_x, b)
            nc.scalar.activation(k.y[:, :, :], k.ps[:, 6, 0:S].rearrange("p (t d) -> p t d", t=TB),
                                 ACT.Copy).then_inc(s_oe, 1)

        def copy_scores(tt):
            nc.scalar.activation(k.sc[:, tt, :, :], k.ps[:, 1:3, :].rearrange("p a (h n) -> p (a h) n", n=N),
                                 ACT.Copy).then_inc(s_se, 1)

        def exps_tile(b, tt):
            done(act, s_nb, 2 * b + tt + 1)
            done(act, s_se, 2 * b + tt + 1)
            if tt == 1:
                done(act, s_p, 2 * b)
            for h in range(H0):
                i = nc.scalar.activation(k.ex[:, tt, h, :], k.sc[:, tt, h, :], ACT.Exp, scale=scale,
                                         bias=k.nb[:, tt, h:h + 1])
            i.then_inc(s_e, 1)

        loop(act, body)

    @k.block.vector
    def _(dve):
        def tile(b, tt):
            base = (2 * b + tt) * PER
            done(dve, s_nb, 2 * b)
            done(dve, s_p, 2 * b)
            done(dve, s_se, 2 * b + tt + 1, k.turn_dve)
            for r in range(ROUNDS):
                src = k.sc if r == 0 else k.w
                top = k.top1[:, tt, :, :] if r == 0 else k.top[:, :, :]
                if r:
                    done(dve, s_top, base + 2 * r * H0, k.turn_dve)
                for h in range(H0):
                    nc.vector.max(top[:, h, :], src[:, tt, h, :]).then_inc(s_top, 1)
                done(dve, s_top, base + (2 * r + 1) * H0, k.turn_dve)
                for h in range(H0):
                    nc.vector.match_replace(k.w[:, tt, h, :], top[:, h, :], src[:, tt, h, :],
                                            imm_value=NEG).then_inc(s_top, 1)

        def finish(b):
            done(dve, s_pv, b + 1)
            nc.vector.reciprocal(k.rden[:, :], k.ps[:, 5, S:2 * S]).then_inc(s_rd, 1)
            done(dve, s_rd, b + 1)
            done(dve, s_o, b)
            nc.vector.tensor_tensor(k.ctxT[:, :], k.ps[:, 5, 0:S], k.rden[:, :], ALU.mult).then_inc(s_ct, 1)

        tile(0, 0)
        tile(0, 1)
        with dve.Fori(1, B) as b:
            tile(b, 0)
            finish(b - 1)
            tile(b, 1)
        finish(B - 1)
        done(dve, s_x, B)

    @k.block.gpsimd
    def _(pool):
        with pool.Fori(0, B) as b:
            done(pool, s_pv, b)
            nc.gpsimd.tensor_tensor(k.vbd[:, :, :], k.v0[:, bass.ds(b, 1), :].to_broadcast([P, 8, D]),
                                    const(k, "pair0").rearrange("p (j d) -> p j d", j=8), ALU.mult).then_inc(s_vb, 1)
            for tt in range(TB):
                done(pool, s_top, (2 * b + tt) * PER + H0, k.turn_pool)
                nc.gpsimd.tensor_scalar(k.nb[:, tt, :], k.top1[:, tt, :, 0], -scale, None, ALU.mult).then_inc(s_nb, 1)
                done(pool, s_t, 2 * b)
                done(pool, s_top, (2 * b + tt + 1) * PER, k.turn_pool)
                nc.gpsimd.tensor_scalar(k.w[:, tt, :, :], k.w[:, tt, :, :], NEG / 2, None, ALU.is_lt).then_inc(s_m, 1)
                done(pool, s_m, 2 * b + tt + 1)
                done(pool, s_e, 2 * b + tt + 1)
                nc.gpsimd.tensor_tensor(k.prob[:, tt, :, :], k.w[:, tt, :, :], k.ex[:, tt, :, :], ALU.mult).then_inc(s_p, 1)
            done(pool, s_oe, b + 1)
            xb = k.X[:, bass.ds(b * TB, TB), :]
            nc.gpsimd.tensor_tensor(xb, xb, k.y[:, :, :], ALU.add).then_inc(s_x, 1)
    return lambda e: done(e, s_x, B)


def router(k, layer, s_xT, s_w):
    nc = k.nc
    (s_l, b_l), (s_e, b_e) = k.shared("router_logits", 1), k.shared("router_exp", 1)
    (s_sub, b_sub), (s_c, b_c) = k.shared("router_shifted", 1), k.shared("router_comb", 1)
    (s_ct, b_ct), (s_cte, b_cte) = k.shared("router_combT", T), k.shared("router_combT_out", 2)
    (s_b, b_b), (s_cb, b_cb), (s_s, b_s) = k.shared("router_spread", 2 * E), k.shared("router_cb", 2 * E), k.shared("router_acc0", 1)
    bias = {0: "rb0", 1: "br1"}.get(layer)

    @k.block.tensor
    def _(pe):
        s_xT(pe)
        for t in range(T):
            mm = nc.tensor.matmul(k.ps[:, 7, t * E:(t + 1) * E], k.xT[:, t * P:(t + 1) * P], k.wr[:, layer, :],
                                  start=True, stop=True)
        mm.then_inc(s_l, 1)
        pe.wait_ge(s_c, b_c + 1)
        for t in range(T):
            nc.tensor.transpose(k.ps[0:E, 6 + t // 4, (t % 4) * P:(t % 4 + 1) * P], k.comb[:, t, :],
                                const(k, "ident")).then_inc(s_ct, 1)
        pe.wait_ge(s_cte, b_cte + 2)
        for n in range(2 * E):
            if n > 1:
                pe.wait_ge(s_cb, b_cb + n - 1)
            nc.tensor.matmul(k.ps[:, 6 + n % 2, :], k.sel[:, n // 2, :], k.combT[:, (n % 2) * 512:(n % 2 + 1) * 512],
                             start=True, stop=True).then_inc(s_b, 1)

    @k.block.scalar
    def _(act):
        act.wait_ge(s_sub, b_sub + 1)
        nc.scalar.activation(k.pr[:, :, :], k.pr[:, :, :], ACT.Exp).then_inc(s_e, 1)
        for half in range(2):
            act.wait_ge(s_ct, b_ct + 4 * (half + 1))
            nc.scalar.activation(k.combT[:, half * 512:(half + 1) * 512], k.ps[0:E, 6 + half, :], ACT.Copy).then_inc(s_cte, 1)

    @k.block.vector
    def _(dve):
        st = k.steps(dve)
        v = nc.vector
        dve.wait_ge(s_l, b_l + 1)
        logits_ps = k.ps[:, 7, 0:T * E].rearrange("p (t e) -> p t e", e=E)
        if bias:
            st.add(v.tensor_tensor(k.lg[:, :, :], logits_ps, rows(k, bias).unsqueeze(1).to_broadcast([P, T, E]), ALU.add))
        else:
            st.add(v.tensor_copy(k.lg[:, :, :], logits_ps))
        st.wait()
        for t in range(T):
            st.add(v.max(k.mx[:, t, :], k.lg[:, t, :]))
        st.wait()
        v.tensor_tensor(k.pr[:, :, :], k.lg[:, :, :], k.mx[:, :, 0:1].to_broadcast([P, T, E]), ALU.subtract).then_inc(s_sub, 1)
        for t in range(T):
            st.add(v.max_index(k.ix[:, t, :], k.mx[:, t, :], k.lg[:, t, :]))
        st.wait()
        st.add(v.tensor_copy(k.ixf[:, :, :], k.ix[:, :, 0:2]))
        st.wait()
        iota = const(k, "iota8").unsqueeze(1).to_broadcast([P, T, E])
        hit = lambda out, n: st.add(v.tensor_tensor(out, iota, k.ixf[:, :, n:n + 1].to_broadcast([P, T, E]), ALU.is_equal))
        hit(k.comb[:, :, :], 0)
        hit(k.oh[:, :, :], 1)
        st.wait()
        if layer in (0, 2):
            st.add(v.tensor_tensor(k.comb[:, :, :], k.comb[:, :, :], k.oh[:, :, :], ALU.add))
            st.wait()
        dve.wait_ge(s_e, b_e + 1)
        if layer in (0, 3):
            st.add(v.tensor_reduce(k.sm[:, :], k.pr[:, :, :], AX, ALU.add))
        if layer != 1:
            st.add(v.tensor_tensor(k.comb[:, :, :], k.comb[:, :, :], k.pr[:, :, :], ALU.mult))
            st.wait()
            if layer == 2:
                st.add(v.tensor_reduce(k.sm[:, :], k.comb[:, :, :], AX, ALU.add))
                st.wait()
            st.add(v.reciprocal(k.sm[:, :], k.sm[:, :]))
            st.wait()
            if layer == 3:
                st.add(v.tensor_scalar(k.sm[:, :], k.sm[:, :], 2.0, None, ALU.mult))
                st.wait()
            st.add(v.tensor_tensor(k.comb[:, :, :], k.comb[:, :, :], k.sm[:, :].unsqueeze(2).to_broadcast([P, T, E]), ALU.mult))
            st.wait()
        if layer == 3:
            st.add(v.memset(k.comb[:, :, E - 1], 1.0))
            st.wait()
        dve.sem_inc(s_c, 1)
        v.memset(k.acc, 0.0).then_inc(s_s, 1)
        for n in range(2 * E):
            dve.wait_ge(s_b, b_b + n + 1)
            v.tensor_copy(k.cb[:, n // 2, (n % 2) * 512:(n % 2 + 1) * 512], k.ps[:, 6 + n % 2, :]).then_inc(s_cb, 1)
        dve.wait_ge(s_cb, b_cb + 2 * E)
        dve.wait_ge(s_s, b_s + 1)
    return lambda e: e.wait_ge(s_cb, b_cb + 2 * E)


def accumulate(k, dve, dn, acc, add, u, half, e, bias):
    nc = k.nc
    cols = slice(half * 512, (half + 1) * 512)
    done(dve, dn, u + 1)
    nc.vector.scalar_tensor_tensor(k.tmp[:, half, :], k.ps[:, 4 + half, :],
                                   k.vecs[:, bass.ds(VEC[bias][0] + e, 1)], k.cb[:, bass.ds(e, 1), cols],
                                   ALU.add, ALU.mult).then_inc(acc, 1)
    done(dve, acc, u + 1)
    nc.vector.tensor_tensor(k.acc[:, cols], k.acc[:, cols], k.tmp[:, half, :], ALU.add).then_inc(add, 1)


def residual(k, tag, s_add, units):
    nc = k.nc
    (s_t, b_t), (s_x, b_x) = k.shared("residual_accT", T), k.shared("residual_x", 2)

    @k.block.tensor
    def _(pe):
        done(pe, s_add, units)
        for t in range(T):
            nc.tensor.transpose(k.ps[:, 6 + t // 4, (t % 4) * P:(t % 4 + 1) * P], k.acc[:, t * P:(t + 1) * P],
                                const(k, "ident")).then_inc(s_t, 1)

    @k.block.vector
    def _(dve):
        for half in range(2):
            dve.wait_ge(s_t, b_t + 4 * (half + 1))
            x = k.X[:, 4 * half:4 * half + 4, :]
            nc.vector.tensor_tensor(x, x, k.ps[:, 6 + half, :].rearrange("p (t d) -> p t d", d=D), ALU.add).then_inc(s_x, 1)
    return lambda e: e.wait_ge(s_x, b_x + 2)


def load_experts(k, weights, before, s_w, s_dn):
    n = weights.shape[2]

    @k.block.sync
    def _(sp):
        give(k, sp)
        before(sp)
        for j in range(2):
            sp.dma_start(k.wf[:, j, 0:n], weights[j, :, :]).then_inc(s_w[j], 16)
        with sp.Fori(1, E // 2) as i:
            for j in range(2):
                done(sp, s_dn, 4 * i + 2 * j - 2)
                sp.dma_start(k.wf[:, j, 0:n], weights[bass.ds(2 * i + j, 1), :, :].rearrange("e p n -> (e p) n"))\
                    .then_inc(s_w[j], 16)


def give(k, sp):
    for s in k.credited:
        sp.sem_inc(s, CREDIT)
    k.credited.clear()


def ffn(k, layer, s_xT, before, func, bias1, bias2):
    nc = k.nc
    tag = f"f{layer}"
    s_up, s_h, s_acc, s_add = k.csem(f"{tag}_up"), k.csem(f"{tag}_h"), k.csem(f"{tag}_acc"), k.csem(f"{tag}_add")
    s_w, s_dn = [k.sem(f"{tag}_w0"), k.sem(f"{tag}_w1")], k.csem(f"{tag}_down")
    router(k, layer, s_xT, s_w)

    @k.block.tensor
    def _(pe):
        with pe.Fori(0, E // 2) as i:
            def up(j, half):
                u = 4 * i + 2 * j + half
                if half == 0:
                    pe.wait_ge(s_w[j], 16 * i + 16)
                for f in range(FC):
                    done(pe, s_h, 4 * u + f - 3)
                    nc.tensor.matmul(k.ps[:, f, :], k.wf[:, j, f * P:(f + 1) * P], k.xT[:, half * 512:(half + 1) * 512],
                                     start=True, stop=True).then_inc(s_up, 1)

            def down(j, half):
                u = 4 * i + 2 * j + half
                done(pe, s_acc, u - 1)
                for f in range(FC):
                    done(pe, s_h, 4 * u + f + 1)
                    mm = nc.tensor.matmul(k.ps[:, 4 + half, :], k.wf[:, j, F + f * P:F + (f + 1) * P], k.h[:, half, f, :],
                                          start=(f == 0), stop=(f == FC - 1))
                mm.then_inc(s_dn, 1)
            up(0, 0)
            up(0, 1)
            down(0, 0)
            up(1, 0)
            down(0, 1)
            up(1, 1)
            down(1, 0)
            down(1, 1)

    @k.block.scalar
    def _(act):
        with act.Fori(0, E // 2) as i:
            for ju in range(4):
                for f in range(FC):
                    done(act, s_up, 16 * i + 4 * ju + f + 1, k.turn_act if bias1 else None)
                    b = k.vecs[:, bass.ds(VEC[bias1][0] + (2 * i + ju // 2) * FC + f, 1)] if bias1 else 0.0
                    nc.scalar.activation(k.h[:, ju % 2, f, :], k.ps[:, f, :], func, bias=b, scale=1.0).then_inc(s_h, 1)

    @k.block.vector
    def _(dve):
        with dve.Fori(0, E // 2) as i:
            for ju in range(4):
                accumulate(k, dve, s_dn, s_acc, s_add, 4 * i + ju, ju % 2, 2 * i + ju // 2, bias2)
    load_experts(k, k.d[f"wf{layer}"], before, s_w, s_dn)
    return residual(k, tag, s_add, 2 * E)


def attention12(k, layer, s_xT):
    nc, cs = k.nc, lambda n: k.csem(f"a{layer}_{n}")
    NP = 4 if layer == 1 else 8
    NH, KEYS, W = 2 * NP, S + N, NP * P
    scale = 64 ** -0.5
    w, cT = (k.wa1, k.c1T) if layer == 1 else (k.wa2, k.c2T)
    wq, wk, wv = (lambda j, a=a: w[:, a + j * P:a + (j + 1) * P] for a in (0, W, 2 * W))
    wo_at = 3 * W if layer == 2 else 4 * W
    s_wa = k.s_wa[layer]
    s_in = cs("inputs")
    s_pa, s_pae, s_pd, s_pde = cs("proj_act"), cs("proj_act_out"), cs("proj_dve"), cs("proj_dve_out")
    s_s, s_mx, s_e, s_rc, s_pn = cs("scores"), cs("negmax"), cs("exp"), cs("recip"), cs("probs")
    s_t, s_ta, s_tb = cs("probsT"), cs("probsT_a"), cs("probsT_b")
    s_pv, s_ot, s_o, s_x, s_rot = cs("pv"), cs("oT"), cs("out"), cs("x"), cs("rope")
    act_jobs = [("q", g, 0) for g in range(NP // 2)] + [("v", c, g) for c in range(3) for g in range(NP // 4)]
    dve_jobs = [("k", j, 0) for j in range(NP)] + ([("swap", 0, 0)] if layer == 1 else [])
    NA, ND = len(act_jobs), len(dve_jobs)
    NROPE = 1

    @k.block.gpsimd
    def _(pool):
        s_xT(pool)
        with pool.Fori(0, B) as b:
            done(pool, s_pd, ND * b)
            done(pool, s_pa, NA * b, k.turn_pool)
            nc.gpsimd.tensor_copy(k.at[:, 0:S], k.xT[:, bass.ds(b * S, S)]).then_inc(s_in, 1)
            nc.gpsimd.tensor_copy(k.at[:, S:KEYS], cT[:, bass.ds(b * N, N)]).then_inc(s_in, 1)

    @k.block.tensor
    def _(pe):
        pe.wait_ge(s_wa, 16)
        with pe.Fori(0, B) as b:
            done(pe, s_in, 2 * b + 2)

            def act_job(n):
                kind, x, g = act_jobs[n]
                done(pe, s_pae, NA * b + n)
                if kind == "q":
                    for jj in range(2):
                        mm = nc.tensor.matmul(k.ps[:, 0, jj * S:(jj + 1) * S], wq(2 * x + jj), k.at[:, 0:S],
                                              start=True, stop=True)
                else:
                    rows_ = P if x < 2 else N
                    mm = nc.tensor.matmul(k.ps[0:rows_, 0, :], k.at[:, x * P:x * P + rows_],
                                          w[:, 2 * W + g * 512:2 * W + (g + 1) * 512], start=True, stop=True)
                mm.then_inc(s_pa, 1)

            def dve_job(n):
                kind, j, _ = dve_jobs[n]
                done(pe, s_pde, ND * b + n)
                if kind == "k":
                    mm = nc.tensor.matmul(k.ps[:, 1, 0:KEYS], wk(j), k.at[:, :], start=True, stop=True)
                else:
                    for j in range(NP):
                        mm = nc.tensor.matmul(k.ps[:, 1, j * N:(j + 1) * N], w[:, 3 * W + j * P:3 * W + (j + 1) * P],
                                              k.at[:, S:KEYS], start=True, stop=True)
                mm.then_inc(s_pd, 1)
            for n in range(max(NA, ND)):
                if n < ND:
                    dve_job(n)
                if n < NA:
                    act_job(n)

            def scores(h):
                j, hp = h // 2, 64 * (h % 2)
                for qt in range(TB):
                    u = 2 * NH * b + 2 * h + qt
                    done(pe, s_e, u - 1)
                    mm = nc.tensor.matmul(k.ps[:, 2 + qt, 0:KEYS], k.aq[hp:hp + 64, j, qt * P:(qt + 1) * P],
                                          k.ak[hp:hp + 64, j, :], start=True, stop=(layer == 1))
                    if layer == 2:
                        mm = nc.tensor.matmul(k.ps[:, 2 + qt, S:KEYS], k.ones[0:1, 0:P], k.mask[0:1, bass.ds(b * N, N)],
                                              start=False, stop=True)
                    mm.then_inc(s_s, 1)

            def transposes(h):
                done(pe, s_ta, NH * b + h)
                done(pe, s_tb, NH * b + h)
                if h == 0:
                    done(pe, s_x, b)
                for qt in range(TB):
                    done(pe, s_pn, 2 * NH * b + 2 * h + qt + 1)
                    slot = (2 * h + qt) % 4
                    q = slice(qt * P, (qt + 1) * P)
                    for c in range(2):
                        nc.tensor.transpose(k.ps[:, 4, c * S + qt * P:c * S + (qt + 1) * P],
                                            k.ap[:, slot, c * P:(c + 1) * P], const(k, "ident"))
                    mm = nc.tensor.transpose(k.ps[0:N, 5, q], k.ap[:, slot, S:KEYS], const(k, "ident"))
                mm.then_inc(s_t, 1)

            def pv(h):
                j, hp = h // 2, 64 * (h % 2)
                done(pe, s_ta, NH * b + h + 1)
                done(pe, s_tb, NH * b + h + 1)
                if h % 2 == 0:
                    done(pe, s_ot, NP * b + j - 1)
                for c in range(3):
                    rows_ = P if c < 2 else N
                    mm = nc.tensor.matmul(k.ps[hp:hp + 64, 6 + j % 2, 0:S],
                                          k.av[0:rows_, c, h * 64:(h + 1) * 64], k.apt[0:rows_, h % 2, c, :],
                                          start=(c == 0), stop=(c == 2))
                mm.then_inc(s_pv, 1)

            done(pe, s_pae, NA * b + NP // 2)
            done(pe, s_pde, ND * b + ND)
            if layer == 1:
                done(pe, s_rot, b + 1)
            scores(0)
            for h in range(NH):
                if h + 1 < NH:
                    scores(h + 1)
                transposes(h)
                if h == 0:
                    done(pe, s_pae, NA * b + NA)
                pv(h)
            done(pe, s_ot, NP * (b + 1))
            for qt in range(TB):
                for j in range(NP):
                    mm = nc.tensor.matmul(k.ps[:, 4, qt * D:(qt + 1) * D], k.aot[:, j, qt * P:(qt + 1) * P],
                                          w[:, wo_at + j * D:wo_at + (j + 1) * D], start=(j == 0), stop=(j == NP - 1))
            mm.then_inc(s_o, 1)

    @k.block.scalar
    def _(act):
        with act.Fori(0, B) as b:
            for n, (kind, x, g) in enumerate(act_jobs):
                done(act, s_pa, NA * b + n + 1)
                if kind == "q":
                    nc.scalar.activation(k.aq[:, 2 * x:2 * x + 2, :], k.ps[:, 0, :].rearrange("p (j q) -> p j q", j=2),
                                         ACT.Copy, scale=scale).then_inc(s_pae, 1)
                else:
                    rows_ = P if x < 2 else N
                    nc.scalar.activation(k.av[0:rows_, x, g * 512:(g + 1) * 512], k.ps[0:rows_, 0, :],
                                         ACT.Copy).then_inc(s_pae, 1)

            def exps(h):
                for qt in range(TB):
                    u = 2 * NH * b + 2 * h + qt
                    slot = (2 * h + qt) % 4
                    done(act, s_mx, u + 1)
                    done(act, s_t, NH * b + h - 1)
                    nc.scalar.activation(k.ap[:, slot, :], k.ps[:, 2 + qt, 0:KEYS], ACT.Exp, bias=k.anm[:, slot:slot + 1],
                                         scale=1.0, accum_out=k.asm[:, slot:slot + 1]).then_inc(s_e, 1)

            def oT(j):
                done(act, s_pv, NH * b + 2 * j + 2)
                nc.scalar.activation(k.aot[:, j, :], k.ps[:, 6 + j % 2, 0:S], ACT.Copy).then_inc(s_ot, 1)

            exps(0)
            for h in range(NH):
                if h + 1 < NH:
                    exps(h + 1)
                done(act, s_t, NH * b + h + 1)
                nc.scalar.activation(k.apt[:, h % 2, 0:2, :], k.ps[:, 4, :].rearrange("p (c q) -> p c q", c=2),
                                     ACT.Copy).then_inc(s_ta, 1)
                if h % 2 == 0 and h:
                    oT(h // 2 - 1)
            oT(NP - 1)

    @k.block.vector
    def _(dve):
        v = nc.vector
        with dve.Fori(0, B) as b:
            for n, (kind, j, _) in enumerate(dve_jobs):
                done(dve, s_pd, ND * b + n + 1)
                if kind == "swap":
                    bc = lambda name: const(k, name).unsqueeze(1).to_broadcast([P, NP, N])
                    v.tensor_tensor(k.arot[:, :, :], k.ps[:, 1, 0:NP * N].rearrange("p (j n) -> p j n", n=N), bc("sin1"),
                                    ALU.mult).then_inc(s_pde, 1)
                    done(dve, s_pde, ND * b + n + 1)
                    kc = k.ak[:, 0:NP, S:KEYS]
                    v.tensor_tensor(kc, kc, k.arot[:, :, :], ALU.add).then_inc(s_rot, 1)
                elif layer == 1:
                    v.tensor_copy(k.ak[:, j, 0:S], k.ps[:, 1, 0:S])
                    v.tensor_tensor(k.ak[:, j, S:KEYS], k.ps[:, 1, S:KEYS], const(k, "cos1"), ALU.mult).then_inc(s_pde, 1)
                else:
                    v.tensor_copy(k.ak[:, j, :], k.ps[:, 1, 0:KEYS]).then_inc(s_pde, 1)

            def maxes(h):
                for qt in range(TB):
                    slot = (2 * h + qt) % 4
                    done(dve, s_s, 2 * NH * b + 2 * h + qt + 1)
                    v.tensor_reduce(k.anm[:, slot:slot + 1], k.ps[:, 2 + qt, 0:KEYS], AX, ALU.max, negate=True)\
                        .then_inc(s_mx, 1)

            maxes(0)
            for h in range(NH):
                if h + 1 < NH:
                    maxes(h + 1)
                for qt in range(TB):
                    u, slot = 2 * NH * b + 2 * h + qt, (2 * h + qt) % 4
                    done(dve, s_e, u + 1)
                    v.reciprocal(k.asm[:, slot:slot + 1], k.asm[:, slot:slot + 1]).then_inc(s_rc, 1)
                for qt in range(TB):
                    u, slot = 2 * NH * b + 2 * h + qt, (2 * h + qt) % 4
                    done(dve, s_rc, u + 1)
                    v.tensor_scalar(k.ap[:, slot, :], k.ap[:, slot, :], k.asm[:, slot:slot + 1], None,
                                    ALU.mult).then_inc(s_pn, 1)
                done(dve, s_t, NH * b + h + 1)
                v.tensor_copy(k.apt[0:N, h % 2, 2, :], k.ps[0:N, 5, 0:S]).then_inc(s_tb, 1)
            done(dve, s_o, b + 1)
            x = k.X[:, bass.ds(b * TB, TB), :]
            v.tensor_tensor(x, x, k.ps[:, 4, 0:S].rearrange("p (t d) -> p t d", d=D), ALU.add).then_inc(s_x, 1)
        done(dve, s_x, B)
    give_credits(k)
    return lambda e: done(e, s_x, B)


def attention3(k, s_xT):
    nc, cs = k.nc, lambda n: k.csem(f"a3_{n}")
    s_q, s_rs, s_rot = cs("q"), cs("rope_steps"), cs("rope")
    s_s, s_mx, s_sh, s_e, s_sm, s_p = cs("scores"), cs("negmax"), cs("shifted"), cs("exp"), cs("sums"), cs("probs")
    s_t, s_te, s_vb, s_pv, s_c, s_o, s_x = (cs(n) for n in ("probsT", "probsT_out", "vspread", "pv", "ctxT", "out", "x"))
    NB = B
    tiled = lambda a: a.rearrange("p (h n) -> p h n", n=N)

    @k.block.tensor
    def _(pe):
        s_xT(pe)
        with pe.Fori(0, NB) as b:
            done(pe, s_rot, b)
            for n in range(2):
                mm = nc.tensor.matmul(k.ps[:, 0, n * S:(n + 1) * S], k.wa0[:, 4 + n, :], k.xT[:, bass.ds(b * S, S)],
                                      start=True, stop=True)
            mm.then_inc(s_q, 1)
            done(pe, s_rot, b + 1)
            for tt in range(TB):
                done(pe, s_sh, 2 * b + tt - 1)
                nc.tensor.matmul(k.ps[:, 1 + tt, 0:H3 * N], k.q3[:, tt * P:(tt + 1) * P],
                                 k.kbd3[:, bass.ds(b, 1), :, :], start=True, stop=False)
                for h in range(H3):
                    mm = nc.tensor.matmul(k.ps[:, 1 + tt, h * N:(h + 1) * N], k.ones[0:1, 0:P],
                                          k.mask[0:1, bass.ds(b * N, N)], start=False, stop=(h == H3 - 1))
                mm.then_inc(s_s, 1)
            for tt in range(TB):
                done(pe, s_p, 2 * b + tt + 1)
                done(pe, s_te, 2 * b + tt)
                for j in range(2):
                    mm = nc.tensor.transpose(k.ps[:, 3, j * P:(j + 1) * P], k.p3[:, tt, 2 * j:2 * j + 2, :],
                                             const(k, "ident"))
                mm.then_inc(s_t, 1)
            done(pe, s_te, 2 * b + 2)
            done(pe, s_vb, b + 1)
            for j in range(2):
                mm = nc.tensor.matmul(k.ps[:, 4, 0:S], k.vbd3[:, j, :], k.p3T[:, j, :], start=(j == 0), stop=(j == 1))
            mm.then_inc(s_pv, 1)
            done(pe, s_c, b + 1)
            done(pe, s_x, b)
            for tt in range(TB):
                mm = nc.tensor.matmul(k.ps[:, 5, tt * D:(tt + 1) * D], k.ctxT[:, tt * P:(tt + 1) * P], k.wa0[:, 9, :],
                                      start=True, stop=True)
            mm.then_inc(s_o, 1)

    @k.block.scalar
    def _(act):
        with act.Fori(0, NB) as b:
            for tt in range(TB):
                done(act, s_sh, 2 * b + tt + 1)
                nc.scalar.activation(k.p3[:, tt, :, :], k.p3[:, tt, :, :], ACT.Exp).then_inc(s_e, 1)
            for tt in range(TB):
                done(act, s_t, 2 * b + tt + 1)
                nc.scalar.activation(k.p3T[:, :, tt * P:(tt + 1) * P], k.ps[:, 3, 0:2 * P].rearrange("p (j q) -> p j q", j=2),
                                     ACT.Copy).then_inc(s_te, 1)
            done(act, s_pv, b + 1)
            nc.scalar.activation(k.ctxT[:, :], k.ps[:, 4, 0:S], ACT.Copy).then_inc(s_c, 1)

    @k.block.vector
    def _(dve):
        v = nc.vector
        with dve.Fori(0, NB) as b:
            done(dve, s_q, b + 1)
            v.scalar_tensor_tensor(k.q3[:, :], k.ps[:, 0, 0:S], HD3 ** -0.5, const(k, "cosq3"), ALU.mult, ALU.mult)\
                .then_inc(s_rs, 1)
            v.scalar_tensor_tensor(k.q3s[:, :], k.ps[:, 0, S:2 * S], HD3 ** -0.5, const(k, "sinq3"), ALU.mult, ALU.mult)\
                .then_inc(s_rs, 1)
            done(dve, s_rs, 2 * b + 2)
            v.tensor_tensor(k.q3[:, :], k.q3[:, :], k.q3s[:, :], ALU.add).then_inc(s_rot, 1)
            for tt in range(TB):
                done(dve, s_s, 2 * b + tt + 1)
                v.tensor_reduce(k.m3[:, tt, :], tiled(k.ps[:, 1 + tt, 0:H3 * N]), AX, ALU.max).then_inc(s_mx, 1)
                done(dve, s_mx, 2 * b + tt + 1)
                v.tensor_tensor(k.p3[:, tt, :, :], tiled(k.ps[:, 1 + tt, 0:H3 * N]),
                                k.m3[:, tt, :].unsqueeze(2).to_broadcast([P, H3, N]), ALU.subtract).then_inc(s_sh, 1)
            for tt in range(TB):
                done(dve, s_e, 2 * b + tt + 1)
                v.tensor_reduce(k.m3[:, tt, :], k.p3[:, tt, :, :], AX, ALU.add).then_inc(s_sm, 1)
                done(dve, s_sm, 4 * b + 2 * tt + 1)
                v.reciprocal(k.m3[:, tt, :], k.m3[:, tt, :]).then_inc(s_sm, 1)
                done(dve, s_sm, 4 * b + 2 * tt + 2)
                v.tensor_tensor(k.p3[:, tt, :, :], k.p3[:, tt, :, :],
                                k.m3[:, tt, :].unsqueeze(2).to_broadcast([P, H3, N]), ALU.mult).then_inc(s_p, 1)
            done(dve, s_o, b + 1)
            x = k.X[:, bass.ds(b * TB, TB), :]
            v.tensor_tensor(x, x, k.ps[:, 5, 0:S].rearrange("p (t d) -> p t d", d=D), ALU.add).then_inc(s_x, 1)
        done(dve, s_x, B)

    @k.block.gpsimd
    def _(pool):
        s_xT(pool)
        with pool.Fori(0, NB) as b:
            done(pool, s_pv, b)
            nc.gpsimd.tensor_tensor(k.vbd3[:, :, :], k.v3[:, bass.ds(b, 1), :].to_broadcast([P, 2, D]),
                                    const(k, "pair3").rearrange("p (j d) -> p j d", j=2), ALU.mult).then_inc(s_vb, 1)
    give_credits(k)
    return lambda e: done(e, s_x, B)


def ffn2(k, s_xT, before):
    nc, cs = k.nc, lambda n: k.csem(f"f2_{n}")
    GROUPS = 2
    s_w, s_dn = [k.sem("f2_w0"), k.sem("f2_w1")], cs("down")
    s_up, s_h, s_acc, s_add = cs("products"), cs("h"), cs("acc"), cs("add")
    s_z, s_za, s_st, s_mv, s_r, s_rp, s_zn = (cs(n) for n in ("z", "z_out", "z_stats", "z_moments", "z_rstd", "z_rstd_steps", "z_normed"))
    s_sw = {n: k.sem(f"f2_spec_{n}_loaded") for n in ("0", "1a", "1b", "2")}
    at = {"0": (0, 2048), "1a": (2048, 3072), "1b": (3072, 4096), "2": (4096, 6144)}
    spec = {n: k.ws2[:, a:b] for n, (a, b) in at.items()}
    cb_ready = router(k, 2, s_xT, s_w)

    order = ["U00", "U01", "Z00", "Z01", "U10", "R00", "D00", "U11", "R01", "D01", "A10", "A11", "Z10", "Z11",
             "U20", "R10", "D10", "U21", "R11", "D11", "S20", "S21", "U30", "D20", "U31", "D21", "D30", "D31"]
    jobs = [(o[0], int(o[1]), int(o[2])) for o in order]
    banks = {"U": 4, "R": 4, "A": 2, "S": 4}
    index, last, before_bank, n = {}, {}, {}, 0
    for job in jobs:
        if job[0] in banks:
            for f in range(banks[job[0]]):
                index[job + (f,)] = n
                before_bank[job + (f,)] = last.get(f)
                last[f] = n
                n += 1
    PER = n
    for key, v in before_bank.items():
        if v is None:
            before_bank[key] = last[key[3]] - PER
    downs = [j for j in jobs if j[0] == "D"]
    zs = [j for j in jobs if j[0] == "Z"]

    @k.block.tensor
    def _(pe):
        pe_ = nc.tensor
        cb_ready(pe)
        with pe.Fori(0, GROUPS) as i:
            for job in jobs:
                kind, e, half = job
                cols = slice(half * 512, (half + 1) * 512)
                wf = lambda a, c: k.wf[:, e % 2, a + c * P:a + (c + 1) * P]

                def product(f, lhs, rhs, chunks):
                    done(pe, s_h, PER * i + before_bank[job + (f,)] + 1)
                    for c in range(chunks):
                        mm = pe_.matmul(k.ps[:, f, :], lhs(c), rhs(c), start=(c == 0), stop=(c == chunks - 1))
                    mm.then_inc(s_up, 1)

                if kind == "U":
                    if half == 0:
                        pe.wait_ge(s_w[e % 2], 32 * i + 16 * (e // 2 + 1))
                    for f in range(FC):
                        product(f, lambda c: wf(0, f), lambda c: k.xT[:, cols], 1)
                elif kind in "AS":
                    name = "1a" if kind == "A" else "2"
                    width = 256 if kind == "A" else F
                    src = index[("U", e, half, FC - 1)]
                    pe.wait_ge(s_sw[name], 16 * i + 16)
                    done(pe, s_h, PER * i + src + 1)
                    for f in range(banks[kind]):
                        product(f, lambda c: spec[name][:, c * width + f * P:c * width + (f + 1) * P],
                                lambda c: k.h[:, half, c, :], FC)
                elif kind == "Z":
                    name, chunks, h = ("0", FC, k.h) if e == 0 else ("1b", 2, k.t1)
                    src = index[("U", e, half, FC - 1) if e == 0 else ("A", e, half, 1)]
                    pe.wait_ge(s_sw[name], 16 * i + 16)
                    done(pe, s_h, PER * i + src + 1)
                    for tt in range(4):
                        n = 16 * i + 4 * zs.index(job) + tt
                        done(pe, s_za, n - 1)
                        for c in range(chunks):
                            mm = pe_.matmul(k.ps[:, 6 + tt % 2, :], h[:, half, c, tt * P:(tt + 1) * P],
                                            spec[name][:, c * F:(c + 1) * F], start=(c == 0), stop=(c == chunks - 1))
                        mm.then_inc(s_z, 1)
                elif kind == "R":
                    z = zs.index(("Z", e, half))
                    done(pe, s_zn, 16 * i + 4 * z + 4)
                    for f in range(FC):
                        done(pe, s_h, PER * i + before_bank[job + (f,)] + 1)
                        for tt in range(4):
                            mm = pe_.transpose(k.ps[:, f, tt * P:(tt + 1) * P], k.z[:, half, tt, f * P:(f + 1) * P],
                                               const(k, "ident"))
                        mm.then_inc(s_up, 1)
                else:
                    d = downs.index(job)
                    src = index[({0: "R", 1: "R", 2: "S", 3: "U"}[e], e, half, FC - 1)]
                    h = k.h if e == 3 else k.h2
                    done(pe, s_acc, 8 * i + d - 1)
                    done(pe, s_h, PER * i + src + 1)
                    for f in range(FC):
                        mm = pe_.matmul(k.ps[:, 4 + half, :], wf(F, f), h[:, half, f, :], start=(f == 0), stop=(f == FC - 1))
                    mm.then_inc(s_dn, 1)

    @k.block.scalar
    def _(act):
        a = nc.scalar.activation
        with act.Fori(0, GROUPS) as i:
            for job in jobs:
                kind, e, half = job
                if kind not in banks:
                    continue
                v = lambda name, per, f: k.vecs[:, bass.ds(VEC[name][0] + per * i + f, 1)]
                for f in range(banks[kind]):
                    done(act, s_up, PER * i + index[job + (f,)] + 1, k.turn_act)
                    src = k.ps[:, f, :]
                    if kind == "U":
                        m = a(k.h[:, half, f, :], src, ACT.Gelu, bias=v("up_b", 4 * FC, e * FC + f), scale=1.0)
                    elif kind == "A":
                        m = a(k.t1[:, half, f, :], src, ACT.Gelu, bias=v("s1a_b", 2, f), scale=1.0)
                    elif kind == "S":
                        m = a(k.h2[:, half, f, :], src, ACT.Gelu, bias=v("s2_b", FC, f), scale=1.0)
                    elif e == 0:
                        m = a(k.h2[:, half, f, :], src, ACT.Gelu, bias=v("ln0_b", FC, f), scale=v("ln0_g", FC, f))
                    else:
                        m = a(k.h2[:, half, f, :], src, ACT.Identity, bias=v("ln1_b", FC, f), scale=v("ln1_g", FC, f))
                    m.then_inc(s_h, 1)

    @k.block.vector
    def _(dve):
        v = nc.vector
        with dve.Fori(0, GROUPS) as i:
            def stats(job):
                z = zs.index(job)
                _, e, half = job
                name = "s0_b" if e == 0 else "s1b_b"
                for tt in range(4):
                    n = 16 * i + 4 * z + tt
                    done(dve, s_z, n + 1)
                    v.tensor_tensor(k.z[:, half, tt, :], k.ps[:, 6 + tt % 2, :],
                                    k.rowv[:, bass.ds(ROW[name][0] + F * i, F)], ALU.add).then_inc(s_za, 1)
                for tt in range(4):
                    n = 16 * i + 4 * z + tt
                    done(dve, s_za, n + 1)
                    v.bn_stats(k.stat[:, tt, :], k.z[:, half, tt, :]).then_inc(s_st, 1)
                done(dve, s_st, 16 * i + 4 * z + 4, k.turn_dve)
                for tt in range(4):
                    v.bn_aggr(k.mv[:, 4 * half + tt, :], k.stat[:, tt, :]).then_inc(s_mv, 1)

            def norm(job):
                z = zs.index(job)
                half = job[2]
                done(dve, s_r, 4 * i + z + 1)
                for tt in range(4):
                    t = 4 * half + tt
                    v.tensor_scalar(k.z[:, half, tt, :], k.z[:, half, tt, :], k.mv[:, t, 0:1], k.r1[:, t:t + 1],
                                    ALU.subtract, ALU.mult).then_inc(s_zn, 1)

            for e in range(4):
                if e < 2:
                    for half in range(2):
                        stats(("Z", e, half))
                    for half in range(2):
                        norm(("Z", e, half))
                for half in range(2):
                    accumulate(k, dve, s_dn, s_acc, s_add, 8 * i + 2 * e + half, half, 4 * i + e, "down_b")

    @k.block.gpsimd
    def _(pool):
        with pool.Fori(0, GROUPS) as i:
            for z, (_, e, half) in enumerate(zs):
                r = k.r1[:, 4 * half:4 * half + 4]
                done(pool, s_mv, 16 * i + 4 * z + 4, k.turn_pool)
                nc.gpsimd.tensor_scalar(r, k.mv[:, 4 * half:4 * half + 4, 1], EPS, None, ALU.add).then_inc(s_rp, 1)
                done(pool, s_rp, 4 * i + z + 1)
                nc.gpsimd.tensor_tensor(r, r, k.mhalf[:, 0:4], ALU.pow).then_inc(s_r, 1)


    @k.block.sync
    def _(sp):
        give(k, sp)
        wf = k.d["wf2"]
        for n, (a, b) in at.items():
            sp.dma_start(k.ws2[:, a:b], k.d["ws2"][0, :, a:b]).then_inc(s_sw[n], 16)
        before(sp)
        for j in range(2):
            sp.dma_start(k.wf[:, j, 0:2 * F], wf[j, :, :]).then_inc(s_w[j], 16)
        for e in range(2, E):
            done(sp, s_dn, 2 * e - 2)
            sp.dma_start(k.wf[:, e % 2, 0:2 * F], wf[e, :, :]).then_inc(s_w[e % 2], 16)
            if e in (2, 3, 4):
                for n in {2: ("0",), 3: ("1a", "1b"), 4: ("2",)}[e]:
                    a, b = at[n]
                    sp.dma_start(k.ws2[:, a:b], k.d["ws2"][1, :, a:b]).then_inc(s_sw[n], 16)
    return residual(k, "f2", s_add, 2 * E)


def ffn3(k, s_xT, before):
    nc, cs = k.nc, lambda n: k.csem(f"f3_{n}")
    s_w, s_dn = [k.sem("f3_w0"), k.sem("f3_w1")], cs("down")
    s_up, s_g, s_h, s_acc, s_add = cs("up"), cs("gate"), cs("h"), cs("acc"), cs("add")
    router(k, 3, s_xT, s_w)

    @k.block.tensor
    def _(pe):
        with pe.Fori(0, E // 2) as i:
            def up(j, half):
                u = 4 * i + 2 * j + half
                if half == 0:
                    pe.wait_ge(s_w[j], 16 * i + 16)
                for f in range(FC):
                    done(pe, s_h, 4 * u + f - 1)
                    for g in (1, 0):
                        mm = nc.tensor.matmul(k.ps[:, 2 * (f % 2) + g, :], k.wf[:, j, g * F + f * P:g * F + (f + 1) * P],
                                              k.xT[:, half * 512:(half + 1) * 512], start=True, stop=True)
                    mm.then_inc(s_up, 1)

            def down(j, half):
                u = 4 * i + 2 * j + half
                done(pe, s_acc, u - 1)
                done(pe, s_h, 4 * u + FC)
                for f in range(FC):
                    mm = nc.tensor.matmul(k.ps[:, 4 + half, :], k.wf[:, j, 2 * F + f * P:2 * F + (f + 1) * P],
                                          k.h[:, half, f, :], start=(f == 0), stop=(f == FC - 1))
                mm.then_inc(s_dn, 1)
            up(0, 0)
            up(0, 1)
            down(0, 0)
            up(1, 0)
            down(0, 1)
            up(1, 1)
            down(1, 0)
            down(1, 1)

    @k.block.scalar
    def _(act):
        with act.Fori(0, E // 2) as i:
            for ju in range(4):
                for f in range(FC):
                    n = 16 * i + 4 * ju + f
                    done(act, s_up, n + 1)
                    done(act, s_h, n - 1)
                    nc.scalar.activation(k.gate[:, f % 2, :], k.ps[:, 2 * (f % 2) + 1, :], ACT.Silu).then_inc(s_g, 1)

    @k.block.vector
    def _(dve):
        with dve.Fori(0, E // 2) as i:
            def hidden(ju):
                for f in range(FC):
                    n = 16 * i + 4 * ju + f
                    done(dve, s_g, n + 1)
                    nc.vector.tensor_tensor(k.h[:, ju % 2, f, :], k.ps[:, 2 * (f % 2), :], k.gate[:, f % 2, :],
                                            ALU.mult).then_inc(s_h, 1)

            def add(ju):
                accumulate(k, dve, s_dn, s_acc, s_add, 4 * i + ju, ju % 2, 2 * i + ju // 2, "zero8")
            hidden(0)
            hidden(1)
            add(0)
            hidden(2)
            add(1)
            hidden(3)
            add(2)
            add(3)
    load_experts(k, k.d["wf3"], before, s_w, s_dn)
    return residual(k, "f3", s_add, 2 * E)




def program(nc, d):
    with ExitStack() as ctx:
        k = State()
        k.nc, k.d, k.credited = nc, d, []
        sb = lambda name, shape, dt=F32: ctx.enter_context(nc.sbuf_tensor(name, shape, dt))
        k.sem = lambda name: ctx.enter_context(nc.semaphore(name))

        def csem(name):
            s = k.sem(name)
            k.credited.append(s)
            return s
        k.csem = csem
        shared = {}

        def shared_sem(name, total):
            if name not in shared:
                shared[name] = [k.sem(name), 0]
            sem, base = shared[name]
            shared[name][1] += total
            return sem, base
        k.shared = shared_sem
        own = {}

        def steps(engine):
            key = "pool" if "GpSimd" in type(engine).__name__ or "Pool" in type(engine).__name__ else "dve"
            if key not in own:
                own[key] = Steps(k.sem(f"{key}_steps"))
            own[key].engine = engine
            return own[key]
        k.steps = steps

        k.ps = ctx.enter_context(nc.psum_tensor("ps", [P, 8, 512], F32))
        k.X = sb("x_res", [P, T, D])
        k.xh = sb("xhat", [P, T, D])
        k.xT = sb("xT", [P, T * P])
        k.acc = k.xh[:, :, :].rearrange("p t d -> p (t d)")
        k.ctx = sb("ctx_sb", [P, 2, D])
        k.consts = sb("consts_sb", [P, NCONST])
        k.vecs = sb("vecs_sb", [P, NVEC])
        k.rowv = sb("rows_sb", [P, NROW])
        k.sel = sb("sel_sb", [E, E, P])
        k.wr = sb("wr_sb", [P, 4, E])
        k.wa0 = sb("wa0_sb", [P, 10, P])
        k.mask_u8 = sb("mask_u8", [1, B * N], U8)
        k.maskf = sb("maskf", [1, B * N])
        k.mask = sb("mask_sb", [1, B * N])
        k.mhalf = sb("mhalf", [P, 8])
        k.ones = sb("ones", [1, 512])
        k.stat = sb("stat", [P, T, 6])
        k.mv = sb("mv", [P, T, 2])
        k.r1 = sb("r1", [P, T])
        k.r2 = sb("r2", [P, T])
        k.rms1 = sb("rms1", [P, 1])
        k.c1T, k.c2T, k.c3T, k.k3T = (sb(n, [P, B * N]) for n in ("c1T", "c2T", "c3T", "k3T"))
        k.v3 = sb("v3", [P, B, D])
        k.kbd3 = sb("kbd3", [P, B, H3, N])
        k.y = sb("y", [P, TB, D])
        k.ctxT = sb("ctxT", [P, S])
        k.qT = sb("qT", [P, S])

        k.wa2 = sb("wa_sb", [P, 32 * P])
        k.wa1 = k.wa2[:, 0:20 * P]
        k.ws2 = sb("ws2_sb", [P, 12 * F])
        k.wf = sb("wf_sb", [P, 2, 3 * F])
        k.lg, k.pr, k.comb, k.oh, k.mx = (sb(n, [P, T, E]) for n in ("r_lg", "r_pr", "r_comb", "r_oh", "r_mx"))
        k.ix = sb("r_ix", [P, T, 8], U32)
        k.ixf = sb("r_ixf", [P, T, 2])
        k.sm = sb("r_sm", [P, T])

        with ExitStack() as c0:
            s0 = lambda name, shape, dt=F32: c0.enter_context(nc.sbuf_tensor(name, shape, dt))
            k.sc = s0("a0_sc", [P, TB, H0, N])
            k.w = s0("a0_w", [P, TB, H0, N])
            k.ex = s0("a0_ex", [P, TB, H0, N])
            k.prob = s0("a0_prob", [P, TB, H0, N])
            k.probT = s0("a0_probT", [P, 8, S])
            k.vbd = s0("a0_vbd", [P, 8, D])
            k.top1 = s0("a0_top1", [P, TB, H0, 8])
            k.top = s0("a0_top", [P, H0, 8])
            k.nb = s0("a0_nb", [P, TB, H0])
            k.rden = s0("a0_rden", [P, S])
            k.dup3 = s0("dup3", [P, B, 2, N])
            k.c0T, k.k0T, k.k3s = (s0(n, [P, B * N]) for n in ("c0T", "k0T", "k3s"))
            k.dup = s0("dup", [P, B, 2, N])
            k.v0 = s0("v0", [P, B, D])
            k.kbd0 = s0("kbd0", [P, B, H0, N])
        with ExitStack() as c1:
            s1 = lambda name, shape, dt=F32: c1.enter_context(nc.sbuf_tensor(name, shape, dt))
            k.cb = s1("f_cb", [P, E, T * P])
            k.h = s1("f_h", [P, 2, FC, 512])
            k.tmp = s1("f_tmp", [P, 2, 512])
            k.combT = s1("f_combT", [E, T * P])
            k.h2 = s1("f2_h2", [P, 2, FC, 512])
            k.t1 = s1("f2_t1", [P, 2, 2, 512])
            k.z = s1("f2_z", [P, 2, 4, F])
            k.gate = k.z[:, 0, :, :]
        with ExitStack() as c2:
            s2 = lambda name, shape, dt=F32: c2.enter_context(nc.sbuf_tensor(name, shape, dt))
            k.q3 = s2("a3_q", [P, S])
            k.q3s = s2("a3_qs", [P, S])
            k.p3 = s2("a3_p", [P, TB, H3, N])
            k.p3T = s2("a3_pT", [P, 2, S])
            k.vbd3 = s2("a3_vbd", [P, 2, D])
            k.m3 = s2("a3_m", [P, TB, H3])
            k.at = s2("a_in", [P, S + N])
            k.aq = s2("a_q", [P, 8, S])
            k.ak = s2("a_k", [P, 8, S + N])
            k.av = s2("a_v", [P, 3, 8 * P])
            k.ap = s2("a_probs", [P, 4, S + N])
            k.apt = s2("a_probsT", [P, 2, 3, S])
            k.aot = s2("a_oT", [P, 8, S])
            k.first = k.aot[:, 0:4, :].rearrange("p j q -> p (j q)")
            k.arot = s2("a_rot", [P, 4, N])
            k.anm = s2("a_negmax", [P, 4])
            k.asm = s2("a_sums", [P, 4])
        k.block = ctx.enter_context(nc.Block())
        s_out = k.sem("out_stored")
        load_constants(k)
        context(k)
        s_xT = normalize(k, "n0", lambda e: e.wait_ge(k.s_x, 16))
        ready = attention0(k, s_xT)
        give_credits(k)
        nothing = lambda e: None
        s_xT = normalize(k, "n1", ready)
        ready = ready_ff = ffn(k, 0, s_xT, nothing, ACT.Gelu, None, "zero8")
        s_xT = normalize(k, "n2", ready, second=EPS, xT_scale=vec(k, "gl1"), xT_bias=vec(k, "bl1"))
        ready = attention12(k, 1, s_xT)
        @k.block.sync
        def _(sp, ready=ready):
            ready(sp)
            sp.dma_start(k.wa2[:, :], d["wa2"]).then_inc(k.s_wa[2], 16)
        s_xT = normalize(k, "n3", ready)
        ready = ready_ff = ffn(k, 1, s_xT, ready_ff, ACT.Relu, "b1_1", "b2_1")
        s_xT = normalize(k, "n4", ready, second=EPS, xT_scale=vec(k, "g2_2"), xT_bias=vec(k, "b2_2"))
        ready = attention12(k, 2, s_xT)
        s_xT = normalize(k, "n5", ready, second=EPS, xT_scale=vec(k, "ln_g"), xT_bias=vec(k, "ln_b"), keep_first=True)
        ready = ready_ff = ffn2(k, s_xT, ready_ff)
        s_xT = normalize(k, "n6", ready, second=1e-6, xT_scale=k.rms1[:, 0:1])
        ready = attention3(k, s_xT)
        s_xT = normalize(k, "n7", ready)
        ready = ffn3(k, s_xT, ready_ff)
        give_credits(k)

        @k.block.sync
        def _(sp):
            ready(sp)
            sp.dma_start(d["out"].rearrange("(t p) d -> p t d", p=P), k.X[:, :, :]).then_inc(s_out, 16)
            sp.wait_ge(s_out, 16)


def constants():
    p = np.arange(P)
    c = np.zeros((P, NCONST), np.float32)

    def put(name, a):
        c[:, CONST[name][0]:CONST[name][1]] = a
    put("ident", np.eye(P))
    col = np.arange(D)
    put("pair0", np.concatenate([(col[None] // HD0 == 2 * j + p[:, None] // N) for j in range(8)], 1))
    put("pair3", np.concatenate([(col[None] // HD3 == 2 * j + p[:, None] // N) for j in range(2)], 1))
    put("head0", p[:, None] // HD0 == np.arange(H0)[None])
    put("head3", p[:, None] // HD3 == np.arange(H3)[None])
    put("iota8", np.arange(E)[None])

    def rope(dim, freq, pos):
        half = dim // 2
        ang = (pos[None, :].astype(np.float32) * freq[(p % dim) % half][:, None]).astype(np.float32)
        sign = np.where(p % dim < half, -1.0, 1.0)[:, None]
        return np.cos(ang), np.sin(ang) * sign
    f1 = (1.0 / 10000.0 ** (np.arange(0, 64, 2, dtype=np.float32) / 64)).astype(np.float32)
    a, b = rope(64, f1, np.arange(N))
    put("cos1", a), put("sin1", b)
    f3 = (1.0 / 10000.0 ** (np.float32(2.0 / 32) * np.arange(16, dtype=np.float32))).astype(np.float32)
    a, b = rope(32, f3, np.arange(N, N + S))
    put("cosq3", a), put("sinq3", b)
    a, b = rope(32, f3, np.arange(N))
    put("cosk3", a), put("sink3", b)
    sel = np.zeros((E, E, P), np.float32)
    sel[np.arange(E), np.arange(E)] = 1.0
    return c, sel


def swap_halves(w, dim):
    a = w.reshape(w.shape[0], -1, 2, dim // 2)
    return np.ascontiguousarray(a[:, :, ::-1]).reshape(w.shape)


def layout(i):
    g = {n: np.asarray(a) for n, a in i.items()}
    c, sel = constants()
    col = lambda a: a.reshape(-1, P).T
    vecs = {"bq0": g["L0_xattn_bq"], "bk0": g["L0_xattn_bk"], "gx1": g["L1_xattn_gamma_x"], "bx1": g["L1_xattn_beta_x"],
            "gl1": g["L1_xattn_gamma_l"], "bl1": g["L1_xattn_beta_l"], "b1_1": g["L1_ffn_b1"], "b2_1": g["L1_ffn_b2"],
            "g1_2": g["L2_xattn_g1"], "b1_2": g["L2_xattn_b1"], "g2_2": g["L2_xattn_g2"], "b2_2": g["L2_xattn_b2"],
            "ln_g": g["L2_ffn_ln_g"], "ln_b": g["L2_ffn_ln_b"], "up_b": g["L2_ffn_up_b"], "down_b": g["L2_ffn_down_b"],
            "ln0_g": g["L2_ffn_ln0_g"], "ln0_b": g["L2_ffn_ln0_b"], "s1a_b": g["L2_ffn_spec1a_b"],
            "ln1_g": g["L2_ffn_ln1_g"], "ln1_b": g["L2_ffn_ln1_b"], "s2_b": g["L2_ffn_spec2_b"],
            "rms": g["L3_xattn_rms_scale"], "zero8": np.zeros(E * P, np.float32)}
    rows_ = {"bv0": g["L0_xattn_bv"], "bo0": g["L0_xattn_bo"], "rb0": g["L0_ffn_router_b"], "br1": g["L1_ffn_br"],
             "s0_b": g["L2_ffn_spec0_b"], "s1b_b": g["L2_ffn_spec1b_b"]}
    kv = g["L3_xattn_kv_w"][:, 0]
    q3 = g["L3_xattn_q_w"].transpose(1, 0, 2).reshape(D, D)
    k3, v3 = np.tile(kv[0], (1, H3)), np.tile(kv[1], (1, H3))
    wa0 = np.stack([g["L0_xattn_Wq"].T, g["L0_xattn_Wk"].T, g["L0_xattn_Wv"].T, g["L0_xattn_Wo"].T,
                    q3, swap_halves(q3, HD3), k3, swap_halves(k3, HD3), v3, g["L3_xattn_out_w"].reshape(D, D)], 1)
    wr = np.stack([g["L0_ffn_router_w"], g["L1_ffn_Wr"].T, g["L2_ffn_router_w"], g["L3_ffn_Wr"]], 1)
    a = {"x": g["x"].reshape(B * S, D), "ctx": g["ctx_1024"].reshape(B * N, D),
         "mask": g["mask_BxS2_bk0"].reshape(1, B * N), "consts": c, "sel": sel,
         "vecs": np.concatenate([col(vecs[n]) for n in VEC], 1), "rows": np.concatenate([rows_[n].reshape(-1) for n in ROW]),
         "wa0": wa0, "wr": wr}
    up = lambda w: w
    down = lambda w: w.reshape(-1, w.shape[1] // P, P, w.shape[2]).transpose(0, 2, 1, 3).reshape(w.shape[0], P, -1)
    a["wf0"] = np.concatenate([up(g["L0_ffn_expert_up"].transpose(0, 2, 1)), down(g["L0_ffn_expert_down"].transpose(0, 2, 1))], 2)
    a["wf1"] = np.concatenate([up(g["L1_ffn_W1"].transpose(0, 2, 1)), down(g["L1_ffn_W2"].transpose(0, 2, 1))], 2)
    rows_of = lambda w: w.reshape(-1, P, w.shape[1]).transpose(1, 0, 2).reshape(P, -1)
    wkv1 = g["L1_xattn_Wkv"]
    a["wa1"] = np.concatenate([g["L1_xattn_Wq"], wkv1, swap_halves(wkv1[:, :512], 64), rows_of(g["L1_xattn_Wo"])], 1)
    a["wa2"] = np.concatenate([g["L2_xattn_Wq"], g["L2_xattn_Wkv"], rows_of(g["L2_xattn_Wout"])], 1)
    a["wf2"] = np.concatenate([g["L2_ffn_up_W"], down(g["L2_ffn_down_W"])], 2)
    a["ws2"] = np.concatenate([down(g["L2_ffn_spec0_W"]), down(g["L2_ffn_spec1a_W"]), down(g["L2_ffn_spec1b_W"]),
                               down(g["L2_ffn_spec2_W"])], 2)
    cat = lambda w, s: np.concatenate([w, s[None]], 0)
    a["wf3"] = np.concatenate([cat(g["L3_ffn_Wu"], g["L3_ffn_Wu_s"]), cat(g["L3_ffn_Wg"], g["L3_ffn_Wg_s"]),
                               down(cat(g["L3_ffn_Wd"], g["L3_ffn_Wd_s"]))], 2)
    return {n: np.ascontiguousarray(v) for n, v in a.items()}


def kernel(**inputs):
    import concourse.bacc as _bacc
    from concourse.bass_utils import run_bass_kernel_spmd as _run

    nc = _bacc.Bacc("TRN2", target_bir_lowering=False, num_devices=1)
    a = layout(inputs)
    arrays, d = {}, {}
    for n, v in a.items():
        arrays[f"{n}_dram"] = v
        d[n] = nc.dram_tensor(f"{n}_dram", v.shape, mybir.dt.from_np(v.dtype), kind="ExternalInput").ap()
    d["out"] = nc.dram_tensor("out_dram", (B * S, D), F32, kind="ExternalOutput").ap()
    program(nc, d)
    r = _run(nc, [arrays], core_ids=[0])
    return r.results[0]["out_dram"].reshape(B, S, D)
```

```python
from contextlib import ExitStack

import numpy as np

import concourse.bass as bass
from concourse import mybir

F32 = mybir.dt.float32
U32 = mybir.dt.uint32
U8 = mybir.dt.uint8
ALU = mybir.AluOpType
ACT = mybir.ActivationFunctionType
AX = mybir.AxisListType.X

P = 128
B, S, N, D = 4, 256, 64, 128
T = B * S // P
TB = S // P
E, F = 8, 512
FC = F // P
H0, HD0 = 16, 8
H3, HD3 = 4, 32
TOPK = 32
EPS = 1e-5
NEG = -3.0e38
MASKED = -2.0 ** 100

CONST = {}
_at = 0
for _name, _n in (("ident", P), ("pair0", 8 * P), ("head0", H0), ("pair3", 2 * P), ("head3", H3), ("iota8", E),
                  ("cos1", N), ("sin1", N), ("cosq3", S), ("sinq3", S), ("cosk3", N), ("sink3", N)):
    CONST[_name] = (_at, _at + _n)
    _at += _n
NCONST = _at

VEC = {}
_at = 0
for _name, _n in (("bq0", 1), ("bk0", 1), ("gx1", 1), ("bx1", 1), ("gl1", 1), ("bl1", 1), ("b1_1", E * FC),
                  ("g1_2", 1), ("b1_2", 1), ("g2_2", 1), ("b2_2", 1), ("ln_g", 1), ("ln_b", 1), ("up_b", E * FC),
                  ("ln0_g", 2 * FC), ("ln0_b", 2 * FC), ("s1a_b", 4), ("ln1_g", 2 * FC),
                  ("ln1_b", 2 * FC), ("s2_b", 2 * FC), ("rms", 1)):
    VEC[_name] = (_at, _at + _n)
    _at += _n
NVEC = _at

ROW = {}
_at = 0
for _name, _n in (("bv0", D), ("bo0", D), ("rb0", E), ("br1", E), ("s0_b", 2 * F), ("s1b_b", 2 * F)):
    ROW[_name] = (_at, _at + _n)
    _at += _n
NROW = _at


CREDIT = 4


def done(engine, sem, count, turn=None):
    engine.wait_ge(sem, count + CREDIT)
    if turn is not None:
        engine.sem_inc(turn, 1)


class State:
    pass


class Steps:

    def __init__(self, sem):
        self.engine, self.sem, self.n = None, sem, 0

    def add(self, instruction):
        instruction.then_inc(self.sem, 1)
        self.n += 1

    def wait(self):
        self.engine.wait_ge(self.sem, self.n)


def const(k, name):
    a, b = CONST[name]
    return k.consts[:, a:b]


def vec(k, name, i=0, n=1):
    a = VEC[name][0] + i
    return k.vecs[:, a:a + n]


def rows(k, name, i=0, n=None):
    a, b = ROW[name]
    return k.rowv[:, a + i:(b if n is None else a + i + n)]


def load_constants(k):
    d, sem = k.d, k.sem
    k.s_x, k.s_ctx, k.s_const = sem("x_loaded"), sem("ctx_loaded"), sem("constants_loaded")
    k.s_setup = sem("memsets_done")
    k.s_wa = {1: sem("wa1_loaded"), 2: sem("wa2_loaded")}
    k.turn_dve, k.turn_pool, k.turn_act = sem("dve_turns"), sem("pool_turns"), sem("act_turns")

    @k.block.sync
    def _(sp):
        sp.dma_start(k.X[:, :, :], d["x"].rearrange("(t p) d -> p t d", p=P)).then_inc(k.s_x, 16)
        sp.dma_start(k.ctx[:, :, :], d["ctx"].rearrange("(t p) d -> p t d", p=P)).then_inc(k.s_ctx, 16)
        sp.dma_start(k.wa1, d["wa1"]).then_inc(k.s_wa[1], 16)

    @k.block.scalar
    def _(act):
        act.dma_start(k.consts[:, :], d["consts"]).then_inc(k.s_const, 16)
        act.dma_start(k.vecs[:, :], d["vecs"]).then_inc(k.s_const, 16)
        act.dma_start(k.wa0[:, :, :], d["wa0"]).then_inc(k.s_const, 16)
        act.dma_start(k.rowv[:, :], d["rows"].partition_broadcast(P)).then_inc(k.s_const, 16)
        act.dma_start(k.bias2[:, :], d["bias2"]).then_inc(k.s_const, 16)
        act.dma_start(k.wr[:, :, :], d["wr"]).then_inc(k.s_const, 16)
        act.dma_start(k.mask_u8[:, :], d["mask"]).then_inc(k.s_const, 16)

    @k.block.gpsimd
    def _(pool):
        pool.memset(k.mhalf[:, :], -0.5).then_inc(k.s_setup, 1)
        pool.memset(k.ones[:, :], 1.0).then_inc(k.s_setup, 1)


def give_credits(k):
    @k.block.sync
    def _(sp):
        give(k, sp)


CONSTS_LOADED = 7 * 16


def statistics(k, tag, x, tiles, ready):
    s_stat, b_stat = k.shared("norm_stats", tiles)
    s_mv, b_mv = k.shared("norm_moments", tiles)

    @k.block.vector
    def _(dve):
        for t in range(tiles):
            ready(dve, t)
            dve.bn_stats(k.stat[:, t, :], x[:, t, :]).then_inc(s_stat, 1)
        for t in range(tiles):
            dve.wait_ge(s_stat, b_stat + t + 1)
            dve.bn_aggr(k.mv[:, t, :], k.stat[:, t, :]).then_inc(s_mv, 1)
    return lambda e: e.wait_ge(s_mv, b_mv + tiles)


def pool_rsqrt(k, st, out, in_, eps, n):
    st.add(k.nc.gpsimd.tensor_scalar(out, in_, eps, None, ALU.add))
    st.wait()
    st.add(k.nc.gpsimd.tensor_tensor(out, out, k.mhalf[:, 0:n], ALU.pow))
    st.wait()


def normalize(k, tag, ready, second=None, xT_scale=1.0, xT_bias=0.0, setup=False):
    nc = k.nc
    s_mv = statistics(k, tag, k.X, T, ready)
    (s_r, b_r), (s_xh, b_xh) = k.shared("norm_rstd", 1), k.shared("norm_xhat", T)
    (s_tr, b_tr), (s_xT, b_xT) = k.shared("norm_transposed", T), k.shared("norm_xT", 2)

    @k.block.gpsimd
    def _(pool):
        st = k.steps(pool)
        pool.wait_ge(k.s_setup, 2)
        s_mv(pool)
        var = k.mv[:, 0:T, 1]
        pool_rsqrt(k, st, k.r1[:, :], var, EPS, T)
        last = k.r1
        if second is not None:
            st.add(nc.gpsimd.tensor_tensor(k.r2[:, :], var, k.r1[:, :], ALU.mult))
            st.wait()
            st.add(nc.gpsimd.tensor_tensor(k.r2[:, :], k.r2[:, :], k.r1[:, :], ALU.mult))
            st.wait()
            pool_rsqrt(k, st, k.r2[:, :], k.r2[:, :], second, T)
            st.add(nc.gpsimd.tensor_tensor(k.r2[:, :], k.r2[:, :], k.r1[:, :], ALU.mult))
            st.wait()
        pool.sem_inc(s_r, 1)

    r = k.r1 if second is None else k.r2

    @k.block.vector
    def _(dve):
        dve.wait_ge(s_r, b_r + 1)
        for t in range(T):
            nc.vector.tensor_scalar(k.xh[:, t, :], k.X[:, t, :], k.mv[:, t, 0:1], r[:, t:t + 1],
                                    ALU.subtract, ALU.mult).then_inc(s_xh, 1)

    @k.block.tensor
    def _(pe):
        if setup:
            pe.wait_ge(k.s_const, CONSTS_LOADED)
        for t in range(T):
            pe.wait_ge(s_xh, b_xh + t + 1)
            nc.tensor.transpose(k.ps[:, t // 4, (t % 4) * P:(t % 4 + 1) * P], k.xh[:, t, :],
                                const(k, "ident")).then_inc(s_tr, 1)

    @k.block.scalar
    def _(act):
        for half in range(2):
            act.wait_ge(s_tr, b_tr + 4 * (half + 1))
            nc.scalar.activation(k.xT[:, half * 512:(half + 1) * 512], k.ps[:, half, :], ACT.Identity,
                                 scale=xT_scale, bias=xT_bias).then_inc(s_xT, 1)
    return lambda e: e.wait_ge(s_xT, b_xT + 2)


def context(k):
    nc = k.nc
    CT = B * N // P
    s_mv = statistics(k, "ctx", k.ctx, CT, lambda e, t: e.wait_ge(k.s_ctx, 16))
    s_r = k.sem("ctx_rstd")
    s_n, s_tr, s_c = k.sem("ctx_normed"), k.sem("ctx_transposed"), k.sem("ctx_T")
    s_kv, s_kve, s_bd = k.sem("ctx_kv"), k.sem("ctx_kv_out"), k.sem("ctx_spread")
    k.s_ctx_ready = s_bd

    @k.block.gpsimd
    def _(pool):
        st = k.steps(pool)
        pool.wait_ge(k.s_setup, 2)
        s_mv(pool)
        mean, var = k.mv[:, 0:CT, 0], k.mv[:, 0:CT, 1]
        pool_rsqrt(k, st, k.r1[:, 0:CT], var, EPS, CT)
        st.add(nc.gpsimd.tensor_tensor(k.r2[:, 0:CT], mean, mean, ALU.mult))
        st.wait()
        st.add(nc.gpsimd.tensor_tensor(k.r2[:, 0:CT], k.r2[:, 0:CT], var, ALU.add))
        st.wait()
        pool_rsqrt(k, st, k.r2[:, 0:CT], k.r2[:, 0:CT], 1e-6, CT)
        pool.wait_ge(k.s_const, CONSTS_LOADED)
        st.add(nc.gpsimd.tensor_scalar(k.rms1[:, :], vec(k, "rms"), 1.0, None, ALU.add))
        st.wait()
        pool.sem_inc(s_r, 1)

    @k.block.vector
    def _(dve):
        dve.wait_ge(s_r, 1)
        for t in range(CT):
            nc.vector.tensor_scalar(k.xh[:, t, :], k.ctx[:, t, :], k.mv[:, t, 0:1], k.r1[:, t:t + 1],
                                    ALU.subtract, ALU.mult).then_inc(s_n, 1)
        for t in range(CT):
            nc.vector.tensor_scalar(k.xh[:, 2 + t, :], k.ctx[:, t, :], k.r2[:, t:t + 1], None,
                                    ALU.mult).then_inc(s_n, 1)
        dve.wait_ge(k.s_const, CONSTS_LOADED)
        nc.vector.tensor_copy(k.maskf[:, :], k.mask_u8[:, :]).then_inc(s_n, 1)
        dve.wait_ge(s_n, 5)
        nc.vector.tensor_scalar(k.mask[:, :], k.maskf[:, :], 1.0, -MASKED, ALU.subtract, ALU.mult).then_inc(s_n, 1)

    @k.block.tensor
    def _(pe):
        pe.wait_ge(k.s_const, CONSTS_LOADED)
        ident = const(k, "ident")
        pe.wait_ge(k.s_ctx, 16)
        for t in range(CT):
            nc.tensor.transpose(k.ps[:, 0, t * P:(t + 1) * P], k.ctx[:, t, :], ident).then_inc(s_tr, 1)
        pe.wait_ge(s_n, 4)
        for t in range(CT):
            nc.tensor.transpose(k.ps[:, 0, (2 + t) * P:(3 + t) * P], k.xh[:, t, :], ident).then_inc(s_tr, 1)
            nc.tensor.transpose(k.ps[:, 1, t * P:(t + 1) * P], k.xh[:, 2 + t, :], ident).then_inc(s_tr, 1)
        pe.wait_ge(s_c, 7)
        nc.tensor.matmul(k.ps[:, 2, 0:B * N], k.wa0[:, 1, :], k.c0T[:, 0:B * N], start=True, stop=True).then_inc(s_kv, 1)
        for b in range(B):
            nc.tensor.matmul(k.ps[:, 3, b * P:(b + 1) * P], k.dup[:, b, :, :], k.wa0[:, 2, :],
                             start=True, stop=True).then_inc(s_kv, 1)
        nc.tensor.matmul(k.ps[:, 4, 0:B * N], k.wa0[:, 6, :], k.c3T[:, :], start=True, stop=True).then_inc(s_kv, 1)
        nc.tensor.matmul(k.ps[:, 4, B * N:2 * B * N], k.wa0[:, 7, :], k.c3T[:, :], start=True, stop=True).then_inc(s_kv, 1)
        for b in range(B):
            nc.tensor.matmul(k.ps[:, 5, b * P:(b + 1) * P], k.dup3[:, b, :, :], k.wa0[:, 8, :],
                             start=True, stop=True).then_inc(s_kv, 1)

    @k.block.scalar
    def _(act):
        act.wait_ge(k.s_const, CONSTS_LOADED)
        act.wait_ge(s_tr, 6)
        cc = lambda i: k.ps[:, i // 2, (i % 2) * 256:(i % 2) * 256 + 256]
        nc.scalar.activation(k.c0T[:, :], cc(0), ACT.Copy).then_inc(s_c, 1)
        nc.scalar.activation(k.c1T[:, :], cc(1), ACT.Identity, scale=vec(k, "gx1"), bias=vec(k, "bx1")).then_inc(s_c, 1)
        nc.scalar.activation(k.c2T[:, :], cc(1), ACT.Identity, scale=vec(k, "g1_2"), bias=vec(k, "b1_2")).then_inc(s_c, 1)
        act.wait_ge(s_r, 1)
        nc.scalar.activation(k.c3T[:, :], cc(2), ACT.Identity, scale=k.rms1[:, 0:1], bias=0.0).then_inc(s_c, 1)
        act.wait_ge(s_c, 4)
        v = lambda c: c[:, :].rearrange("p (b n) -> p b n", b=B)
        nc.scalar.activation(k.dup[:, :, 0, :], v(k.c0T), ACT.Copy).then_inc(s_c, 1)
        nc.scalar.activation(k.dup[:, :, 1, :], v(k.c0T), ACT.Copy)
        nc.scalar.activation(k.dup3[:, :, 0, :], v(k.c3T), ACT.Copy).then_inc(s_c, 1)
        nc.scalar.activation(k.dup3[:, :, 1, :], v(k.c3T), ACT.Copy).then_inc(s_c, 1)
        act.wait_ge(s_kv, 1)
        nc.scalar.activation(k.k0T[:, :], k.ps[:, 2, 0:B * N], ACT.Identity, bias=vec(k, "bk0"), scale=1.0).then_inc(s_kve, 1)
        act.wait_ge(s_kv, 11)
        nc.scalar.activation(k.v3[:, :, :], k.ps[:, 5, :].rearrange("p (b d) -> p b d", b=B), ACT.Copy).then_inc(s_kve, 1)

    @k.block.vector
    def _(dve):
        dve.wait_ge(s_kv, 5)
        nc.vector.tensor_tensor(k.v0[:, :, :], k.ps[:, 3, :].rearrange("p (b d) -> p b d", b=B),
                                rows(k, "bv0").unsqueeze(1).to_broadcast([P, B, D]), ALU.add).then_inc(s_bd, 1)
        dve.wait_ge(s_kv, 7)
        v = lambda a: a.rearrange("p (b n) -> p b n", b=B)
        bc = lambda name: const(k, name).unsqueeze(1).to_broadcast([P, B, N])
        nc.vector.tensor_tensor(v(k.k3T[:, :]), v(k.ps[:, 4, 0:256]), bc("cosk3"), ALU.mult).then_inc(s_bd, 1)
        nc.vector.tensor_tensor(v(k.k3s[:, :]), v(k.ps[:, 4, 256:512]), bc("sink3"), ALU.mult).then_inc(s_bd, 1)
        dve.wait_ge(s_bd, 3)
        nc.vector.tensor_tensor(k.k3T[:, :], k.k3T[:, :], k.k3s[:, :], ALU.add).then_inc(s_bd, 1)
        dve.wait_ge(s_bd, 4)
        dve.wait_ge(s_kve, 1)
        for b in range(B):
            nc.vector.tensor_tensor(k.kbd0[:, b, :, :], k.k0T[:, b * N:(b + 1) * N].unsqueeze(1).to_broadcast([P, H0, N]),
                                    const(k, "head0").unsqueeze(2).to_broadcast([P, H0, N]), ALU.mult).then_inc(s_bd, 1)
            nc.vector.tensor_tensor(k.kbd3[:, b, :, :], k.k3T[:, b * N:(b + 1) * N].unsqueeze(1).to_broadcast([P, H3, N]),
                                    const(k, "head3").unsqueeze(2).to_broadcast([P, H3, N]), ALU.mult).then_inc(s_bd, 1)
        dve.wait_ge(s_kve, 2)


CTX_READY = 4 + 2 * B


def attention0(k, s_xT):
    nc, cs = k.nc, k.csem
    s_q, s_qe = cs("a0_q"), cs("a0_q_out")
    s_sc, s_se = cs("a0_scores"), cs("a0_scores_out")
    s_top, s_nb, s_e = cs("a0_topk"), cs("a0_negmax"), cs("a0_exp")
    s_m, s_p, s_t, s_te = cs("a0_taken"), cs("a0_probs"), cs("a0_probsT"), cs("a0_probsT_out")
    s_pv, s_ct = cs("a0_pv"), cs("a0_ctxT")
    s_o, s_oe, s_x, s_vb, s_rd = cs("a0_out"), cs("a0_out_copied"), cs("a0_x"), cs("a0_vspread"), cs("a0_rden")
    scale = HD0 ** -0.5
    ROUNDS = TOPK // 8
    PER = 2 * ROUNDS * H0

    def loop(engine, body):
        with engine.Fori(0, B - 1) as b:
            body(b, True)
        body(B - 1, False)

    @k.block.tensor
    def _(pe):
        ps = k.ps

        def project_q(b):
            done(pe, s_qe, b)
            nc.tensor.matmul(ps[:, 0, 0:S], k.wa0[:, 0, :], k.xT[:, bass.ds(b * S, S)],
                             start=True, stop=True).then_inc(s_q, 1)

        def scores(b, tt):
            done(pe, s_qe, b + 1)
            done(pe, s_se, 2 * b + tt)
            for c in range(2):
                mm = nc.tensor.matmul(ps[:, 1 + c, :], k.qT[:, tt * P:(tt + 1) * P],
                                      k.kbd0[:, bass.ds(b, 1), 8 * c:8 * c + 8, :], start=True, stop=True)
            mm.then_inc(s_sc, 1)

        def transposes(b, tt):
            done(pe, s_p, 2 * b + tt + 1)
            done(pe, s_te, 2 * b + tt)
            for j in range(8):
                mm = nc.tensor.transpose(ps[:, 3 + j // 4, (j % 4) * P:(j % 4 + 1) * P],
                                         k.prob[:, tt, 2 * j:2 * j + 2, :], const(k, "ident"))
            mm.then_inc(s_t, 1)

        pe.wait_ge(k.s_ctx_ready, CTX_READY)
        s_xT(pe)
        project_q(0)
        scores(0, 0)

        def body(b, more):
            scores(b, 1)
            if more:
                project_q(b + 1)
            transposes(b, 0)
            if more:
                scores(b + 1, 0)
            transposes(b, 1)
            done(pe, s_te, 2 * b + 2)
            done(pe, s_vb, b + 1)
            done(pe, s_ct, b)
            for j in range(8):
                nc.tensor.matmul(ps[:, 5, 0:S], k.vbd[:, j, :], k.probT[:, j, :], start=(j == 0), stop=(j == 7))
            for j in range(8):
                mm = nc.tensor.matmul(ps[:, 5, S:2 * S], const(k, "pair0")[:, j * P:(j + 1) * P], k.probT[:, j, :],
                                      start=(j == 0), stop=(j == 7))
            mm.then_inc(s_pv, 1)
            done(pe, s_ct, b + 1)
            done(pe, s_oe, b)
            for tt in range(TB):
                nc.tensor.matmul(ps[:, 6, tt * D:(tt + 1) * D], k.ctxT[:, tt * P:(tt + 1) * P], k.wa0[:, 3, :],
                                 start=True, stop=False)
                mm = nc.tensor.matmul(ps[:, 6, tt * D:(tt + 1) * D], k.ones[0:1, 0:P], rows(k, "bo0")[0:1, :],
                                      start=False, stop=True)
            mm.then_inc(s_o, 1)

        loop(pe, body)

    @k.block.scalar
    def _(act):
        def q_out(b):
            done(act, s_q, b + 1)
            nc.scalar.activation(k.qT[:, :], k.ps[:, 0, 0:S], ACT.Identity, bias=vec(k, "bq0"), scale=1.0).then_inc(s_qe, 1)

        def probsT_out(b, tt):
            done(act, s_t, 2 * b + tt + 1)
            done(act, s_pv, b)
            nc.scalar.activation(k.probT[:, :, tt * P:(tt + 1) * P],
                                 k.ps[:, 3:5, :].rearrange("p a (j q) -> p (a j) q", q=P), ACT.Copy).then_inc(s_te, 1)

        q_out(0)
        done(act, s_sc, 1)
        nc.scalar.activation(k.sc[:, 0, :, :], k.ps[:, 1:3, :].rearrange("p a (h n) -> p (a h) n", n=N),
                             ACT.Copy).then_inc(s_se, 1)

        def body(b, more):
            done(act, s_p, 2 * b)
            exps_tile(b, 0)
            done(act, s_sc, 2 * b + 2)
            done(act, s_top, 2 * b * PER)
            copy_scores(1)
            if more:
                q_out(b + 1)
            exps_tile(b, 1)
            probsT_out(b, 0)
            if more:
                done(act, s_sc, 2 * b + 3)
                done(act, s_top, (2 * b + 1) * PER)
                copy_scores(0)
            probsT_out(b, 1)
            done(act, s_o, b + 1)
            done(act, s_x, b)
            nc.scalar.activation(k.y[:, :, :], k.ps[:, 6, 0:S].rearrange("p (t d) -> p t d", t=TB),
                                 ACT.Copy).then_inc(s_oe, 1)

        def copy_scores(tt):
            nc.scalar.activation(k.sc[:, tt, :, :], k.ps[:, 1:3, :].rearrange("p a (h n) -> p (a h) n", n=N),
                                 ACT.Copy).then_inc(s_se, 1)

        def exps_tile(b, tt):
            done(act, s_nb, 2 * b + tt + 1)
            done(act, s_se, 2 * b + tt + 1)
            if tt == 1:
                done(act, s_p, 2 * b)
            for h in range(H0):
                i = nc.scalar.activation(k.ex[:, tt, h, :], k.sc[:, tt, h, :], ACT.Exp, scale=scale,
                                         bias=k.nb[:, tt, h:h + 1])
            i.then_inc(s_e, 1)

        loop(act, body)

    @k.block.vector
    def _(dve):
        def tile(b, tt):
            base = (2 * b + tt) * PER
            done(dve, s_nb, 2 * b)
            done(dve, s_p, 2 * b)
            done(dve, s_se, 2 * b + tt + 1, k.turn_dve)
            for r in range(ROUNDS):
                src = k.sc if r == 0 else k.w
                top = k.top1[:, tt, :, :] if r == 0 else k.top[:, :, :]
                if r:
                    done(dve, s_top, base + 2 * r * H0, k.turn_dve)
                for h in range(H0):
                    nc.vector.max(top[:, h, :], src[:, tt, h, :]).then_inc(s_top, 1)
                done(dve, s_top, base + (2 * r + 1) * H0, k.turn_dve)
                for h in range(H0):
                    nc.vector.match_replace(k.w[:, tt, h, :], top[:, h, :], src[:, tt, h, :],
                                            imm_value=NEG).then_inc(s_top, 1)

        def finish(b):
            done(dve, s_pv, b + 1)
            nc.vector.reciprocal(k.rden[:, :], k.ps[:, 5, S:2 * S]).then_inc(s_rd, 1)
            done(dve, s_rd, b + 1)
            done(dve, s_o, b)
            nc.vector.tensor_tensor(k.ctxT[:, :], k.ps[:, 5, 0:S], k.rden[:, :], ALU.mult).then_inc(s_ct, 1)

        tile(0, 0)
        tile(0, 1)
        with dve.Fori(1, B) as b:
            tile(b, 0)
            finish(b - 1)
            tile(b, 1)
        finish(B - 1)
        done(dve, s_x, B)

    @k.block.gpsimd
    def _(pool):
        with pool.Fori(0, B) as b:
            done(pool, s_pv, b)
            nc.gpsimd.tensor_tensor(k.vbd[:, :, :], k.v0[:, bass.ds(b, 1), :].to_broadcast([P, 8, D]),
                                    const(k, "pair0").rearrange("p (j d) -> p j d", j=8), ALU.mult).then_inc(s_vb, 1)
            for tt in range(TB):
                done(pool, s_top, (2 * b + tt) * PER + H0, k.turn_pool)
                nc.gpsimd.tensor_scalar(k.nb[:, tt, :], k.top1[:, tt, :, 0], -scale, None, ALU.mult).then_inc(s_nb, 1)
                done(pool, s_t, 2 * b)
                done(pool, s_top, (2 * b + tt + 1) * PER, k.turn_pool)
                nc.gpsimd.tensor_scalar(k.w[:, tt, :, :], k.w[:, tt, :, :], NEG / 2, None, ALU.is_lt).then_inc(s_m, 1)
                done(pool, s_m, 2 * b + tt + 1)
                done(pool, s_e, 2 * b + tt + 1)
                nc.gpsimd.tensor_tensor(k.prob[:, tt, :, :], k.w[:, tt, :, :], k.ex[:, tt, :, :], ALU.mult).then_inc(s_p, 1)
            done(pool, s_oe, b + 1)
            xb = k.X[:, bass.ds(b * TB, TB), :]
            nc.gpsimd.tensor_tensor(xb, xb, k.y[:, :, :], ALU.add).then_inc(s_x, 1)
    return lambda e, t=0: done(e, s_x, B)


def router(k, layer, s_xT):
    nc = k.nc
    (s_l, b_l), (s_e, b_e) = k.shared("router_logits", 1), k.shared("router_exp", 1)
    (s_sub, b_sub), (s_c, b_c) = k.shared("router_shifted", 1), k.shared("router_comb", 1)
    bias = {0: "rb0", 1: "br1"}.get(layer)

    @k.block.tensor
    def _(pe):
        s_xT(pe)
        for t in range(T):
            mm = nc.tensor.matmul(k.ps[:, 7, t * E:(t + 1) * E], k.xT[:, t * P:(t + 1) * P], k.wr[:, layer, :],
                                  start=True, stop=True)
        mm.then_inc(s_l, 1)

    @k.block.scalar
    def _(act):
        act.wait_ge(s_sub, b_sub + 1)
        nc.scalar.activation(k.pr[:, :, :], k.pr[:, :, :], ACT.Exp).then_inc(s_e, 1)

    @k.block.vector
    def _(dve):
        st = k.steps(dve)
        v = nc.vector
        dve.wait_ge(s_l, b_l + 1)
        logits_ps = k.ps[:, 7, 0:T * E].rearrange("p (t e) -> p t e", e=E)
        if bias:
            st.add(v.tensor_tensor(k.lg[:, :, :], logits_ps, rows(k, bias).unsqueeze(1).to_broadcast([P, T, E]), ALU.add))
        else:
            st.add(v.tensor_copy(k.lg[:, :, :], logits_ps))
        st.wait()
        for t in range(T):
            st.add(v.max(k.mx[:, t, :], k.lg[:, t, :]))
        st.wait()
        v.tensor_tensor(k.pr[:, :, :], k.lg[:, :, :], k.mx[:, :, 0:1].to_broadcast([P, T, E]), ALU.subtract).then_inc(s_sub, 1)
        for t in range(T):
            st.add(v.max_index(k.ix[:, t, :], k.mx[:, t, :], k.lg[:, t, :]))
        st.wait()
        st.add(v.tensor_copy(k.ixf[:, :, :], k.ix[:, :, 0:2]))
        st.wait()
        iota = const(k, "iota8").unsqueeze(1).to_broadcast([P, T, E])
        hit = lambda out, n: st.add(v.tensor_tensor(out, iota, k.ixf[:, :, n:n + 1].to_broadcast([P, T, E]), ALU.is_equal))
        hit(k.comb[:, :, :], 0)
        hit(k.oh[:, :, :], 1)
        st.wait()
        if layer in (0, 2):
            st.add(v.tensor_tensor(k.comb[:, :, :], k.comb[:, :, :], k.oh[:, :, :], ALU.add))
            st.wait()
        dve.wait_ge(s_e, b_e + 1)
        if layer in (0, 3):
            st.add(v.tensor_reduce(k.sm[:, :], k.pr[:, :, :], AX, ALU.add))
        if layer != 1:
            st.add(v.tensor_tensor(k.comb[:, :, :], k.comb[:, :, :], k.pr[:, :, :], ALU.mult))
            st.wait()
            if layer == 2:
                st.add(v.tensor_reduce(k.sm[:, :], k.comb[:, :, :], AX, ALU.add))
                st.wait()
            st.add(v.reciprocal(k.sm[:, :], k.sm[:, :]))
            st.wait()
            if layer == 3:
                st.add(v.tensor_scalar(k.sm[:, :], k.sm[:, :], 2.0, None, ALU.mult))
                st.wait()
            st.add(v.tensor_tensor(k.comb[:, :, :], k.comb[:, :, :], k.sm[:, :].unsqueeze(2).to_broadcast([P, T, E]), ALU.mult))
            st.wait()
        if layer == 3:
            st.add(v.memset(k.comb[:, :, E - 1], 1.0))
            st.wait()
        dve.sem_inc(s_c, 1)
        if layer == 2:
            for t in range(T):
                st.add(v.tensor_scalar(k.xh[:, t, :], k.X[:, t, :], k.mv[:, t, 0:1], k.r1[:, t:t + 1],
                                       ALU.subtract, ALU.mult))
            st.wait()
            st.add(v.tensor_tensor(k.X[:, :, :], k.X[:, :, :], k.xh[:, :, :], ALU.add))
            st.wait()
    return lambda e: e.wait_ge(s_sub, b_sub + 1), lambda e: e.wait_ge(s_c, b_c + 1)


HALF = T // 2


def down_product(k, pe, w, h, half, s_dn):
    for tt in range(HALF):
        for f in range(FC):
            mm = k.nc.tensor.matmul(k.ps[:, 4 + half, tt * P:(tt + 1) * P], h[:, half, f, tt * P:(tt + 1) * P],
                                    w(f), start=(f == 0), stop=(f == FC - 1))
    mm.then_inc(s_dn, 1)


def accumulate(k, dve, s_dn, s_acc, u, half, e):
    done(dve, s_dn, u + 1)
    done(dve, s_acc, HALF * (u - 1))
    for tt in range(HALF):
        t = HALF * half + tt
        k.nc.vector.scalar_tensor_tensor(k.X[:, t, :], k.ps[:, 4 + half, tt * P:(tt + 1) * P],
                                         k.comb[:, t, bass.ds(e, 1)], k.X[:, t, :], ALU.mult, ALU.add).then_inc(s_acc, 1)


def summed(s_acc):
    n = 2 * E * HALF
    return lambda e, t=T - 1: done(e, s_acc, n - HALF if t < HALF else n - T + t + 1)


def expert_biases(k, bias, comb_ready, s_acc):
    nc = k.nc
    (s_t, b_t), (s_te, b_te) = k.shared("bias_combT", 2), k.shared("bias_combT_out", 2)
    (s_b, b_b), (s_x, b_x) = k.shared("bias_product", 2), k.shared("bias_x", 2)

    @k.block.tensor
    def _(pe):
        comb_ready(pe)
        for half in range(2):
            for tt in range(HALF):
                mm = nc.tensor.transpose(k.ps[0:E, 6 + half, tt * P:(tt + 1) * P], k.comb[:, HALF * half + tt, :],
                                         const(k, "ident"))
            mm.then_inc(s_t, 1)
        for half in range(2):
            pe.wait_ge(s_te, b_te + half + 1)
            for tt in range(HALF):
                t = HALF * half + tt
                mm = nc.tensor.matmul(k.ps[:, half, tt * P:(tt + 1) * P], k.combT[:, t * P:(t + 1) * P],
                                      bias, start=True, stop=True)
            mm.then_inc(s_b, 1)

    @k.block.scalar
    def _(act):
        for half in range(2):
            act.wait_ge(s_t, b_t + half + 1)
            nc.scalar.activation(k.combT[:, half * 512:(half + 1) * 512], k.ps[0:E, 6 + half, :], ACT.Copy).then_inc(s_te, 1)

    @k.block.vector
    def _(dve):
        summed(s_acc)(dve)
        for half in range(2):
            dve.wait_ge(s_b, b_b + half + 1)
            x = k.X[:, HALF * half:HALF * (half + 1), :]
            nc.vector.tensor_tensor(x, x, k.ps[:, half, :].rearrange("p (t d) -> p t d", d=D), ALU.add).then_inc(s_x, 1)
    return lambda e, t=T - 1: e.wait_ge(s_x, b_x + t // HALF + 1)


def load_experts(k, weights, before, s_w, s_dn):
    n = weights.shape[2]

    @k.block.sync
    def _(sp):
        give(k, sp)
        before(sp)
        for j in range(2):
            sp.dma_start(k.wf[:, j, 0:n], weights[j, :, :]).then_inc(s_w[j], 16)
        with sp.Fori(1, E // 2) as i:
            for j in range(2):
                done(sp, s_dn, 4 * i + 2 * j - 2)
                sp.dma_start(k.wf[:, j, 0:n], weights[bass.ds(2 * i + j, 1), :, :].rearrange("e p n -> (e p) n"))\
                    .then_inc(s_w[j], 16)


def give(k, sp):
    for s in k.credited:
        sp.sem_inc(s, CREDIT)
    k.credited.clear()


def ffn(k, layer, s_xT, before, func, bias1):
    nc = k.nc
    tag = f"f{layer}"
    s_up, s_h, s_acc = k.csem(f"{tag}_up"), k.csem(f"{tag}_h"), k.csem(f"{tag}_acc")
    s_w, s_dn = [k.sem(f"{tag}_w0"), k.sem(f"{tag}_w1")], k.csem(f"{tag}_down")
    _, comb_ready = router(k, layer, s_xT)

    @k.block.tensor
    def _(pe):
        with pe.Fori(0, E // 2) as i:
            def up(j, half):
                u = 4 * i + 2 * j + half
                if half == 0:
                    pe.wait_ge(s_w[j], 16 * i + 16)
                for f in range(FC):
                    done(pe, s_h, 4 * u + f - 3)
                    nc.tensor.matmul(k.ps[:, f, :], k.wf[:, j, f * P:(f + 1) * P], k.xT[:, half * 512:(half + 1) * 512],
                                     start=True, stop=True).then_inc(s_up, 1)

            def down(j, half):
                u = 4 * i + 2 * j + half
                done(pe, s_acc, HALF * (u - 1))
                done(pe, s_h, 4 * u + FC)
                down_product(k, pe, lambda f: k.wf[:, j, F + f * P:F + (f + 1) * P], k.h, half, s_dn)
            up(0, 0)
            up(0, 1)
            down(0, 0)
            up(1, 0)
            down(0, 1)
            up(1, 1)
            down(1, 0)
            down(1, 1)

    @k.block.scalar
    def _(act):
        with act.Fori(0, E // 2) as i:
            for ju in range(4):
                for f in range(FC):
                    done(act, s_up, 16 * i + 4 * ju + f + 1, k.turn_act if bias1 else None)
                    b = k.vecs[:, bass.ds(VEC[bias1][0] + (2 * i + ju // 2) * FC + f, 1)] if bias1 else 0.0
                    nc.scalar.activation(k.h[:, ju % 2, f, :], k.ps[:, f, :], func, bias=b, scale=1.0).then_inc(s_h, 1)

    @k.block.vector
    def _(dve):
        with dve.Fori(0, E // 2) as i:
            for ju in range(4):
                accumulate(k, dve, s_dn, s_acc, 4 * i + ju, ju % 2, 2 * i + ju // 2)
    load_experts(k, k.d[f"wf{layer}"], before, s_w, s_dn)
    return expert_biases(k, k.bias2[:, 0:D], comb_ready, s_acc) if layer == 1 else summed(s_acc)


def attention12(k, layer, s_xT):
    nc, cs = k.nc, lambda n: k.csem(f"a{layer}_{n}")
    NP = 4 if layer == 1 else 8
    NH, KEYS, W = 2 * NP, S + N, NP * P
    scale = 64 ** -0.5
    w, cT = (k.wa1, k.c1T) if layer == 1 else (k.wa2, k.c2T)
    wq, wk, wv = (lambda j, a=a: w[:, a + j * P:a + (j + 1) * P] for a in (0, W, 2 * W))
    wo_at = 3 * W if layer == 2 else 4 * W
    s_wa = k.s_wa[layer]
    s_in = cs("inputs")
    s_pa, s_pae, s_pd, s_pde = cs("proj_act"), cs("proj_act_out"), cs("proj_dve"), cs("proj_dve_out")
    s_s, s_mx, s_e, s_rc, s_pn = cs("scores"), cs("negmax"), cs("exp"), cs("recip"), cs("probs")
    s_t, s_ta, s_tb = cs("probsT"), cs("probsT_a"), cs("probsT_b")
    s_pv, s_ot, s_o, s_x, s_rot = cs("pv"), cs("oT"), cs("out"), cs("x"), cs("rope")
    act_jobs = [("q", g, 0) for g in range(NP // 2)] + [("v", c, g) for c in range(3) for g in range(NP // 4)]
    dve_jobs = [("k", j, 0) for j in range(NP)] + ([("swap", 0, 0)] if layer == 1 else [])
    NA, ND = len(act_jobs), len(dve_jobs)
    NROPE = 1

    @k.block.gpsimd
    def _(pool):
        s_xT(pool)
        with pool.Fori(0, B) as b:
            done(pool, s_pd, ND * b)
            done(pool, s_pa, NA * b, k.turn_pool)
            nc.gpsimd.tensor_copy(k.at[:, 0:S], k.xT[:, bass.ds(b * S, S)]).then_inc(s_in, 1)
            nc.gpsimd.tensor_copy(k.at[:, S:KEYS], cT[:, bass.ds(b * N, N)]).then_inc(s_in, 1)

    @k.block.tensor
    def _(pe):
        pe.wait_ge(s_wa, 16)
        with pe.Fori(0, B) as b:
            done(pe, s_in, 2 * b + 2)

            def act_job(n):
                kind, x, g = act_jobs[n]
                done(pe, s_pae, NA * b + n)
                if kind == "q":
                    for jj in range(2):
                        mm = nc.tensor.matmul(k.ps[:, 0, jj * S:(jj + 1) * S], wq(2 * x + jj), k.at[:, 0:S],
                                              start=True, stop=True)
                else:
                    rows_ = P if x < 2 else N
                    mm = nc.tensor.matmul(k.ps[0:rows_, 0, :], k.at[:, x * P:x * P + rows_],
                                          w[:, 2 * W + g * 512:2 * W + (g + 1) * 512], start=True, stop=True)
                mm.then_inc(s_pa, 1)

            def dve_job(n):
                kind, j, _ = dve_jobs[n]
                done(pe, s_pde, ND * b + n)
                if kind == "k":
                    mm = nc.tensor.matmul(k.ps[:, 1, 0:KEYS], wk(j), k.at[:, :], start=True, stop=True)
                else:
                    for j in range(NP):
                        mm = nc.tensor.matmul(k.ps[:, 1, j * N:(j + 1) * N], w[:, 3 * W + j * P:3 * W + (j + 1) * P],
                                              k.at[:, S:KEYS], start=True, stop=True)
                mm.then_inc(s_pd, 1)
            for n in range(max(NA, ND)):
                if n < ND:
                    dve_job(n)
                if n < NA:
                    act_job(n)

            def scores(j):
                for m in range(4):
                    qt, hh = m // 2, m % 2
                    done(pe, s_e, 4 * (NP * b + j) + m - 3)
                    mm = nc.tensor.matmul(k.ps[:, m, 0:KEYS], k.aq[64 * hh:64 * hh + 64, j, qt * P:(qt + 1) * P],
                                          k.ak[64 * hh:64 * hh + 64, j, :], start=True, stop=(layer == 1))
                    if layer == 1:
                        mm.then_inc(s_s, 1)
                if layer == 2:
                    for m in range(4):
                        nc.tensor.matmul(k.ps[:, m, S:KEYS], k.ones[0:1, 0:P], k.mask[0:1, bass.ds(b * N, N)],
                                         start=False, stop=True).then_inc(s_s, 1)

            def transposes(j):
                done(pe, s_ta, 2 * (NP * b + j))
                done(pe, s_tb, NP * b + j)
                if j == 0:
                    done(pe, s_x, b)
                for m in range(4):
                    qt, hh = m // 2, m % 2
                    done(pe, s_pn, 4 * (NP * b + j) + m + 1)
                    prob = k.ap[:, 4 * (j % 2) + m, :]
                    for c in range(2):
                        nc.tensor.transpose(k.ps[:, 4 + hh, c * S + qt * P:c * S + (qt + 1) * P],
                                            prob[:, c * P:(c + 1) * P], const(k, "ident"))
                    mm = nc.tensor.transpose(k.ps[0:N, 6, hh * S + qt * P:hh * S + (qt + 1) * P], prob[:, S:KEYS],
                                             const(k, "ident"))
                mm.then_inc(s_t, 1)

            def pv(j):
                done(pe, s_ta, 2 * (NP * b + j) + 2)
                done(pe, s_tb, NP * b + j + 1)
                done(pe, s_ot, NP * b + j)
                for c in range(3):
                    rows_ = P if c < 2 else N
                    for hh in range(2):
                        h = 2 * j + hh
                        mm = nc.tensor.matmul(k.ps[64 * hh:64 * hh + 64, 7, 0:S], k.av[0:rows_, c, h * 64:(h + 1) * 64],
                                              k.apt[0:rows_, j % 2, hh, c, :], start=(c == 0), stop=(c == 2))
                mm.then_inc(s_pv, 1)

            done(pe, s_pae, NA * b + NA)
            done(pe, s_pde, ND * b + ND)
            if layer == 1:
                done(pe, s_rot, b + 1)
            scores(0)
            for j in range(NP):
                if j + 1 < NP:
                    scores(j + 1)
                transposes(j)
                if j:
                    pv(j - 1)
            pv(NP - 1)
            done(pe, s_ot, NP * (b + 1))
            for qt in range(TB):
                for j in range(NP):
                    mm = nc.tensor.matmul(k.ps[:, 4, qt * D:(qt + 1) * D], k.aot[:, j, qt * P:(qt + 1) * P],
                                          w[:, wo_at + j * D:wo_at + (j + 1) * D], start=(j == 0), stop=(j == NP - 1))
            mm.then_inc(s_o, 1)

    @k.block.scalar
    def _(act):
        with act.Fori(0, B) as b:
            for n, (kind, x, g) in enumerate(act_jobs):
                done(act, s_pa, NA * b + n + 1)
                if kind == "q":
                    nc.scalar.activation(k.aq[:, 2 * x:2 * x + 2, :], k.ps[:, 0, :].rearrange("p (j q) -> p j q", j=2),
                                         ACT.Copy, scale=scale).then_inc(s_pae, 1)
                else:
                    rows_ = P if x < 2 else N
                    nc.scalar.activation(k.av[0:rows_, x, g * 512:(g + 1) * 512], k.ps[0:rows_, 0, :],
                                         ACT.Copy).then_inc(s_pae, 1)

            def exps(j):
                done(act, s_t, NP * b + j - 1)
                for m in range(4):
                    slot = 4 * (j % 2) + m
                    done(act, s_mx, 4 * (NP * b + j) + m + 1)
                    nc.scalar.activation(k.ap[:, slot, :], k.ps[:, m, 0:KEYS], ACT.Exp, bias=k.anm[:, slot:slot + 1],
                                         scale=1.0, accum_out=k.asm[:, slot:slot + 1]).then_inc(s_e, 1)

            def oT(j):
                done(act, s_pv, NP * b + j + 1)
                nc.scalar.activation(k.aot[:, j, :], k.ps[:, 7, 0:S], ACT.Copy).then_inc(s_ot, 1)

            exps(0)
            for j in range(NP):
                if j + 1 < NP:
                    exps(j + 1)
                done(act, s_t, NP * b + j + 1)
                for hh in range(2):
                    nc.scalar.activation(k.apt[:, j % 2, hh, 0:2, :], k.ps[:, 4 + hh, :].rearrange("p (c q) -> p c q", c=2),
                                         ACT.Copy).then_inc(s_ta, 1)
                if j:
                    oT(j - 1)
            oT(NP - 1)

    @k.block.vector
    def _(dve):
        v = nc.vector
        with dve.Fori(0, B) as b:
            for n, (kind, j, _) in enumerate(dve_jobs):
                done(dve, s_pd, ND * b + n + 1)
                if kind == "swap":
                    bc = lambda name: const(k, name).unsqueeze(1).to_broadcast([P, NP, N])
                    v.tensor_tensor(k.arot[:, :, :], k.ps[:, 1, 0:NP * N].rearrange("p (j n) -> p j n", n=N), bc("sin1"),
                                    ALU.mult).then_inc(s_pde, 1)
                    done(dve, s_pde, ND * b + n + 1)
                    kc = k.ak[:, 0:NP, S:KEYS]
                    v.tensor_tensor(kc, kc, k.arot[:, :, :], ALU.add).then_inc(s_rot, 1)
                elif layer == 1:
                    v.tensor_copy(k.ak[:, j, 0:S], k.ps[:, 1, 0:S])
                    v.tensor_tensor(k.ak[:, j, S:KEYS], k.ps[:, 1, S:KEYS], const(k, "cos1"), ALU.mult).then_inc(s_pde, 1)
                else:
                    v.tensor_copy(k.ak[:, j, :], k.ps[:, 1, 0:KEYS]).then_inc(s_pde, 1)

            def maxes(j):
                for m in range(4):
                    slot = 4 * (j % 2) + m
                    done(dve, s_s, 4 * (NP * b + j) + m + 1)
                    v.tensor_reduce(k.anm[:, slot:slot + 1], k.ps[:, m, 0:KEYS], AX, ALU.max, negate=True)\
                        .then_inc(s_mx, 1)

            def normal(j):
                sums = k.asm[:, 4 * (j % 2):4 * (j % 2) + 4]
                done(dve, s_e, 4 * (NP * b + j) + 4)
                v.reciprocal(sums, sums).then_inc(s_rc, 1)
                done(dve, s_rc, NP * b + j + 1)
                for m in range(4):
                    slot = 4 * (j % 2) + m
                    v.tensor_scalar(k.ap[:, slot, :], k.ap[:, slot, :], k.asm[:, slot:slot + 1], None,
                                    ALU.mult).then_inc(s_pn, 1)

            maxes(0)
            normal(0)
            for j in range(NP):
                if j + 1 < NP:
                    maxes(j + 1)
                done(dve, s_t, NP * b + j + 1)
                v.tensor_copy(k.apt[0:N, j % 2, :, 2, :], k.ps[0:N, 6, :].rearrange("p (h q) -> p h q", h=2)).then_inc(s_tb, 1)
                if j + 1 < NP:
                    normal(j + 1)
            done(dve, s_o, b + 1)
            x = k.X[:, bass.ds(b * TB, TB), :]
            v.tensor_tensor(x, x, k.ps[:, 4, 0:S].rearrange("p (t d) -> p t d", d=D), ALU.add).then_inc(s_x, 1)
        done(dve, s_x, B)
    give_credits(k)
    return lambda e, t=0: done(e, s_x, B)


def attention3(k, s_xT):
    nc, cs = k.nc, lambda n: k.csem(f"a3_{n}")
    s_q, s_rs, s_rot = cs("q"), cs("rope_steps"), cs("rope")
    s_s, s_mx, s_sh, s_e, s_sm, s_p = cs("scores"), cs("negmax"), cs("shifted"), cs("exp"), cs("sums"), cs("probs")
    s_t, s_te, s_vb, s_pv, s_c, s_o, s_x = (cs(n) for n in ("probsT", "probsT_out", "vspread", "pv", "ctxT", "out", "x"))
    NB = B
    tiled = lambda a: a.rearrange("p (h n) -> p h n", n=N)

    @k.block.tensor
    def _(pe):
        s_xT(pe)
        with pe.Fori(0, NB) as b:
            done(pe, s_rot, b)
            for n in range(2):
                mm = nc.tensor.matmul(k.ps[:, 0, n * S:(n + 1) * S], k.wa0[:, 4 + n, :], k.xT[:, bass.ds(b * S, S)],
                                      start=True, stop=True)
            mm.then_inc(s_q, 1)
            done(pe, s_rot, b + 1)
            for tt in range(TB):
                done(pe, s_sh, 2 * b + tt - 1)
                nc.tensor.matmul(k.ps[:, 1 + tt, 0:H3 * N], k.q3[:, tt * P:(tt + 1) * P],
                                 k.kbd3[:, bass.ds(b, 1), :, :], start=True, stop=False)
                for h in range(H3):
                    mm = nc.tensor.matmul(k.ps[:, 1 + tt, h * N:(h + 1) * N], k.ones[0:1, 0:P],
                                          k.mask[0:1, bass.ds(b * N, N)], start=False, stop=(h == H3 - 1))
                mm.then_inc(s_s, 1)
            for tt in range(TB):
                done(pe, s_p, 2 * b + tt + 1)
                done(pe, s_te, 2 * b + tt)
                for j in range(2):
                    mm = nc.tensor.transpose(k.ps[:, 3, j * P:(j + 1) * P], k.p3[:, tt, 2 * j:2 * j + 2, :],
                                             const(k, "ident"))
                mm.then_inc(s_t, 1)
            done(pe, s_te, 2 * b + 2)
            done(pe, s_vb, b + 1)
            for j in range(2):
                mm = nc.tensor.matmul(k.ps[:, 4, 0:S], k.vbd3[:, j, :], k.p3T[:, j, :], start=(j == 0), stop=(j == 1))
            mm.then_inc(s_pv, 1)
            done(pe, s_c, b + 1)
            done(pe, s_x, b)
            for tt in range(TB):
                mm = nc.tensor.matmul(k.ps[:, 5, tt * D:(tt + 1) * D], k.ctxT[:, tt * P:(tt + 1) * P], k.wa0[:, 9, :],
                                      start=True, stop=True)
            mm.then_inc(s_o, 1)

    @k.block.scalar
    def _(act):
        with act.Fori(0, NB) as b:
            for tt in range(TB):
                done(act, s_sh, 2 * b + tt + 1)
                nc.scalar.activation(k.p3[:, tt, :, :], k.p3[:, tt, :, :], ACT.Exp).then_inc(s_e, 1)
            for tt in range(TB):
                done(act, s_t, 2 * b + tt + 1)
                nc.scalar.activation(k.p3T[:, :, tt * P:(tt + 1) * P], k.ps[:, 3, 0:2 * P].rearrange("p (j q) -> p j q", j=2),
                                     ACT.Copy).then_inc(s_te, 1)
            done(act, s_pv, b + 1)
            nc.scalar.activation(k.ctxT[:, :], k.ps[:, 4, 0:S], ACT.Copy).then_inc(s_c, 1)

    @k.block.vector
    def _(dve):
        v = nc.vector
        with dve.Fori(0, NB) as b:
            done(dve, s_q, b + 1)
            v.scalar_tensor_tensor(k.q3[:, :], k.ps[:, 0, 0:S], HD3 ** -0.5, const(k, "cosq3"), ALU.mult, ALU.mult)\
                .then_inc(s_rs, 1)
            v.scalar_tensor_tensor(k.q3s[:, :], k.ps[:, 0, S:2 * S], HD3 ** -0.5, const(k, "sinq3"), ALU.mult, ALU.mult)\
                .then_inc(s_rs, 1)
            done(dve, s_rs, 2 * b + 2)
            v.tensor_tensor(k.q3[:, :], k.q3[:, :], k.q3s[:, :], ALU.add).then_inc(s_rot, 1)
            for tt in range(TB):
                done(dve, s_s, 2 * b + tt + 1)
                v.tensor_reduce(k.m3[:, tt, :], tiled(k.ps[:, 1 + tt, 0:H3 * N]), AX, ALU.max).then_inc(s_mx, 1)
                done(dve, s_mx, 2 * b + tt + 1)
                v.tensor_tensor(k.p3[:, tt, :, :], tiled(k.ps[:, 1 + tt, 0:H3 * N]),
                                k.m3[:, tt, :].unsqueeze(2).to_broadcast([P, H3, N]), ALU.subtract).then_inc(s_sh, 1)
            for tt in range(TB):
                done(dve, s_e, 2 * b + tt + 1)
                v.tensor_reduce(k.m3[:, tt, :], k.p3[:, tt, :, :], AX, ALU.add).then_inc(s_sm, 1)
                done(dve, s_sm, 4 * b + 2 * tt + 1)
                v.reciprocal(k.m3[:, tt, :], k.m3[:, tt, :]).then_inc(s_sm, 1)
                done(dve, s_sm, 4 * b + 2 * tt + 2)
                v.tensor_tensor(k.p3[:, tt, :, :], k.p3[:, tt, :, :],
                                k.m3[:, tt, :].unsqueeze(2).to_broadcast([P, H3, N]), ALU.mult).then_inc(s_p, 1)
            done(dve, s_o, b + 1)
            x = k.X[:, bass.ds(b * TB, TB), :]
            v.tensor_tensor(x, x, k.ps[:, 5, 0:S].rearrange("p (t d) -> p t d", d=D), ALU.add).then_inc(s_x, 1)
        done(dve, s_x, B)

    @k.block.gpsimd
    def _(pool):
        s_xT(pool)
        with pool.Fori(0, NB) as b:
            done(pool, s_pv, b)
            nc.gpsimd.tensor_tensor(k.vbd3[:, :, :], k.v3[:, bass.ds(b, 1), :].to_broadcast([P, 2, D]),
                                    const(k, "pair3").rearrange("p (j d) -> p j d", j=2), ALU.mult).then_inc(s_vb, 1)
    give_credits(k)
    return lambda e, t=0: done(e, s_x, B)


def ffn2(k, s_xT, before):
    nc, cs = k.nc, lambda n: k.csem(f"f2_{n}")
    GROUPS = 2
    s_w, s_dn = [k.sem("f2_w0"), k.sem("f2_w1")], cs("down")
    s_up, s_h, s_acc = cs("products"), cs("h"), cs("acc")
    s_z, s_za, s_st, s_mv, s_r, s_rp, s_zn = (cs(n) for n in ("z", "z_out", "z_stats", "z_moments", "z_rstd", "z_rstd_steps", "z_normed"))
    s_sw = {n: k.sem(f"f2_spec_{n}_loaded") for n in ("0", "1a", "1b", "2")}
    at = {"0": (0, 2048), "1a": (2048, 3072), "1b": (3072, 4096), "2": (4096, 6144)}
    spec = {n: k.ws2[:, a:b] for n, (a, b) in at.items()}
    logits_read, comb_ready = router(k, 2, s_xT)

    order = ["U00", "U01", "Z00", "Z01", "U10", "R00", "D00", "U11", "R01", "D01", "A10", "A11", "Z10", "Z11",
             "U20", "R10", "D10", "U21", "R11", "D11", "S20", "S21", "U30", "D20", "U31", "D21", "D30", "D31"]
    jobs = [(o[0], int(o[1]), int(o[2])) for o in order]
    banks = {"U": 4, "R": 4, "A": 2, "S": 4}
    index, last, before_bank, n = {}, {}, {}, 0
    for job in jobs:
        if job[0] in banks:
            for f in range(banks[job[0]]):
                index[job + (f,)] = n
                before_bank[job + (f,)] = last.get(f)
                last[f] = n
                n += 1
    PER = n
    for key, v in before_bank.items():
        if v is None:
            before_bank[key] = last[key[3]] - PER
    downs = [j for j in jobs if j[0] == "D"]
    zs = [j for j in jobs if j[0] == "Z"]

    @k.block.tensor
    def _(pe):
        pe_ = nc.tensor
        logits_read(pe)
        with pe.Fori(0, GROUPS) as i:
            for job in jobs:
                kind, e, half = job
                cols = slice(half * 512, (half + 1) * 512)
                wf = lambda a, c: k.wf[:, e % 2, a + c * P:a + (c + 1) * P]

                def product(f, lhs, rhs, chunks):
                    done(pe, s_h, PER * i + before_bank[job + (f,)] + 1)
                    for c in range(chunks):
                        mm = pe_.matmul(k.ps[:, f, :], lhs(c), rhs(c), start=(c == 0), stop=(c == chunks - 1))
                    mm.then_inc(s_up, 1)

                if kind == "U":
                    if half == 0:
                        pe.wait_ge(s_w[e % 2], 32 * i + 16 * (e // 2 + 1))
                    for f in range(FC):
                        product(f, lambda c: wf(0, f), lambda c: k.xT[:, cols], 1)
                elif kind in "AS":
                    name = "1a" if kind == "A" else "2"
                    width = 256 if kind == "A" else F
                    src = index[("U", e, half, FC - 1)]
                    pe.wait_ge(s_sw[name], 16 * i + 16)
                    done(pe, s_h, PER * i + src + 1)
                    for f in range(banks[kind]):
                        product(f, lambda c: spec[name][:, c * width + f * P:c * width + (f + 1) * P],
                                lambda c: k.h[:, half, c, :], FC)
                elif kind == "Z":
                    name, chunks, h = ("0", FC, k.h) if e == 0 else ("1b", 2, k.t1)
                    src = index[("U", e, half, FC - 1) if e == 0 else ("A", e, half, 1)]
                    pe.wait_ge(s_sw[name], 16 * i + 16)
                    done(pe, s_h, PER * i + src + 1)
                    for tt in range(4):
                        n = 16 * i + 4 * zs.index(job) + tt
                        done(pe, s_za, n - 1)
                        for c in range(chunks):
                            mm = pe_.matmul(k.ps[:, 6 + tt % 2, :], h[:, half, c, tt * P:(tt + 1) * P],
                                            spec[name][:, c * F:(c + 1) * F], start=(c == 0), stop=(c == chunks - 1))
                        mm.then_inc(s_z, 1)
                elif kind == "R":
                    z = zs.index(("Z", e, half))
                    done(pe, s_zn, 16 * i + 4 * z + 4)
                    for f in range(FC):
                        done(pe, s_h, PER * i + before_bank[job + (f,)] + 1)
                        for tt in range(4):
                            mm = pe_.transpose(k.ps[:, f, tt * P:(tt + 1) * P], k.z[:, half, tt, f * P:(f + 1) * P],
                                               const(k, "ident"))
                        mm.then_inc(s_up, 1)
                else:
                    d = downs.index(job)
                    src = index[({0: "R", 1: "R", 2: "S", 3: "U"}[e], e, half, FC - 1)]
                    h = k.h if e == 3 else k.h2
                    done(pe, s_acc, HALF * (8 * i + d - 1))
                    done(pe, s_h, PER * i + src + 1)
                    down_product(k, pe, lambda f: wf(F, f), h, half, s_dn)

    @k.block.scalar
    def _(act):
        a = nc.scalar.activation
        with act.Fori(0, GROUPS) as i:
            for job in jobs:
                kind, e, half = job
                if kind not in banks:
                    continue
                v = lambda name, per, f: k.vecs[:, bass.ds(VEC[name][0] + per * i + f, 1)]
                for f in range(banks[kind]):
                    done(act, s_up, PER * i + index[job + (f,)] + 1, k.turn_act)
                    src = k.ps[:, f, :]
                    if kind == "U":
                        m = a(k.h[:, half, f, :], src, ACT.Gelu, bias=v("up_b", 4 * FC, e * FC + f), scale=1.0)
                    elif kind == "A":
                        m = a(k.t1[:, half, f, :], src, ACT.Gelu, bias=v("s1a_b", 2, f), scale=1.0)
                    elif kind == "S":
                        m = a(k.h2[:, half, f, :], src, ACT.Gelu, bias=v("s2_b", FC, f), scale=1.0)
                    elif e == 0:
                        m = a(k.h2[:, half, f, :], src, ACT.Gelu, bias=v("ln0_b", FC, f), scale=v("ln0_g", FC, f))
                    else:
                        m = a(k.h2[:, half, f, :], src, ACT.Identity, bias=v("ln1_b", FC, f), scale=v("ln1_g", FC, f))
                    m.then_inc(s_h, 1)

    @k.block.vector
    def _(dve):
        v = nc.vector
        with dve.Fori(0, GROUPS) as i:
            def stats(job):
                z = zs.index(job)
                _, e, half = job
                name = "s0_b" if e == 0 else "s1b_b"
                for tt in range(4):
                    n = 16 * i + 4 * z + tt
                    done(dve, s_z, n + 1)
                    v.tensor_tensor(k.z[:, half, tt, :], k.ps[:, 6 + tt % 2, :],
                                    k.rowv[:, bass.ds(ROW[name][0] + F * i, F)], ALU.add).then_inc(s_za, 1)
                for tt in range(4):
                    n = 16 * i + 4 * z + tt
                    done(dve, s_za, n + 1)
                    v.bn_stats(k.stat[:, tt, :], k.z[:, half, tt, :]).then_inc(s_st, 1)
                done(dve, s_st, 16 * i + 4 * z + 4, k.turn_dve)
                for tt in range(4):
                    v.bn_aggr(k.mv[:, 4 * half + tt, :], k.stat[:, tt, :]).then_inc(s_mv, 1)

            def norm(job):
                z = zs.index(job)
                half = job[2]
                done(dve, s_r, 4 * i + z + 1)
                for tt in range(4):
                    t = 4 * half + tt
                    v.tensor_scalar(k.z[:, half, tt, :], k.z[:, half, tt, :], k.mv[:, t, 0:1], k.r1[:, t:t + 1],
                                    ALU.subtract, ALU.mult).then_inc(s_zn, 1)

            for e in range(4):
                if e < 2:
                    for half in range(2):
                        stats(("Z", e, half))
                    for half in range(2):
                        norm(("Z", e, half))
                for half in range(2):
                    accumulate(k, dve, s_dn, s_acc, 8 * i + 2 * e + half, half, 4 * i + e)

    @k.block.gpsimd
    def _(pool):
        with pool.Fori(0, GROUPS) as i:
            for z, (_, e, half) in enumerate(zs):
                r = k.r1[:, 4 * half:4 * half + 4]
                done(pool, s_mv, 16 * i + 4 * z + 4, k.turn_pool)
                nc.gpsimd.tensor_scalar(r, k.mv[:, 4 * half:4 * half + 4, 1], EPS, None, ALU.add).then_inc(s_rp, 1)
                done(pool, s_rp, 4 * i + z + 1)
                nc.gpsimd.tensor_tensor(r, r, k.mhalf[:, 0:4], ALU.pow).then_inc(s_r, 1)


    @k.block.sync
    def _(sp):
        give(k, sp)
        wf = k.d["wf2"]
        for n, (a, b) in at.items():
            sp.dma_start(k.ws2[:, a:b], k.d["ws2"][0, :, a:b]).then_inc(s_sw[n], 16)
        before(sp)
        for j in range(2):
            sp.dma_start(k.wf[:, j, 0:2 * F], wf[j, :, :]).then_inc(s_w[j], 16)
        for e in range(2, E):
            done(sp, s_dn, 2 * e - 2)
            sp.dma_start(k.wf[:, e % 2, 0:2 * F], wf[e, :, :]).then_inc(s_w[e % 2], 16)
            if e in (2, 3, 4):
                for n in {2: ("0",), 3: ("1a", "1b"), 4: ("2",)}[e]:
                    a, b = at[n]
                    sp.dma_start(k.ws2[:, a:b], k.d["ws2"][1, :, a:b]).then_inc(s_sw[n], 16)
    return expert_biases(k, k.bias2[:, D:2 * D], comb_ready, s_acc)


def ffn3(k, s_xT, before):
    nc, cs = k.nc, lambda n: k.csem(f"f3_{n}")
    s_w, s_dn = [k.sem("f3_w0"), k.sem("f3_w1")], cs("down")
    s_up, s_g, s_h, s_acc = cs("up"), cs("gate"), cs("h"), cs("acc")
    router(k, 3, s_xT)

    @k.block.tensor
    def _(pe):
        with pe.Fori(0, E // 2) as i:
            def up(j, half):
                u = 4 * i + 2 * j + half
                if half == 0:
                    pe.wait_ge(s_w[j], 16 * i + 16)
                for f in range(FC):
                    done(pe, s_h, 4 * u + f - 1)
                    for g in (1, 0):
                        mm = nc.tensor.matmul(k.ps[:, 2 * (f % 2) + g, :], k.wf[:, j, g * F + f * P:g * F + (f + 1) * P],
                                              k.xT[:, half * 512:(half + 1) * 512], start=True, stop=True)
                    mm.then_inc(s_up, 1)

            def down(j, half):
                u = 4 * i + 2 * j + half
                done(pe, s_acc, HALF * (u - 1))
                done(pe, s_h, 4 * u + FC)
                down_product(k, pe, lambda f: k.wf[:, j, 2 * F + f * P:2 * F + (f + 1) * P], k.h, half, s_dn)
            up(0, 0)
            up(0, 1)
            down(0, 0)
            up(1, 0)
            down(0, 1)
            up(1, 1)
            down(1, 0)
            down(1, 1)

    @k.block.scalar
    def _(act):
        with act.Fori(0, E // 2) as i:
            for ju in range(4):
                for f in range(FC):
                    n = 16 * i + 4 * ju + f
                    done(act, s_up, n + 1)
                    done(act, s_h, n - 1)
                    nc.scalar.activation(k.gate[:, f % 2, :], k.ps[:, 2 * (f % 2) + 1, :], ACT.Silu).then_inc(s_g, 1)

    @k.block.vector
    def _(dve):
        with dve.Fori(0, E // 2) as i:
            def hidden(ju):
                for f in range(FC):
                    n = 16 * i + 4 * ju + f
                    done(dve, s_g, n + 1)
                    nc.vector.tensor_tensor(k.h[:, ju % 2, f, :], k.ps[:, 2 * (f % 2), :], k.gate[:, f % 2, :],
                                            ALU.mult).then_inc(s_h, 1)

            def add(ju):
                accumulate(k, dve, s_dn, s_acc, 4 * i + ju, ju % 2, 2 * i + ju // 2)
            hidden(0)
            hidden(1)
            add(0)
            hidden(2)
            add(1)
            hidden(3)
            add(2)
            add(3)
    load_experts(k, k.d["wf3"], before, s_w, s_dn)
    return summed(s_acc)


def program(nc, d):
    with ExitStack() as ctx:
        k = State()
        k.nc, k.d, k.credited = nc, d, []
        sb = lambda name, shape, dt=F32: ctx.enter_context(nc.sbuf_tensor(name, shape, dt))
        k.sem = lambda name: ctx.enter_context(nc.semaphore(name))

        def csem(name):
            s = k.sem(name)
            k.credited.append(s)
            return s
        k.csem = csem
        shared = {}

        def shared_sem(name, total):
            if name not in shared:
                shared[name] = [k.sem(name), 0]
            sem, base = shared[name]
            shared[name][1] += total
            return sem, base
        k.shared = shared_sem
        own = {}

        def steps(engine):
            key = "pool" if "GpSimd" in type(engine).__name__ or "Pool" in type(engine).__name__ else "dve"
            if key not in own:
                own[key] = Steps(k.sem(f"{key}_steps"))
            own[key].engine = engine
            return own[key]
        k.steps = steps

        k.ps = ctx.enter_context(nc.psum_tensor("ps", [P, 8, 512], F32))
        k.X = sb("x_res", [P, T, D])
        k.xh = sb("xhat", [P, T, D])
        k.xT = sb("xT", [P, T * P])
        k.ctx = sb("ctx_sb", [P, 2, D])
        k.consts = sb("consts_sb", [P, NCONST])
        k.vecs = sb("vecs_sb", [P, NVEC])
        k.rowv = sb("rows_sb", [P, NROW])
        k.bias2 = sb("bias2_sb", [E, 2 * D])
        k.wr = sb("wr_sb", [P, 4, E])
        k.wa0 = sb("wa0_sb", [P, 10, P])
        k.mask_u8 = sb("mask_u8", [1, B * N], U8)
        k.maskf = sb("maskf", [1, B * N])
        k.mask = sb("mask_sb", [1, B * N])
        k.mhalf = sb("mhalf", [P, 8])
        k.ones = sb("ones", [1, 512])
        k.stat = sb("stat", [P, T, 6])
        k.mv = sb("mv", [P, T, 2])
        k.r1 = sb("r1", [P, T])
        k.r2 = sb("r2", [P, T])
        k.rms1 = sb("rms1", [P, 1])
        k.c1T, k.c2T, k.c3T, k.k3T = (sb(n, [P, B * N]) for n in ("c1T", "c2T", "c3T", "k3T"))
        k.v3 = sb("v3", [P, B, D])
        k.kbd3 = sb("kbd3", [P, B, H3, N])
        k.y = sb("y", [P, TB, D])
        k.ctxT = sb("ctxT", [P, S])
        k.qT = sb("qT", [P, S])

        k.wa2 = sb("wa_sb", [P, 32 * P])
        k.wa1 = k.wa2[:, 0:20 * P]
        k.ws2 = sb("ws2_sb", [P, 12 * F])
        k.wf = sb("wf_sb", [P, 2, 3 * F])
        k.lg, k.pr, k.comb, k.oh, k.mx = (sb(n, [P, T, E]) for n in ("r_lg", "r_pr", "r_comb", "r_oh", "r_mx"))
        k.ix = sb("r_ix", [P, T, 8], U32)
        k.ixf = sb("r_ixf", [P, T, 2])
        k.sm = sb("r_sm", [P, T])

        with ExitStack() as c0:
            s0 = lambda name, shape, dt=F32: c0.enter_context(nc.sbuf_tensor(name, shape, dt))
            k.sc = s0("a0_sc", [P, TB, H0, N])
            k.w = s0("a0_w", [P, TB, H0, N])
            k.ex = s0("a0_ex", [P, TB, H0, N])
            k.prob = s0("a0_prob", [P, TB, H0, N])
            k.probT = s0("a0_probT", [P, 8, S])
            k.vbd = s0("a0_vbd", [P, 8, D])
            k.top1 = s0("a0_top1", [P, TB, H0, 8])
            k.top = s0("a0_top", [P, H0, 8])
            k.nb = s0("a0_nb", [P, TB, H0])
            k.rden = s0("a0_rden", [P, S])
            k.dup3 = s0("dup3", [P, B, 2, N])
            k.c0T, k.k0T, k.k3s = (s0(n, [P, B * N]) for n in ("c0T", "k0T", "k3s"))
            k.dup = s0("dup", [P, B, 2, N])
            k.v0 = s0("v0", [P, B, D])
            k.kbd0 = s0("kbd0", [P, B, H0, N])
        with ExitStack() as c1:
            s1 = lambda name, shape, dt=F32: c1.enter_context(nc.sbuf_tensor(name, shape, dt))
            k.h = s1("f_h", [P, 2, FC, 512])
            k.combT = s1("f_combT", [E, T * P])
            k.h2 = s1("f2_h2", [P, 2, FC, 512])
            k.t1 = s1("f2_t1", [P, 2, 2, 512])
            k.z = s1("f2_z", [P, 2, 4, F])
            k.gate = k.z[:, 0, :, :]
        with ExitStack() as c2:
            s2 = lambda name, shape, dt=F32: c2.enter_context(nc.sbuf_tensor(name, shape, dt))
            k.q3 = s2("a3_q", [P, S])
            k.q3s = s2("a3_qs", [P, S])
            k.p3 = s2("a3_p", [P, TB, H3, N])
            k.p3T = s2("a3_pT", [P, 2, S])
            k.vbd3 = s2("a3_vbd", [P, 2, D])
            k.m3 = s2("a3_m", [P, TB, H3])
            k.at = s2("a_in", [P, S + N])
            k.aq = s2("a_q", [P, 8, S])
            k.ak = s2("a_k", [P, 8, S + N])
            k.av = s2("a_v", [P, 3, 8 * P])
            k.ap = s2("a_probs", [P, 8, S + N])
            k.apt = s2("a_probsT", [P, 2, 2, 3, S])
            k.aot = s2("a_oT", [P, 8, S])
            k.arot = s2("a_rot", [P, 4, N])
            k.anm = s2("a_negmax", [P, 8])
            k.asm = s2("a_sums", [P, 8])
        k.block = ctx.enter_context(nc.Block())
        s_out = k.sem("out_stored")
        load_constants(k)
        context(k)
        s_xT = normalize(k, "n0", lambda e, t: e.wait_ge(k.s_x, 16))
        ready = attention0(k, s_xT)
        give_credits(k)
        s_xT = normalize(k, "n1", ready)
        ready = ready_ff = ffn(k, 0, s_xT, lambda e: None, ACT.Gelu, None)
        s_xT = normalize(k, "n2", ready, second=EPS, xT_scale=vec(k, "gl1"), xT_bias=vec(k, "bl1"))
        ready = attention12(k, 1, s_xT)
        @k.block.sync
        def _(sp, ready=ready):
            ready(sp)
            sp.dma_start(k.wa2[:, :], d["wa2"]).then_inc(k.s_wa[2], 16)
        s_xT = normalize(k, "n3", ready)
        ready = ready_ff = ffn(k, 1, s_xT, ready_ff, ACT.Relu, "b1_1")
        s_xT = normalize(k, "n4", ready, second=EPS, xT_scale=vec(k, "g2_2"), xT_bias=vec(k, "b2_2"))
        ready = attention12(k, 2, s_xT)
        s_xT = normalize(k, "n5", ready, second=EPS, xT_scale=vec(k, "ln_g"), xT_bias=vec(k, "ln_b"))
        ready = ready_ff = ffn2(k, s_xT, ready_ff)
        s_xT = normalize(k, "n6", ready, second=1e-6, xT_scale=k.rms1[:, 0:1])
        ready = attention3(k, s_xT)
        s_xT = normalize(k, "n7", ready)
        ready = ffn3(k, s_xT, ready_ff)
        give_credits(k)

        @k.block.sync
        def _(sp):
            ready(sp)
            sp.dma_start(d["out"].rearrange("(t p) d -> p t d", p=P), k.X[:, :, :]).then_inc(s_out, 16)
            sp.wait_ge(s_out, 16)


def constants():
    p = np.arange(P)
    c = np.zeros((P, NCONST), np.float32)

    def put(name, a):
        c[:, CONST[name][0]:CONST[name][1]] = a
    put("ident", np.eye(P))
    col = np.arange(D)
    put("pair0", np.concatenate([(col[None] // HD0 == 2 * j + p[:, None] // N) for j in range(8)], 1))
    put("pair3", np.concatenate([(col[None] // HD3 == 2 * j + p[:, None] // N) for j in range(2)], 1))
    put("head0", p[:, None] // HD0 == np.arange(H0)[None])
    put("head3", p[:, None] // HD3 == np.arange(H3)[None])
    put("iota8", np.arange(E)[None])

    def rope(dim, freq, pos):
        half = dim // 2
        ang = (pos[None, :].astype(np.float32) * freq[(p % dim) % half][:, None]).astype(np.float32)
        sign = np.where(p % dim < half, -1.0, 1.0)[:, None]
        return np.cos(ang), np.sin(ang) * sign
    f1 = (1.0 / 10000.0 ** (np.arange(0, 64, 2, dtype=np.float32) / 64)).astype(np.float32)
    a, b = rope(64, f1, np.arange(N))
    put("cos1", a), put("sin1", b)
    f3 = (1.0 / 10000.0 ** (np.float32(2.0 / 32) * np.arange(16, dtype=np.float32))).astype(np.float32)
    a, b = rope(32, f3, np.arange(N, N + S))
    put("cosq3", a), put("sinq3", b)
    a, b = rope(32, f3, np.arange(N))
    put("cosk3", a), put("sink3", b)
    return c


def swap_halves(w, dim):
    a = w.reshape(w.shape[0], -1, 2, dim // 2)
    return np.ascontiguousarray(a[:, :, ::-1]).reshape(w.shape)


def layout(i):
    g = {n: np.asarray(a) for n, a in i.items()}
    c = constants()
    col = lambda a: a.reshape(-1, P).T
    vecs = {"bq0": g["L0_xattn_bq"], "bk0": g["L0_xattn_bk"], "gx1": g["L1_xattn_gamma_x"], "bx1": g["L1_xattn_beta_x"],
            "gl1": g["L1_xattn_gamma_l"], "bl1": g["L1_xattn_beta_l"], "b1_1": g["L1_ffn_b1"],
            "g1_2": g["L2_xattn_g1"], "b1_2": g["L2_xattn_b1"], "g2_2": g["L2_xattn_g2"], "b2_2": g["L2_xattn_b2"],
            "ln_g": g["L2_ffn_ln_g"], "ln_b": g["L2_ffn_ln_b"], "up_b": g["L2_ffn_up_b"],
            "ln0_g": g["L2_ffn_ln0_g"], "ln0_b": g["L2_ffn_ln0_b"], "s1a_b": g["L2_ffn_spec1a_b"],
            "ln1_g": g["L2_ffn_ln1_g"], "ln1_b": g["L2_ffn_ln1_b"], "s2_b": g["L2_ffn_spec2_b"],
            "rms": g["L3_xattn_rms_scale"]}
    rows_ = {"bv0": g["L0_xattn_bv"], "bo0": g["L0_xattn_bo"], "rb0": g["L0_ffn_router_b"], "br1": g["L1_ffn_br"],
             "s0_b": g["L2_ffn_spec0_b"], "s1b_b": g["L2_ffn_spec1b_b"]}
    kv = g["L3_xattn_kv_w"][:, 0]
    q3 = g["L3_xattn_q_w"].transpose(1, 0, 2).reshape(D, D)
    k3, v3 = np.tile(kv[0], (1, H3)), np.tile(kv[1], (1, H3))
    wa0 = np.stack([g["L0_xattn_Wq"].T, g["L0_xattn_Wk"].T, g["L0_xattn_Wv"].T, g["L0_xattn_Wo"].T,
                    q3, swap_halves(q3, HD3), k3, swap_halves(k3, HD3), v3, g["L3_xattn_out_w"].reshape(D, D)], 1)
    wr = np.stack([g["L0_ffn_router_w"], g["L1_ffn_Wr"].T, g["L2_ffn_router_w"], g["L3_ffn_Wr"]], 1)
    a = {"x": g["x"].reshape(B * S, D), "ctx": g["ctx_1024"].reshape(B * N, D),
         "mask": g["mask_BxS2_bk0"].reshape(1, B * N), "consts": c,
         "bias2": np.concatenate([g["L1_ffn_b2"], g["L2_ffn_down_b"]], 1),
         "vecs": np.concatenate([col(vecs[n]) for n in VEC], 1), "rows": np.concatenate([rows_[n].reshape(-1) for n in ROW]),
         "wa0": wa0, "wr": wr}
    up = lambda w: w
    down = lambda w: w.reshape(-1, w.shape[1] // P, P, w.shape[2]).transpose(0, 2, 1, 3).reshape(w.shape[0], P, -1)
    a["wf0"] = np.concatenate([up(g["L0_ffn_expert_up"].transpose(0, 2, 1)), down(g["L0_ffn_expert_down"].transpose(0, 2, 1))], 2)
    a["wf1"] = np.concatenate([up(g["L1_ffn_W1"].transpose(0, 2, 1)), down(g["L1_ffn_W2"].transpose(0, 2, 1))], 2)
    rows_of = lambda w: w.reshape(-1, P, w.shape[1]).transpose(1, 0, 2).reshape(P, -1)
    wkv1 = g["L1_xattn_Wkv"]
    a["wa1"] = np.concatenate([g["L1_xattn_Wq"], wkv1, swap_halves(wkv1[:, :512], 64), rows_of(g["L1_xattn_Wo"])], 1)
    a["wa2"] = np.concatenate([g["L2_xattn_Wq"], g["L2_xattn_Wkv"], rows_of(g["L2_xattn_Wout"])], 1)
    a["wf2"] = np.concatenate([g["L2_ffn_up_W"], down(g["L2_ffn_down_W"])], 2)
    a["ws2"] = np.concatenate([down(g["L2_ffn_spec0_W"]), down(g["L2_ffn_spec1a_W"]), down(g["L2_ffn_spec1b_W"]),
                               down(g["L2_ffn_spec2_W"])], 2)
    cat = lambda w, s: np.concatenate([w, s[None]], 0)
    a["wf3"] = np.concatenate([cat(g["L3_ffn_Wu"], g["L3_ffn_Wu_s"]), cat(g["L3_ffn_Wg"], g["L3_ffn_Wg_s"]),
                               down(cat(g["L3_ffn_Wd"], g["L3_ffn_Wd_s"]))], 2)
    return {n: np.ascontiguousarray(v) for n, v in a.items()}


def kernel(**inputs):
    import concourse.bacc as _bacc
    from concourse.bass_utils import run_bass_kernel_spmd as _run

    nc = _bacc.Bacc("TRN2", target_bir_lowering=False, num_devices=1)
    a = layout(inputs)
    arrays, d = {}, {}
    for n, v in a.items():
        arrays[f"{n}_dram"] = v
        d[n] = nc.dram_tensor(f"{n}_dram", v.shape, mybir.dt.from_np(v.dtype), kind="ExternalInput").ap()
    d["out"] = nc.dram_tensor("out_dram", (B * S, D), F32, kind="ExternalOutput").ap()
    program(nc, d)
    r = _run(nc, [arrays], core_ids=[0])
    return r.results[0]["out_dram"].reshape(B, S, D)
```

```python
from contextlib import ExitStack

import numpy as np

import concourse.bass as bass
from concourse import mybir

F32 = mybir.dt.float32
F32R = mybir.dt.float32r
BF16 = mybir.dt.bfloat16
U32 = mybir.dt.uint32
U8 = mybir.dt.uint8
ALU = mybir.AluOpType
ACT = mybir.ActivationFunctionType
AX = mybir.AxisListType.X

P = 128
B, S, N, D = 4, 256, 64, 128
T = B * S // P
TB = S // P
HALF = T // 2
E, F = 8, 512
FC = F // P
H0, HD0 = 16, 8
H3, HD3 = 4, 32
TOPK = 32
EPS = 1e-5
NEG = -3.0e38
MASKED = -2.0 ** 100

CONST = {}
_at = 0
for _name, _n in (("ident", P), ("pair0", 8 * P), ("head0", H0), ("pair3", 2 * P), ("head3", H3), ("iota8", E),
                  ("cos1", N), ("sin1", N), ("cosq3", S), ("sinq3", S), ("cosk3", N), ("sink3", N)):
    CONST[_name] = (_at, _at + _n)
    _at += _n
NCONST = _at

VEC = {}
_at = 0
for _name, _n in (("bq0", 1), ("bk0", 1), ("gx1", 1), ("bx1", 1), ("gl1", 1), ("bl1", 1), ("b1_1", E * FC),
                  ("g1_2", 1), ("b1_2", 1), ("g2_2", 1), ("b2_2", 1), ("ln_g", 1), ("ln_b", 1), ("up_b", E * FC),
                  ("ln0_g", 2 * FC), ("ln0_b", 2 * FC), ("s1a_b", 4), ("ln1_g", 2 * FC),
                  ("ln1_b", 2 * FC), ("s2_b", 2 * FC), ("rms", 1)):
    VEC[_name] = (_at, _at + _n)
    _at += _n
NVEC = _at

ROW = {}
_at = 0
for _name, _n in (("bv0", D), ("bo0", D), ("rb0", E), ("br1", E), ("s0_b", 2 * F), ("s1b_b", 2 * F)):
    ROW[_name] = (_at, _at + _n)
    _at += _n
NROW = _at
NROW_FIRST = ROW["s0_b"][0]


CREDIT = 4


def done(engine, sem, count, turn=None):
    engine.wait_ge(sem, count + CREDIT)
    if turn is not None:
        engine.sem_inc(turn, 1)


class State:
    pass


class Steps:

    def __init__(self, sem):
        self.engine, self.sem, self.n = None, sem, 0

    def add(self, instruction):
        instruction.then_inc(self.sem, 1)
        self.n += 1

    def wait(self):
        self.engine.wait_ge(self.sem, self.n)


def const(k, name):
    a, b = CONST[name]
    return k.consts[:, a:b]


def vec(k, name, i=0, n=1):
    a = VEC[name][0] + i
    return k.vecs[:, a:a + n]


def rows(k, name, i=0, n=None):
    a, b = ROW[name]
    return k.rowv[:, a + i:(b if n is None else a + i + n)]


def load_constants(k):
    d, sem = k.d, k.sem
    k.s_x, k.s_ctx, k.s_const = sem("x_loaded"), sem("ctx_loaded"), sem("constants_loaded")
    k.s_setup, k.s_rows, k.s_first = sem("memsets_done"), sem("layer2_rows_loaded"), sem("first_rstd")
    k.s_wa = {1: sem("wa1_loaded"), 2: sem("wa2_loaded")}
    k.turn_dve, k.turn_pool, k.turn_act = sem("dve_turns"), sem("pool_turns"), sem("act_turns")

    @k.block.sync
    def _(sp):
        sp.dma_start(k.X[:, :, :], d["x"].rearrange("(t p) d -> p t d", p=P)).then_inc(k.s_x, 16)
        sp.dma_start(k.ctx[:, :, :], d["ctx"].rearrange("(t p) d -> p t d", p=P)).then_inc(k.s_ctx, 16)
        sp.wait_ge(k.s_const, CONSTS_LOADED)
        sp.dma_start(k.wa1, d["wa1"]).then_inc(k.s_wa[1], 16)
        sp.dma_start(k.rowv[:, NROW_FIRST:NROW], d["rows"][NROW_FIRST:NROW].partition_broadcast(P)).then_inc(k.s_rows, 16)

    @k.block.scalar
    def _(act):
        act.dma_start(k.consts[:, :], d["consts"]).then_inc(k.s_const, 16)
        act.dma_start(k.vecs[:, :], d["vecs"]).then_inc(k.s_const, 16)
        act.dma_start(k.wa0[:, :, :], d["wa0"]).then_inc(k.s_const, 16)
        act.dma_start(k.rowv[:, 0:NROW_FIRST], d["rows"][0:NROW_FIRST].partition_broadcast(P)).then_inc(k.s_const, 16)
        act.dma_start(k.bias2[:, :], d["bias2"]).then_inc(k.s_const, 16)
        act.dma_start(k.wr[:, :, :], d["wr"]).then_inc(k.s_const, 16)
        act.dma_start(k.mask_u8[:, :], d["mask"]).then_inc(k.s_const, 16)

    @k.block.gpsimd
    def _(pool):
        pool.memset(k.mhalf[:, :], -0.5).then_inc(k.s_setup, 1)
        pool.memset(k.ones[:, :], 1.0).then_inc(k.s_setup, 1)
        pool.memset(k.ones16[:, :], 1.0).then_inc(k.s_setup, 1)


def load_table(k, func):
    k.nc.scalar.activation(k.columns[:, k.column:k.column + 1], const(k, "ident")[:, 0:1], func)
    k.column += 1


def give_credits(k):
    @k.block.sync
    def _(sp):
        give(k, sp)


CONSTS_LOADED = 7 * 16


def statistics(k, x, tiles, ready, group):
    s_stat, b_stat = k.shared("norm_stats", tiles)
    s_mv, b_mv = k.shared("norm_moments", tiles)

    @k.block.vector
    def _(dve):
        for g in range(0, tiles, group):
            for t in range(g, g + group):
                ready(dve, t)
                dve.bn_stats(k.stat[:, t, :], x[:, t, :]).then_inc(s_stat, 1)
            for t in range(g, g + group):
                dve.wait_ge(s_stat, b_stat + t + 1)
                dve.bn_aggr(k.mv[:, t, :], k.stat[:, t, :]).then_inc(s_mv, 1)
    return lambda e, g=tiles // group - 1: e.wait_ge(s_mv, b_mv + (g + 1) * group)


def pool_rsqrt(k, st, out, in_, scale, eps, n):
    st.add(k.nc.gpsimd.tensor_scalar(out, in_, scale, eps, ALU.mult, ALU.add))
    st.wait()
    st.add(k.nc.gpsimd.tensor_tensor(out, out, k.mhalf[:, 0:n], ALU.pow))
    st.wait()


def normalize(k, ready, second=None, xT_scale=1.0, xT_bias=0.0, keep_first=False, setup=False):
    nc = k.nc
    s_mv = statistics(k, k.X, T, ready, HALF)
    (s_r, b_r), (s_xh, b_xh) = k.shared("norm_rstd", 2), k.shared("norm_xhat", T)
    (s_tr, b_tr), (s_xT, b_xT) = k.shared("norm_transposed", T), k.shared("norm_xT", 2 * TB)

    @k.block.gpsimd
    def _(pool):
        st = k.steps(pool)
        pool.wait_ge(k.s_setup, 3)
        for half in range(2):
            a, b = HALF * half, HALF * (half + 1)
            s_mv(pool, half)
            if second is None:
                pool_rsqrt(k, st, k.r2[:, a:b], k.mv[:, a:b, 1], 1.0, EPS, HALF)
            else:
                pool_rsqrt(k, st, k.r2[:, a:b], k.mv[:, a:b, 1], 1.0 + second, second * EPS, HALF)
            pool.sem_inc(s_r, 1)
        if keep_first:
            pool_rsqrt(k, st, k.r1[:, :], k.mv[:, 0:T, 1], 1.0, EPS, T)
            pool.sem_inc(k.s_first, 1)

    @k.block.vector
    def _(dve):
        for half in range(2):
            dve.wait_ge(s_r, b_r + half + 1)
            for t in range(HALF * half, HALF * (half + 1)):
                nc.vector.tensor_scalar(k.xh[:, t, :], k.X[:, t, :], k.mv[:, t, 0:1], k.r2[:, t:t + 1],
                                        ALU.subtract, ALU.mult).then_inc(s_xh, 1)

    @k.block.tensor
    def _(pe):
        if setup:
            pe.wait_ge(k.s_const, CONSTS_LOADED)
        for t in range(T):
            pe.wait_ge(s_xh, b_xh + t + 1)
            nc.tensor.transpose(k.ps[:, t // 4, (t % 4) * P:(t % 4 + 1) * P], k.xh[:, t, :],
                                const(k, "ident")).then_inc(s_tr, 1)

    @k.block.scalar
    def _(act):
        for half in range(2):
            act.wait_ge(s_tr, b_tr + 4 * (half + 1))
            nc.scalar.activation(k.xT[:, half * 512:(half + 1) * 512], k.ps[:, half, :], ACT.Identity,
                                 scale=xT_scale, bias=xT_bias).then_inc(s_xT, TB)
    return lambda e, batch=2 * TB - 1: e.wait_ge(s_xT, b_xT + batch + 1)


def context(k):
    nc = k.nc
    CT = B * N // P
    s_mv = statistics(k, k.ctx, CT, lambda e, t: e.wait_ge(k.s_ctx, 16), CT)
    s_r = k.sem("ctx_rstd")
    s_n, s_tr, s_c = k.sem("ctx_normed"), k.sem("ctx_transposed"), k.sem("ctx_T")
    s_kv, s_kve, s_bd = k.sem("ctx_kv"), k.sem("ctx_kv_out"), k.sem("ctx_spread")
    k.s_ctx_ready, k.s_k0T = s_bd, s_kve

    @k.block.gpsimd
    def _(pool):
        st = k.steps(pool)
        pool.wait_ge(k.s_setup, 3)
        s_mv(pool)
        mean, var = k.mv[:, 0:CT, 0], k.mv[:, 0:CT, 1]
        pool_rsqrt(k, st, k.r1[:, 0:CT], var, 1.0, EPS, CT)
        st.add(nc.gpsimd.tensor_tensor(k.r2[:, 0:CT], mean, mean, ALU.mult))
        st.wait()
        st.add(nc.gpsimd.tensor_tensor(k.r2[:, 0:CT], k.r2[:, 0:CT], var, ALU.add))
        st.wait()
        pool_rsqrt(k, st, k.r2[:, 0:CT], k.r2[:, 0:CT], 1.0, 1e-6, CT)
        pool.wait_ge(k.s_const, CONSTS_LOADED)
        st.add(nc.gpsimd.tensor_scalar(k.rms1[:, :], vec(k, "rms"), 1.0, None, ALU.add))
        st.wait()
        pool.sem_inc(s_r, 1)

    @k.block.vector
    def _(dve):
        dve.wait_ge(s_r, 1)
        for t in range(CT):
            nc.vector.tensor_scalar(k.xh[:, t, :], k.ctx[:, t, :], k.mv[:, t, 0:1], k.r1[:, t:t + 1],
                                    ALU.subtract, ALU.mult).then_inc(s_n, 1)
        for t in range(CT):
            nc.vector.tensor_scalar(k.xh[:, 2 + t, :], k.ctx[:, t, :], k.r2[:, t:t + 1], None,
                                    ALU.mult).then_inc(s_n, 1)
        dve.wait_ge(k.s_const, CONSTS_LOADED)
        nc.vector.tensor_copy(k.maskf[:, :], k.mask_u8[:, :]).then_inc(s_n, 1)
        dve.wait_ge(s_n, 5)
        nc.vector.tensor_scalar(k.mask16[:, :], k.maskf[:, :], 1.0, -MASKED, ALU.subtract, ALU.mult).then_inc(s_n, 1)

    @k.block.tensor
    def _(pe):
        pe.wait_ge(k.s_const, CONSTS_LOADED)
        ident = const(k, "ident")
        pe.wait_ge(k.s_ctx, 16)
        for t in range(CT):
            nc.tensor.transpose(k.ps[:, 0, t * P:(t + 1) * P], k.ctx[:, t, :], ident).then_inc(s_tr, 1)
        pe.wait_ge(s_n, 4)
        for t in range(CT):
            nc.tensor.transpose(k.ps[:, 0, (2 + t) * P:(3 + t) * P], k.xh[:, t, :], ident).then_inc(s_tr, 1)
            nc.tensor.transpose(k.ps[:, 1, t * P:(t + 1) * P], k.xh[:, 2 + t, :], ident).then_inc(s_tr, 1)
        pe.wait_ge(s_c, 7)
        nc.tensor.matmul(k.ps[:, 2, 0:B * N], k.wa0[:, 1, :], k.c0T[:, 0:B * N], start=True, stop=True).then_inc(s_kv, 1)
        for b in range(B):
            nc.tensor.matmul(k.ps[:, 3, b * P:(b + 1) * P], k.dup[:, b, :, :], k.wa0[:, 2, :],
                             start=True, stop=True).then_inc(s_kv, 1)
        nc.tensor.matmul(k.ps[:, 4, 0:B * N], k.wa0[:, 6, :], k.c3T[:, :], start=True, stop=True).then_inc(s_kv, 1)
        nc.tensor.matmul(k.ps[:, 4, B * N:2 * B * N], k.wa0[:, 7, :], k.c3T[:, :], start=True, stop=True).then_inc(s_kv, 1)
        for b in range(B):
            nc.tensor.matmul(k.ps[:, 5, b * P:(b + 1) * P], k.dup3[:, b, :, :], k.wa0[:, 8, :],
                             start=True, stop=True).then_inc(s_kv, 1)

    @k.block.scalar
    def _(act):
        act.wait_ge(k.s_setup, 1)
        nc.scalar.activation(k.columns[:, 15:16], k.mhalf[:, 0:1], ACT.Identity)
        act.wait_ge(k.s_const, CONSTS_LOADED)
        act.wait_ge(s_tr, 6)
        cc = lambda i: k.ps[:, i // 2, (i % 2) * 256:(i % 2) * 256 + 256]
        nc.scalar.activation(k.c0T[:, :], cc(0), ACT.Copy).then_inc(s_c, 1)
        nc.scalar.activation(k.c1T[:, :], cc(1), ACT.Identity, scale=vec(k, "gx1"), bias=vec(k, "bx1")).then_inc(s_c, 1)
        nc.scalar.activation(k.c2T[:, :], cc(1), ACT.Identity, scale=vec(k, "g1_2"), bias=vec(k, "b1_2")).then_inc(s_c, 1)
        act.wait_ge(s_r, 1)
        nc.scalar.activation(k.c3T[:, :], cc(2), ACT.Identity, scale=k.rms1[:, 0:1], bias=0.0).then_inc(s_c, 1)
        act.wait_ge(s_c, 4)
        v = lambda c: c[:, :].rearrange("p (b n) -> p b n", b=B)
        nc.scalar.activation(k.dup[:, :, 0, :], v(k.c0T), ACT.Copy).then_inc(s_c, 1)
        nc.scalar.activation(k.dup[:, :, 1, :], v(k.c0T), ACT.Copy)
        nc.scalar.activation(k.dup3[:, :, 0, :], v(k.c3T), ACT.Copy).then_inc(s_c, 1)
        nc.scalar.activation(k.dup3[:, :, 1, :], v(k.c3T), ACT.Copy).then_inc(s_c, 1)
        act.wait_ge(s_kv, 1)
        nc.scalar.activation(k.k0T[:, :], k.ps[:, 2, 0:B * N], ACT.Identity, bias=vec(k, "bk0"), scale=1.0).then_inc(s_kve, 1)
        act.wait_ge(s_kv, 11)
        nc.scalar.activation(k.v3[:, :, :], k.ps[:, 5, :].rearrange("p (b d) -> p b d", b=B), ACT.Copy).then_inc(s_kve, 1)

    @k.block.vector
    def _(dve):
        dve.wait_ge(s_kv, 5)
        nc.vector.tensor_tensor(k.v0[:, :, :], k.ps[:, 3, :].rearrange("p (b d) -> p b d", b=B),
                                rows(k, "bv0").unsqueeze(1).to_broadcast([P, B, D]), ALU.add).then_inc(s_bd, 1)
        dve.wait_ge(s_kv, 7)
        v = lambda a: a.rearrange("p (b n) -> p b n", b=B)
        bc = lambda name: const(k, name).unsqueeze(1).to_broadcast([P, B, N])
        nc.vector.tensor_tensor(v(k.k3T[:, :]), v(k.ps[:, 4, 0:256]), bc("cosk3"), ALU.mult).then_inc(s_bd, 1)
        nc.vector.tensor_tensor(v(k.k3s[:, :]), v(k.ps[:, 4, 256:512]), bc("sink3"), ALU.mult).then_inc(s_bd, 1)
        dve.wait_ge(s_bd, 3)
        nc.vector.tensor_tensor(k.k3T[:, :], k.k3T[:, :], k.k3s[:, :], ALU.add).then_inc(s_bd, 1)
        dve.wait_ge(s_kve, 2)


CTX_READY = 4


def spread_keys(k):
    nc = k.nc
    k.s_keys0, k.s_keys3 = k.sem("keys0_spread"), k.sem("keys3_spread")

    @k.block.gpsimd
    def _(pool):
        pool.wait_ge(k.s_k0T, 1)
        pool.wait_ge(k.s_ctx_ready, CTX_READY)
        for b in range(B):
            nc.gpsimd.tensor_tensor(k.kbd0[:, b, :, :], k.k0T[:, b * N:(b + 1) * N].unsqueeze(1).to_broadcast([P, H0, N]),
                                    const(k, "head0").unsqueeze(2).to_broadcast([P, H0, N]), ALU.mult).then_inc(k.s_keys0, 1)
        for b in range(B):
            nc.gpsimd.tensor_tensor(k.kbd3[:, b, :, :], k.k3T[:, b * N:(b + 1) * N].unsqueeze(1).to_broadcast([P, H3, N]),
                                    const(k, "head3").unsqueeze(2).to_broadcast([P, H3, N]), ALU.mult).then_inc(k.s_keys3, 1)


def attention0(k, s_xT):
    nc, cs = k.nc, k.csem
    s_q, s_qe = cs("a0_q"), cs("a0_q_out")
    s_sc, s_se = cs("a0_scores"), cs("a0_scores_out")
    s_top, s_nb, s_e = cs("a0_topk"), cs("a0_negmax"), cs("a0_exp")
    s_m, s_p, s_t, s_te = cs("a0_taken"), cs("a0_probs"), cs("a0_probsT"), cs("a0_probsT_out")
    s_pv, s_ct = cs("a0_pv"), cs("a0_ctxT")
    s_o, s_oe, s_x, s_vb, s_rd = cs("a0_out"), cs("a0_out_copied"), cs("a0_x"), cs("a0_vspread"), cs("a0_rden")
    scale = HD0 ** -0.5
    ROUNDS = TOPK // 8
    PER = 2 * ROUNDS * H0

    def loop(engine, body):
        body(0, False, True)
        with engine.Fori(1, B - 1) as b:
            body(b, True, True)
        body(B - 1, True, False)

    @k.block.tensor
    def _(pe):
        ps = k.ps

        def project_q(b):
            done(pe, s_qe, b)
            nc.tensor.matmul(ps[:, 0, 0:S], k.wa0[:, 0, :], k.xT[:, bass.ds(b * S, S)],
                             start=True, stop=True).then_inc(s_q, 1)

        def scores(b, tt):
            done(pe, s_qe, b + 1)
            pe.wait_ge(k.s_keys0, b + 1)
            done(pe, s_se, 2 * b + tt)
            for c in range(2):
                mm = nc.tensor.matmul(ps[:, 1 + c, :], k.qT[:, tt * P:(tt + 1) * P],
                                      k.kbd0[:, bass.ds(b, 1), 8 * c:8 * c + 8, :], start=True, stop=True)
            mm.then_inc(s_sc, 1)

        def transposes(b, tt):
            done(pe, s_p, 2 * b + tt + 1)
            done(pe, s_te, 2 * b + tt)
            for j in range(8):
                mm = nc.tensor.transpose(ps[:, 3 + j // 4, (j % 4) * P:(j % 4 + 1) * P],
                                         k.prob[:, tt, 2 * j:2 * j + 2, :], const(k, "ident"))
            mm.then_inc(s_t, 1)

        pe.wait_ge(k.s_ctx_ready, CTX_READY)
        s_xT(pe)
        project_q(0)
        scores(0, 0)

        def out(b):
            done(pe, s_ct, b + 1)
            done(pe, s_oe, b)
            for tt in range(TB):
                nc.tensor.matmul(ps[:, 6, tt * D:(tt + 1) * D], k.ctxT[:, tt * P:(tt + 1) * P], k.wa0[:, 3, :],
                                 start=True, stop=False)
                mm = nc.tensor.matmul(ps[:, 6, tt * D:(tt + 1) * D], k.ones[0:1, 0:P], rows(k, "bo0")[0:1, :],
                                      start=False, stop=True)
            mm.then_inc(s_o, 1)

        def body(b, before, more):
            scores(b, 1)
            if more:
                project_q(b + 1)
                scores(b + 1, 0)
            if before:
                out(b - 1)
            transposes(b, 0)
            transposes(b, 1)
            done(pe, s_te, 2 * b + 2)
            done(pe, s_vb, b + 1)
            done(pe, s_ct, b)
            for j in range(8):
                nc.tensor.matmul(ps[:, 5, 0:S], k.vbd[:, j, :], k.probT[:, j, :], start=(j == 0), stop=(j == 7))
            for j in range(8):
                mm = nc.tensor.matmul(ps[:, 5, S:2 * S], const(k, "pair0")[:, j * P:(j + 1) * P], k.probT[:, j, :],
                                      start=(j == 0), stop=(j == 7))
            mm.then_inc(s_pv, 1)

        loop(pe, body)
        out(B - 1)

    @k.block.scalar
    def _(act):
        def q_out(b):
            done(act, s_q, b + 1)
            nc.scalar.activation(k.qT[:, :], k.ps[:, 0, 0:S], ACT.Identity, bias=vec(k, "bq0"), scale=1.0).then_inc(s_qe, 1)

        def probsT_out(b, tt):
            done(act, s_t, 2 * b + tt + 1)
            done(act, s_pv, b)
            nc.scalar.activation(k.probT[:, :, tt * P:(tt + 1) * P],
                                 k.ps[:, 3:5, :].rearrange("p a (j q) -> p (a j) q", q=P), ACT.Copy).then_inc(s_te, 1)

        q_out(0)
        done(act, s_sc, 1)
        nc.scalar.activation(k.sc[:, 0, :, :], k.ps[:, 1:3, :].rearrange("p a (h n) -> p (a h) n", n=N),
                             ACT.Copy).then_inc(s_se, 1)

        def out(b):
            done(act, s_o, b + 1)
            done(act, s_x, b)
            nc.scalar.activation(k.y[:, :, :], k.ps[:, 6, 0:S].rearrange("p (t d) -> p t d", t=TB),
                                 ACT.Copy).then_inc(s_oe, 1)

        def body(b, before, more):
            load_table(k, ACT.Exp)
            done(act, s_sc, 2 * b + 2)
            done(act, s_top, 2 * b * PER)
            copy_scores(1)
            exps_tile(b, 0)
            if more:
                q_out(b + 1)
                done(act, s_sc, 2 * b + 3)
                done(act, s_top, (2 * b + 1) * PER)
                copy_scores(0)
            if before:
                out(b - 1)
            exps_tile(b, 1)
            probsT_out(b, 0)
            probsT_out(b, 1)

        def copy_scores(tt):
            nc.scalar.activation(k.sc[:, tt, :, :], k.ps[:, 1:3, :].rearrange("p a (h n) -> p (a h) n", n=N),
                                 ACT.Copy).then_inc(s_se, 1)

        def exps_tile(b, tt):
            done(act, s_nb, 2 * b + tt + 1)
            done(act, s_se, 2 * b + tt + 1)
            done(act, s_p, 2 * b + tt - 1)
            for h in range(H0):
                i = nc.scalar.activation(k.ex[:, tt, h, :], k.sc[:, tt, h, :], ACT.Exp, scale=scale,
                                         bias=k.nb[:, tt, h:h + 1])
            i.then_inc(s_e, 1)

        loop(act, body)
        out(B - 1)

    @k.block.vector
    def _(dve):
        def tile(b, tt):
            base = (2 * b + tt) * PER
            done(dve, s_nb, 2 * b + tt - 1)
            done(dve, s_p, 2 * b + tt - 1)
            done(dve, s_se, 2 * b + tt + 1, k.turn_dve)
            for r in range(ROUNDS):
                src = k.sc if r == 0 else k.w
                top = k.top1[:, tt, :, :] if r == 0 else k.top[:, :, :]
                if r:
                    done(dve, s_top, base + 2 * r * H0, k.turn_dve)
                for h in range(H0):
                    nc.vector.max(top[:, h, :], src[:, tt, h, :]).then_inc(s_top, 1)
                done(dve, s_top, base + (2 * r + 1) * H0, k.turn_dve)
                for h in range(H0):
                    nc.vector.match_replace(k.w[:, tt, h, :], top[:, h, :], src[:, tt, h, :],
                                            imm_value=NEG).then_inc(s_top, 1)

        def finish(b):
            done(dve, s_pv, b + 1)
            nc.vector.reciprocal(k.rden[:, :], k.ps[:, 5, S:2 * S]).then_inc(s_rd, 1)
            done(dve, s_rd, b + 1)
            done(dve, s_o, b)
            nc.vector.tensor_tensor(k.ctxT[:, :], k.ps[:, 5, 0:S], k.rden[:, :], ALU.mult).then_inc(s_ct, 1)

        tile(0, 0)
        tile(0, 1)
        with dve.Fori(1, B) as b:
            tile(b, 0)
            finish(b - 1)
            tile(b, 1)
        done(dve, s_p, 2 * B - 1)
        done(dve, s_top, 2 * B * PER)
        done(dve, s_e, 2 * B)
        nc.vector.scalar_tensor_tensor(k.prob[:, 1, :, :], k.w[:, 1, :, :], NEG / 2, k.ex[:, 1, :, :],
                                       ALU.is_lt, ALU.mult).then_inc(s_p, 1)
        finish(B - 1)
        done(dve, s_x, B)

    @k.block.gpsimd
    def _(pool):
        def add(b):
            done(pool, s_oe, b + 1)
            xb = k.X[:, bass.ds(b * TB, TB), :]
            nc.gpsimd.tensor_tensor(xb, xb, k.y[:, :, :], ALU.add).then_inc(s_x, 1)

        def body(b, before, more):
            done(pool, s_pv, b)
            nc.gpsimd.tensor_tensor(k.vbd[:, :, :], k.v0[:, bass.ds(b, 1), :].to_broadcast([P, 8, D]),
                                    const(k, "pair0").rearrange("p (j d) -> p j d", j=8), ALU.mult).then_inc(s_vb, 1)
            for tt in range(TB):
                done(pool, s_top, (2 * b + tt) * PER + H0, k.turn_pool)
                nc.gpsimd.tensor_scalar(k.nb[:, tt, :], k.top1[:, tt, :, 0], -scale, None, ALU.mult).then_inc(s_nb, 1)
                if not more and tt == 1:
                    continue
                done(pool, s_t, 2 * b + tt - 1)
                done(pool, s_top, (2 * b + tt + 1) * PER, k.turn_pool)
                nc.gpsimd.tensor_scalar(k.w[:, tt, :, :], k.w[:, tt, :, :], NEG / 2, None, ALU.is_lt).then_inc(s_m, 1)
                done(pool, s_m, 2 * b + tt + 1)
                done(pool, s_e, 2 * b + tt + 1)
                nc.gpsimd.tensor_tensor(k.prob[:, tt, :, :], k.w[:, tt, :, :], k.ex[:, tt, :, :], ALU.mult).then_inc(s_p, 1)
                if before and tt == 0:
                    add(b - 1)

        loop(pool, body)
        add(B - 1)
    return lambda e, t=0: done(e, s_x, B)


def router(k, layer, s_xT):
    nc = k.nc
    (s_l, b_l), (s_e, b_e) = k.shared("router_logits", 1), k.shared("router_exp", 1)
    (s_sub, b_sub), (s_c, b_c) = k.shared("router_shifted", 1), k.shared("router_comb", 1)
    bias = {0: "rb0", 1: "br1"}.get(layer)

    @k.block.tensor
    def _(pe):
        for t in range(T):
            s_xT(pe, t // TB)
            mm = nc.tensor.matmul(k.ps[:, 7, t * E:(t + 1) * E], k.xT[:, t * P:(t + 1) * P], k.wr[:, layer, :],
                                  start=True, stop=True)
        mm.then_inc(s_l, 1)

    @k.block.scalar
    def _(act):
        load_table(k, ACT.Exp)
        act.wait_ge(s_sub, b_sub + 1)
        nc.scalar.activation(k.pr[:, :, :], k.pr[:, :, :], ACT.Exp).then_inc(s_e, 1)

    @k.block.vector
    def _(dve):
        st = k.steps(dve)
        v = nc.vector
        dve.wait_ge(s_l, b_l + 1)
        logits_ps = k.ps[:, 7, 0:T * E].rearrange("p (t e) -> p t e", e=E)
        if bias:
            st.add(v.tensor_tensor(k.lg[:, :, :], logits_ps, rows(k, bias).unsqueeze(1).to_broadcast([P, T, E]), ALU.add))
        else:
            st.add(v.tensor_copy(k.lg[:, :, :], logits_ps))
        st.wait()
        for t in range(T):
            st.add(v.max(k.mx[:, t, :], k.lg[:, t, :]))
        st.wait()
        v.tensor_tensor(k.pr[:, :, :], k.lg[:, :, :], k.mx[:, :, 0:1].to_broadcast([P, T, E]), ALU.subtract).then_inc(s_sub, 1)
        for t in range(T):
            st.add(v.max_index(k.ix[:, t, :], k.mx[:, t, :], k.lg[:, t, :]))
        st.wait()
        st.add(v.tensor_copy(k.ixf[:, :, :], k.ix[:, :, 0:2]))
        st.wait()
        iota = const(k, "iota8").unsqueeze(1).to_broadcast([P, T, E])
        hit = lambda out, n: st.add(v.tensor_tensor(out, iota, k.ixf[:, :, n:n + 1].to_broadcast([P, T, E]), ALU.is_equal))
        hit(k.comb[:, :, :], 0)
        hit(k.oh[:, :, :], 1)
        st.wait()
        if layer in (0, 2):
            st.add(v.tensor_tensor(k.comb[:, :, :], k.comb[:, :, :], k.oh[:, :, :], ALU.add))
            st.wait()
        dve.wait_ge(s_e, b_e + 1)
        if layer in (0, 3):
            st.add(v.tensor_reduce(k.sm[:, :], k.pr[:, :, :], AX, ALU.add))
        if layer != 1:
            st.add(v.tensor_tensor(k.comb[:, :, :], k.comb[:, :, :], k.pr[:, :, :], ALU.mult))
            st.wait()
            if layer == 2:
                st.add(v.tensor_reduce(k.sm[:, :], k.comb[:, :, :], AX, ALU.add))
                st.wait()
            st.add(v.reciprocal(k.sm[:, :], k.sm[:, :]))
            st.wait()
            if layer == 3:
                st.add(v.tensor_scalar(k.sm[:, :], k.sm[:, :], 2.0, None, ALU.mult))
                st.wait()
            st.add(v.tensor_tensor(k.comb[:, :, :], k.comb[:, :, :], k.sm[:, :].unsqueeze(2).to_broadcast([P, T, E]), ALU.mult))
            st.wait()
        if layer == 3:
            st.add(v.memset(k.comb[:, :, E - 1], 1.0))
            st.wait()
        dve.sem_inc(s_c, 1)
    return lambda e: e.wait_ge(s_sub, b_sub + 1), lambda e: e.wait_ge(s_c, b_c + 1)



def split_product(nc, out, terms):
    passes = [p for wh, wl, xh, xl in terms for p in ((wh, xl), (wl, xh), (wh, xh))]
    for n, (w, x) in enumerate(passes):
        mm = nc.tensor.matmul(out, w, x, start=(n == 0), stop=(n == len(passes) - 1))
    return mm


def split_input(k, s_xT):
    nc = k.nc
    (s_hi, b_hi), (s_lo, b_lo) = k.shared("xT_high", 2), k.shared("xT_low", 2)
    cols = lambda half: slice(half * 512, (half + 1) * 512)

    @k.block.scalar
    def _(act):
        for half in range(2):
            s_xT(act, TB * half + 1)
            nc.scalar.activation(k.xTh[:, cols(half)], k.xT[:, cols(half)], ACT.Copy).then_inc(s_hi, 1)

    @k.block.vector
    def _(dve):
        for half in range(2):
            dve.wait_ge(s_hi, b_hi + half + 1)
            nc.vector.tensor_tensor(k.xTl[:, cols(half)], k.xT[:, cols(half)], k.xTh[:, cols(half)].bitcast(F32),
                                    ALU.subtract).then_inc(s_lo, 1)
    return lambda e, half=1: e.wait_ge(s_lo, b_lo + half + 1)


def split_step(k, pool, w, high, low, s_high, count, s_split):
    k.nc.gpsimd.tensor_copy(high, w).then_inc(s_high, 1)
    pool.wait_ge(s_high, count)
    k.nc.gpsimd.tensor_tensor(low, w, high.bitcast(F32), ALU.subtract).then_inc(s_split, 1)


def split_first_weights(k, layer, n):
    tag = f"f{layer}"
    s_w, s_ws = [k.sem(f"{tag}_w0"), k.sem(f"{tag}_w1")], k.csem(f"{tag}_w_split")
    s_hi, b_hi = k.shared("weights_high", E)

    @k.block.gpsimd
    def _(pool):
        for j in range(2):
            pool.wait_ge(s_w[j], 16)
            split_step(k, pool, k.wf[:, j, 0:n], k.wh[:, j, 0:n], k.wfl[:, j, 0:n], s_hi, b_hi + j + 1, s_ws)
    return s_w, s_ws, s_hi, b_hi


def split_weights(k, first, n):
    s_w, s_ws, s_hi, b_hi = first

    @k.block.gpsimd
    def _(pool):
        with pool.Fori(1, E // 2) as i:
            for j in range(2):
                pool.wait_ge(s_w[j], 16 * i + 16)
                pool.sem_inc(k.turn_pool, 1)
                split_step(k, pool, k.wf[:, j, 0:n], k.wh[:, j, 0:n], k.wfl[:, j, 0:n], s_hi, b_hi + 2 * i + j + 1, s_ws)
    return s_w, s_ws


def down_product(k, pe, w, h, half, s_dn):
    for tt in range(HALF):
        for f in range(FC):
            mm = k.nc.tensor.matmul(k.ps[:, 4 + half, tt * P:(tt + 1) * P], h[:, half, f, tt * P:(tt + 1) * P],
                                    w(f), start=(f == 0), stop=(f == FC - 1))
    mm.then_inc(s_dn, 1)


def accumulate(k, dve, s_dn, s_acc, u, half, e):
    done(dve, s_dn, u + 1)
    done(dve, s_acc, HALF * (u - 1))
    for tt in range(HALF):
        t = HALF * half + tt
        k.nc.vector.scalar_tensor_tensor(k.X[:, t, :], k.ps[:, 4 + half, tt * P:(tt + 1) * P],
                                         k.comb[:, t, bass.ds(e, 1)], k.X[:, t, :], ALU.mult, ALU.add).then_inc(s_acc, 1)


def summed(s_acc):
    n = 2 * E * HALF
    return lambda e, t=T - 1: done(e, s_acc, n - HALF if t < HALF else n - T + t + 1)


def expert_biases(k, bias, comb_ready, s_acc):
    nc = k.nc
    (s_t, b_t), (s_te, b_te) = k.shared("bias_combT", 2), k.shared("bias_combT_out", 2)
    (s_b, b_b), (s_x, b_x) = k.shared("bias_product", 2), k.shared("bias_x", 2)

    @k.block.tensor
    def _(pe):
        comb_ready(pe)
        for half in range(2):
            for tt in range(HALF):
                mm = nc.tensor.transpose(k.ps[0:E, 6 + half, tt * P:(tt + 1) * P], k.comb[:, HALF * half + tt, :],
                                         const(k, "ident"))
            mm.then_inc(s_t, 1)
        for half in range(2):
            pe.wait_ge(s_te, b_te + half + 1)
            for tt in range(HALF):
                t = HALF * half + tt
                mm = nc.tensor.matmul(k.ps[:, half, tt * P:(tt + 1) * P], k.combT[:, t * P:(t + 1) * P],
                                      bias, start=True, stop=True)
            mm.then_inc(s_b, 1)

    @k.block.scalar
    def _(act):
        for half in range(2):
            act.wait_ge(s_t, b_t + half + 1)
            nc.scalar.activation(k.combT[:, half * 512:(half + 1) * 512], k.ps[0:E, 6 + half, :], ACT.Copy).then_inc(s_te, 1)

    @k.block.vector
    def _(dve):
        summed(s_acc)(dve)
        for half in range(2):
            dve.wait_ge(s_b, b_b + half + 1)
            x = k.X[:, HALF * half:HALF * (half + 1), :]
            nc.vector.tensor_tensor(x, x, k.ps[:, half, :].rearrange("p (t d) -> p t d", d=D), ALU.add).then_inc(s_x, 1)
    return lambda e, t=T - 1: e.wait_ge(s_x, b_x + t // HALF + 1)


def load_experts(k, weights, before, s_w, s_dn):
    n = weights.shape[2]

    @k.block.sync
    def _(sp):
        give(k, sp)
        before(sp)
        for j in range(2):
            sp.dma_start(k.wf[:, j, 0:n], weights[j, :, :]).then_inc(s_w[j], 16)
        with sp.Fori(1, E // 2) as i:
            for j in range(2):
                done(sp, s_dn, 4 * i + 2 * j - 2)
                sp.dma_start(k.wf[:, j, 0:n], weights[bass.ds(2 * i + j, 1), :, :].rearrange("e p n -> (e p) n"))\
                    .then_inc(s_w[j], 16)


def give(k, sp):
    for s in k.credited:
        sp.sem_inc(s, CREDIT)
    k.credited.clear()


def ffn(k, layer, s_xT, before, first, func, bias1):
    nc = k.nc
    tag = f"f{layer}"
    s_up, s_h, s_acc = k.csem(f"{tag}_up"), k.csem(f"{tag}_h"), k.csem(f"{tag}_acc")
    s_dn = k.csem(f"{tag}_down")
    s_w, s_ws = split_weights(k, first, F)
    x_split = split_input(k, s_xT)
    _, comb_ready = router(k, layer, s_xT)

    @k.block.tensor
    def _(pe):
        with pe.Fori(0, E // 2) as i:
            def up(j, half):
                u = 4 * i + 2 * j + half
                if j == 0:
                    x_split(pe, half)
                cols = slice(half * 512, (half + 1) * 512)
                if half == 0:
                    done(pe, s_ws, 2 * i + j + 1)
                for f in range(FC):
                    done(pe, s_h, 4 * u + f - 3)
                    w = slice(f * P, (f + 1) * P)
                    split_product(nc, k.ps[:, f, :], [(k.wh[:, j, w], k.wfl[:, j, w], k.xTh[:, cols], k.xTl[:, cols])])\
                        .then_inc(s_up, 1)

            def down(j, half):
                u = 4 * i + 2 * j + half
                done(pe, s_acc, HALF * (u - 1))
                done(pe, s_h, 4 * u + FC)
                down_product(k, pe, lambda f: k.wf[:, j, F + f * P:F + (f + 1) * P], k.h, half, s_dn)
            up(0, 0)
            up(0, 1)
            down(0, 0)
            up(1, 0)
            down(0, 1)
            up(1, 1)
            down(1, 0)
            down(1, 1)

    @k.block.scalar
    def _(act):
        with act.Fori(0, E // 2) as i:
            load_table(k, func)
            for ju in range(4):
                for f in range(FC):
                    done(act, s_up, 16 * i + 4 * ju + f + 1, k.turn_act if bias1 else None)
                    b = k.vecs[:, bass.ds(VEC[bias1][0] + (2 * i + ju // 2) * FC + f, 1)] if bias1 else 0.0
                    nc.scalar.activation(k.h[:, ju % 2, f, :], k.ps[:, f, :], func, bias=b, scale=1.0).then_inc(s_h, 1)

    @k.block.vector
    def _(dve):
        with dve.Fori(0, E // 2) as i:
            for ju in range(4):
                accumulate(k, dve, s_dn, s_acc, 4 * i + ju, ju % 2, 2 * i + ju // 2)
    load_experts(k, k.d[f"wf{layer}"], before, s_w, s_dn)
    return expert_biases(k, k.bias2[:, 0:D], comb_ready, s_acc) if layer == 1 else summed(s_acc)


def attention12(k, layer, s_xT):
    nc, cs = k.nc, lambda n: k.csem(f"a{layer}_{n}")
    NP = 4 if layer == 1 else 8
    NH, KEYS, W = 2 * NP, S + N, NP * P
    scale = 64 ** -0.5
    w, cT = (k.wa1, k.c1T) if layer == 1 else (k.wa2, k.c2T)
    wq, wk, wv = (lambda j, a=a: w[:, a + j * P:a + (j + 1) * P] for a in (0, W, 2 * W))
    wo_at = 3 * W if layer == 2 else 4 * W
    s_wa = k.s_wa[layer]
    s_in = cs("inputs")
    s_pa, s_pae, s_pd, s_pde = cs("proj_act"), cs("proj_act_out"), cs("proj_dve"), cs("proj_dve_out")
    s_s, s_mx, s_e, s_rc, s_pn = cs("scores"), cs("negmax"), cs("exp"), cs("recip"), cs("probs")
    s_t, s_ta, s_tb = cs("probsT"), cs("probsT_a"), cs("probsT_b")
    s_pv, s_ot, s_o, s_x, s_rot = cs("pv"), cs("oT"), cs("out"), cs("x"), cs("rope")
    act_jobs = [("q", g, 0) for g in range(NP // 2)] + [("v", c, g) for c in range(3) for g in range(NP // 4)]
    dve_jobs = [("k", j, 0) for j in range(NP)] + ([("swap", 0, 0)] if layer == 1 else [])
    NA, ND, NQ = len(act_jobs), len(dve_jobs), NP // 2
    abank = lambda n: 2 * (n % 2) if n < NQ else 4 + n % 2
    dbank = lambda n: 2 * (n % 2) + 1

    @k.block.gpsimd
    def _(pool):
        with pool.Fori(0, B) as b:
            s_xT(pool, b)
            pool.sem_inc(k.turn_pool, 1)
            done(pool, s_pd, ND * b)
            done(pool, s_pa, NA * b, k.turn_pool)
            nc.gpsimd.tensor_copy(k.at[:, 0:S], k.xT[:, bass.ds(b * S, S)]).then_inc(s_in, 1)
            nc.gpsimd.tensor_copy(k.at[:, S:KEYS], cT[:, bass.ds(b * N, N)]).then_inc(s_in, 1)

    @k.block.tensor
    def _(pe):
        pe.wait_ge(s_wa, 16)
        s_xT(pe)
        with pe.Fori(0, B) as b:
            done(pe, s_in, 2 * b + 2)

            def act_job(n):
                kind, x, g = act_jobs[n]
                done(pe, s_pae, NA * b + n - 1)
                if kind == "q":
                    for jj in range(2):
                        mm = nc.tensor.matmul(k.ps[:, abank(n), jj * S:(jj + 1) * S], wq(2 * x + jj), k.at[:, 0:S],
                                              start=True, stop=True)
                else:
                    rows_ = P if x < 2 else N
                    mm = nc.tensor.matmul(k.ps[0:rows_, abank(n), :], k.at[:, x * P:x * P + rows_],
                                          w[:, 2 * W + g * 512:2 * W + (g + 1) * 512], start=True, stop=True)
                mm.then_inc(s_pa, 1)

            def dve_job(n):
                kind, j, _ = dve_jobs[n]
                done(pe, s_pde, ND * b + n - 1)
                if kind == "k":
                    mm = nc.tensor.matmul(k.ps[:, dbank(n), 0:KEYS], wk(j), k.at[:, :], start=True, stop=True)
                else:
                    for j in range(NP):
                        mm = nc.tensor.matmul(k.ps[:, dbank(n), j * N:(j + 1) * N], w[:, 3 * W + j * P:3 * W + (j + 1) * P],
                                              k.at[:, S:KEYS], start=True, stop=True)
                mm.then_inc(s_pd, 1)
            for n in range(ND):
                dve_job(n)
                if n < NQ:
                    act_job(n)

            def scores(j):
                for m in range(4):
                    qt, hh = m // 2, m % 2
                    if hh == 0:
                        done(pe, s_e, 4 * (NP * b + j) + m - 2)
                    mm = nc.tensor.matmul(k.ps[:, m, 0:KEYS], k.aq[64 * hh:64 * hh + 64, j, qt * P:(qt + 1) * P],
                                          k.ak[64 * hh:64 * hh + 64, j, :], start=True, stop=(layer == 1))
                    if layer == 1:
                        mm.then_inc(s_s, 1)
                if layer == 2:
                    for m in range(4):
                        nc.tensor.matmul(k.ps[:, m, S:KEYS], k.ones16[0:1, :], k.mask16[0:1, bass.ds(b * N, N)],
                                         start=False, stop=True).then_inc(s_s, 1)

            def transposes(j):
                done(pe, s_ta, 2 * (NP * b + j))
                done(pe, s_tb, NP * b + j)
                if j == 0:
                    done(pe, s_pae, NA * b + NA)
                for m in range(4):
                    qt, hh = m // 2, m % 2
                    done(pe, s_pn, 4 * (NP * b + j) + m + 1)
                    prob = k.ap[:, 4 * (j % 2) + m, :]
                    for c in range(2):
                        nc.tensor.transpose(k.ps[:, 4 + hh, c * S + qt * P:c * S + (qt + 1) * P],
                                            prob[:, c * P:(c + 1) * P], const(k, "ident"))
                    mm = nc.tensor.transpose(k.ps[0:N, 6, hh * S + qt * P:hh * S + (qt + 1) * P], prob[:, S:KEYS],
                                             const(k, "ident"))
                mm.then_inc(s_t, 1)

            def pv(j):
                done(pe, s_ta, 2 * (NP * b + j) + 2)
                done(pe, s_tb, NP * b + j + 1)
                done(pe, s_ot, NP * b + j)
                for c in range(3):
                    rows_ = P if c < 2 else N
                    for hh in range(2):
                        h = 2 * j + hh
                        mm = nc.tensor.matmul(k.ps[64 * hh:64 * hh + 64, 7, 0:S], k.av[0:rows_, c, h * 64:(h + 1) * 64],
                                              k.apt[0:rows_, j % 2, hh, c, :], start=(c == 0), stop=(c == 2))
                mm.then_inc(s_pv, 1)

            done(pe, s_pae, NA * b + NQ)
            done(pe, s_pde, ND * b + ND)
            if layer == 1:
                done(pe, s_rot, b + 1)
            scores(0)
            done(pe, s_x, b)
            for n in range(NQ, NA):
                act_job(n)
            for j in range(NP):
                if j + 1 < NP:
                    scores(j + 1)
                transposes(j)
                if j:
                    pv(j - 1)
            pv(NP - 1)
            done(pe, s_ot, NP * (b + 1))
            for qt in range(TB):
                for j in range(NP):
                    mm = nc.tensor.matmul(k.ps[:, 4, qt * D:(qt + 1) * D], k.aot[:, j, qt * P:(qt + 1) * P],
                                          w[:, wo_at + j * D:wo_at + (j + 1) * D], start=(j == 0), stop=(j == NP - 1))
            mm.then_inc(s_o, 1)

    @k.block.scalar
    def _(act):
        with act.Fori(0, B) as b:
            load_table(k, ACT.Exp)
            def projected(n):
                kind, x, g = act_jobs[n]
                done(act, s_pa, NA * b + n + 1)
                if kind == "q":
                    nc.scalar.activation(k.aq[:, 2 * x:2 * x + 2, :], k.ps[:, abank(n), :].rearrange("p (j q) -> p j q", j=2),
                                         ACT.Copy, scale=scale).then_inc(s_pae, 1)
                else:
                    rows_ = P if x < 2 else N
                    nc.scalar.activation(k.av[0:rows_, x, g * 512:(g + 1) * 512], k.ps[0:rows_, abank(n), :],
                                         ACT.Copy).then_inc(s_pae, 1)

            for n in range(NQ):
                projected(n)

            def exps(j):
                done(act, s_t, NP * b + j - 1)
                for m in range(4):
                    slot = 4 * (j % 2) + m
                    done(act, s_mx, 4 * (NP * b + j) + m + 1)
                    nc.scalar.activation(k.ap[:, slot, :], k.ps[:, m, 0:KEYS], ACT.Exp, bias=k.anm[:, slot:slot + 1],
                                         scale=1.0, accum_out=k.asm[:, slot:slot + 1]).then_inc(s_e, 1)

            def oT(j):
                done(act, s_pv, NP * b + j + 1)
                nc.scalar.activation(k.aot[:, j, :], k.ps[:, 7, 0:S], ACT.Copy).then_inc(s_ot, 1)

            exps(0)
            for n in range(NQ, NA):
                projected(n)
            for j in range(NP):
                if j + 1 < NP:
                    exps(j + 1)
                done(act, s_t, NP * b + j + 1)
                for hh in range(2):
                    nc.scalar.activation(k.apt[:, j % 2, hh, 0:2, :], k.ps[:, 4 + hh, :].rearrange("p (c q) -> p c q", c=2),
                                         ACT.Copy).then_inc(s_ta, 1)
                if j:
                    oT(j - 1)
            oT(NP - 1)

    @k.block.vector
    def _(dve):
        v = nc.vector
        with dve.Fori(0, B) as b:
            for n, (kind, j, _) in enumerate(dve_jobs):
                done(dve, s_pd, ND * b + n + 1)
                if kind == "swap":
                    bc = lambda name: const(k, name).unsqueeze(1).to_broadcast([P, NP, N])
                    v.tensor_tensor(k.arot[:, :, :], k.ps[:, dbank(n), 0:NP * N].rearrange("p (j n) -> p j n", n=N), bc("sin1"),
                                    ALU.mult).then_inc(s_pde, 1)
                    done(dve, s_pde, ND * b + n + 1)
                    kc = k.ak[:, 0:NP, S:KEYS]
                    v.tensor_tensor(kc, kc, k.arot[:, :, :], ALU.add).then_inc(s_rot, 1)
                elif layer == 1:
                    v.tensor_copy(k.ak[:, j, 0:S], k.ps[:, dbank(n), 0:S])
                    v.tensor_tensor(k.ak[:, j, S:KEYS], k.ps[:, dbank(n), S:KEYS], const(k, "cos1"), ALU.mult).then_inc(s_pde, 1)
                else:
                    v.tensor_copy(k.ak[:, j, :], k.ps[:, dbank(n), 0:KEYS]).then_inc(s_pde, 1)

            def maxes(j):
                for m in range(4):
                    slot = 4 * (j % 2) + m
                    done(dve, s_s, 4 * (NP * b + j) + m + 1)
                    v.tensor_reduce(k.anm[:, slot:slot + 1], k.ps[:, m, 0:KEYS], AX, ALU.max, negate=True)\
                        .then_inc(s_mx, 1)

            def normal(j):
                sums = k.asm[:, 4 * (j % 2):4 * (j % 2) + 4]
                done(dve, s_e, 4 * (NP * b + j) + 4)
                v.reciprocal(sums, sums).then_inc(s_rc, 1)
                done(dve, s_rc, NP * b + j + 1)
                for m in range(4):
                    slot = 4 * (j % 2) + m
                    v.tensor_scalar(k.ap[:, slot, :], k.ap[:, slot, :], k.asm[:, slot:slot + 1], None,
                                    ALU.mult).then_inc(s_pn, 1)

            maxes(0)
            normal(0)
            for j in range(NP):
                if j + 1 < NP:
                    maxes(j + 1)
                done(dve, s_t, NP * b + j + 1)
                v.tensor_copy(k.apt[0:N, j % 2, :, 2, :], k.ps[0:N, 6, :].rearrange("p (h q) -> p h q", h=2)).then_inc(s_tb, 1)
                if j + 1 < NP:
                    normal(j + 1)
            done(dve, s_o, b + 1)
            x = k.X[:, bass.ds(b * TB, TB), :]
            v.tensor_tensor(x, x, k.ps[:, 4, 0:S].rearrange("p (t d) -> p t d", d=D), ALU.add).then_inc(s_x, 1)
        done(dve, s_x, B)
    give_credits(k)
    return lambda e, t=0: done(e, s_x, B)


def attention3(k, s_xT):
    nc, cs = k.nc, lambda n: k.csem(f"a3_{n}")
    s_q, s_rs, s_rot = cs("q"), cs("rope_steps"), cs("rope")
    s_s, s_mx, s_sh, s_e, s_sm, s_p = cs("scores"), cs("negmax"), cs("shifted"), cs("exp"), cs("sums"), cs("probs")
    s_t, s_te, s_vb, s_pv, s_c, s_o, s_x = (cs(n) for n in ("probsT", "probsT_out", "vspread", "pv", "ctxT", "out", "x"))
    TURNS, NB = B // 2, 2
    SCORES = (1, 2, 7, 5)
    tiled = lambda a: a.rearrange("p (h n) -> p h n", n=N)

    @k.block.tensor
    def _(pe):
        s_xT(pe)
        pe.wait_ge(k.s_keys3, B)
        with pe.Fori(0, TURNS) as i:
            done(pe, s_rot, i)
            for n in range(2):
                mm = nc.tensor.matmul(k.ps[:, 6 * n, :], k.wa0[:, 4 + n, :], k.xT[:, bass.ds(i * NB * S, NB * S)],
                                      start=True, stop=True)
            mm.then_inc(s_q, 1)
            done(pe, s_sh, HALF * i)
            done(pe, s_c, NB * i)
            done(pe, s_x, i)
            done(pe, s_rot, i + 1)
            for t in range(HALF):
                b = bass.ds(NB * i + t // TB, 1)
                nc.tensor.matmul(k.ps[:, SCORES[t], 0:H3 * N], k.q3[:, t * P:(t + 1) * P], k.kbd3[:, b, :, :],
                                 start=True, stop=False)
                for h in range(H3):
                    mm = nc.tensor.matmul(k.ps[:, SCORES[t], h * N:(h + 1) * N], k.ones16[0:1, :],
                                          k.mask16[0:1, bass.ds((NB * i + t // TB) * N, N)],
                                          start=False, stop=(h == H3 - 1))
                mm.then_inc(s_s, 1)
            done(pe, s_te, NB * i)
            for bb in range(NB):
                for tt in range(TB):
                    done(pe, s_p, HALF * i + TB * bb + tt + 1)
                    for j in range(2):
                        mm = nc.tensor.transpose(k.ps[:, 3 + bb, j * S + tt * P:j * S + (tt + 1) * P],
                                                 k.p3[:, TB * bb + tt, 2 * j:2 * j + 2, :], const(k, "ident"))
                mm.then_inc(s_t, 1)
            done(pe, s_vb, i + 1)
            for bb in range(NB):
                done(pe, s_te, NB * i + bb + 1)
                for j in range(2):
                    mm = nc.tensor.matmul(k.ps[:, 1 + bb, 0:S], k.vbd3[:, bb, j, :], k.p3T[:, j, bb * S:(bb + 1) * S],
                                          start=(j == 0), stop=(j == 1))
                mm.then_inc(s_pv, 1)
            for bb in range(NB):
                done(pe, s_c, NB * i + bb + 1)
                for t in range(TB * bb, TB * bb + TB):
                    mm = nc.tensor.matmul(k.ps[:, 7, t * D:(t + 1) * D], k.ctxT3[:, t * P:(t + 1) * P], k.wa0[:, 9, :],
                                          start=True, stop=True)
            mm.then_inc(s_o, 1)

    @k.block.scalar
    def _(act):
        with act.Fori(0, TURNS) as i:
            load_table(k, ACT.Exp)
            for t in range(HALF):
                done(act, s_sh, HALF * i + t + 1)
                nc.scalar.activation(k.p3[:, t, :, :], k.p3[:, t, :, :], ACT.Exp).then_inc(s_e, 1)
            done(act, s_pv, NB * i)
            for bb in range(NB):
                done(act, s_t, NB * i + bb + 1)
                nc.scalar.activation(k.p3T[:, :, bb * S:(bb + 1) * S], k.ps[:, 3 + bb, :].rearrange("p (j q) -> p j q", j=2),
                                     ACT.Copy).then_inc(s_te, 1)
            done(act, s_o, i)
            for bb in range(NB):
                done(act, s_pv, NB * i + bb + 1)
                nc.scalar.activation(k.ctxT3[:, bb * S:(bb + 1) * S], k.ps[:, 1 + bb, 0:S], ACT.Copy).then_inc(s_c, 1)

    @k.block.vector
    def _(dve):
        v = nc.vector
        batched = lambda a: a.rearrange("p (b q) -> p b q", b=NB)
        table = lambda name: const(k, name).unsqueeze(1).to_broadcast([P, NB, S])
        with dve.Fori(0, TURNS) as i:
            done(dve, s_s, HALF * i)
            done(dve, s_q, i + 1)
            v.scalar_tensor_tensor(batched(k.q3[:, :]), batched(k.ps[:, 0, :]), HD3 ** -0.5, table("cosq3"),
                                   ALU.mult, ALU.mult).then_inc(s_rs, 1)
            v.scalar_tensor_tensor(batched(k.q3s[:, :]), batched(k.ps[:, 6, :]), HD3 ** -0.5, table("sinq3"),
                                   ALU.mult, ALU.mult).then_inc(s_rs, 1)
            done(dve, s_rs, 2 * i + 2)
            v.tensor_tensor(k.q3[:, :], k.q3[:, :], k.q3s[:, :], ALU.add).then_inc(s_rot, 1)
            done(dve, s_t, NB * i)
            for t in range(HALF):
                done(dve, s_s, HALF * i + t + 1)
                v.tensor_reduce(k.m3[:, t, :], tiled(k.ps[:, SCORES[t], 0:H3 * N]), AX, ALU.max).then_inc(s_mx, 1)
                done(dve, s_mx, HALF * i + t + 1)
                v.tensor_tensor(k.p3[:, t, :, :], tiled(k.ps[:, SCORES[t], 0:H3 * N]),
                                k.m3[:, t, :].unsqueeze(2).to_broadcast([P, H3, N]), ALU.subtract).then_inc(s_sh, 1)
            for bb in range(NB):
                sums = 3 * (NB * i + bb)
                for t in range(TB * bb, TB * bb + TB):
                    done(dve, s_e, HALF * i + t + 1)
                    v.tensor_reduce(k.m3[:, t, :], k.p3[:, t, :, :], AX, ALU.add).then_inc(s_sm, 1)
                done(dve, s_sm, sums + 2)
                m = k.m3[:, TB * bb:TB * (bb + 1), :]
                v.reciprocal(m, m).then_inc(s_sm, 1)
                done(dve, s_sm, sums + 3)
                for t in range(TB * bb, TB * bb + TB):
                    v.tensor_tensor(k.p3[:, t, :, :], k.p3[:, t, :, :],
                                    k.m3[:, t, :].unsqueeze(2).to_broadcast([P, H3, N]), ALU.mult).then_inc(s_p, 1)
            done(dve, s_o, i + 1)
            x = k.X[:, bass.ds(i * HALF, HALF), :]
            v.tensor_tensor(x, x, k.ps[:, 7, :].rearrange("p (t d) -> p t d", d=D), ALU.add).then_inc(s_x, 1)
        done(dve, s_x, TURNS)

    @k.block.gpsimd
    def _(pool):
        s_xT(pool)
        with pool.Fori(0, TURNS) as i:
            done(pool, s_pv, NB * i)
            for bb in range(NB):
                op = nc.gpsimd.tensor_tensor(k.vbd3[:, bb, :, :], k.v3[:, bass.ds(NB * i + bb, 1), :].to_broadcast([P, 2, D]),
                                             const(k, "pair3").rearrange("p (j d) -> p j d", j=2), ALU.mult)
            op.then_inc(s_vb, 1)
    give_credits(k)
    return lambda e, t=T - 1: done(e, s_x, t // HALF + 1)


def add_first(k):
    @k.block.vector
    def _(dve):
        st = k.steps(dve)
        v = k.nc.vector
        first = k.z[:, 0, 0:2, :].rearrange("p a (t d) -> p (a t) d", d=D)
        dve.wait_ge(k.s_first, 1)
        for t in range(T):
            st.add(v.tensor_scalar(first[:, t, :], k.X[:, t, :], k.mv[:, t, 0:1], k.r1[:, t:t + 1],
                                   ALU.subtract, ALU.mult))
        st.wait()
        st.add(v.tensor_tensor(k.X[:, :, :], k.X[:, :, :], first, ALU.add))
        st.wait()


SPEC = {"0": (0, 2048), "1a": (2048, 3072), "1b": (3072, 4096), "2": (4096, 6144)}


def ffn2_first_weights(k):
    s_w, s_ws, s_wss = [k.sem("f2_w0"), k.sem("f2_w1")], k.csem("f2_w_split"), k.csem("f2_spec_split")
    s_sw = {n: k.sem(f"f2_spec_{n}_loaded") for n in SPEC}
    s_wh = k.sem("f2_split_high")

    @k.block.gpsimd
    def _(pool):
        a, b = SPEC["0"]
        pool.wait_ge(s_w[0], 16)
        split_step(k, pool, k.wf[:, 0, 0:F], k.wh[:, 0, 0:F], k.wfl[:, 0, 0:F], s_wh, 1, s_ws)
        pool.wait_ge(s_sw["0"], 16)
        split_step(k, pool, k.ws2[:, a:b], k.ws2h[:, a:b], k.ws2l[:, a:b], s_wh, 2, s_wss)
    return s_w, s_ws, s_wss, s_sw, s_wh


def ffn2(k, s_xT, before, first):
    nc, cs = k.nc, lambda n: k.csem(f"f2_{n}")
    GROUPS = 2
    s_w, s_ws, s_wss, s_sw, s_wh = first
    s_dn = cs("down")
    s_up, s_h, s_acc = cs("products"), cs("h"), cs("acc")
    s_z, s_za, s_st, s_mv, s_r, s_rp, s_zn = (cs(n) for n in ("z", "z_out", "z_stats", "z_moments", "z_rstd", "z_rstd_steps", "z_normed"))
    at = SPEC
    spec = {n: (k.ws2h[:, a:b], k.ws2l[:, a:b]) for n, (a, b) in at.items()}
    s_hi, s_lo = cs("h_high"), cs("h_low")
    x_split = split_input(k, s_xT)
    add_first(k)
    logits_read, comb_ready = router(k, 2, s_xT)

    order = ["U00", "U01", "Z00", "Z01", "U10", "U11", "R00", "R01", "D00", "D01", "A10", "A11", "Z10", "Z11",
             "U20", "U21", "R10", "R11", "D10", "D11", "S20", "S21", "U30", "D20", "U31", "D21", "D30", "D31"]
    jobs = [(o[0], int(o[1]), int(o[2])) for o in order]
    banks = {"U": 4, "R": 4, "A": 2, "S": 4}
    index, last, before_bank, n = {}, {}, {}, 0
    for job in jobs:
        if job[0] in banks:
            for f in range(banks[job[0]]):
                index[job + (f,)] = n
                before_bank[job + (f,)] = last.get(f)
                last[f] = n
                n += 1
    PER = n
    for key, v in before_bank.items():
        if v is None:
            before_bank[key] = last[key[3]] - PER
    low, LOWS = {}, 0
    for job in [("U", 0, 0), ("U", 0, 1), ("U", 1, 0), ("U", 1, 1), ("A", 1, 0), ("A", 1, 1), ("U", 2, 0), ("U", 2, 1)]:
        LOWS += banks[job[0]]
        low[job] = LOWS
    downs = [j for j in jobs if j[0] == "D"]
    zs = [j for j in jobs if j[0] == "Z"]

    @k.block.tensor
    def _(pe):
        pe_ = nc.tensor
        x_split(pe)
        with pe.Fori(0, GROUPS) as i:
            for job in jobs:
                kind, e, half = job
                cols = slice(half * 512, (half + 1) * 512)
                wf = lambda a, c: k.wf[:, e % 2, a + c * P:a + (c + 1) * P]

                def product(f, terms):
                    done(pe, s_h, PER * i + before_bank[job + (f,)] + 1)
                    split_product(nc, k.ps[:, f, :], terms).then_inc(s_up, 1)

                if kind == "U":
                    if half == 0:
                        done(pe, s_ws, 4 * i + e + 1)
                    for f in range(FC):
                        product(f, [(k.wh[:, e % 2, f * P:(f + 1) * P], k.wfl[:, e % 2, f * P:(f + 1) * P], k.xTh[:, cols], k.xTl[:, cols])])
                elif kind in "AS":
                    name = "1a" if kind == "A" else "2"
                    width = 256 if kind == "A" else F
                    done(pe, s_wss, 4 * i + list(at).index(name) + 1)
                    done(pe, s_lo, LOWS * i + low["U", e, half])
                    wh, wl = spec[name]
                    for f in range(banks[kind]):
                        product(f, [(wh[:, c * width + f * P:c * width + (f + 1) * P],
                                     wl[:, c * width + f * P:c * width + (f + 1) * P],
                                     k.hh[:, half, c, :], k.hl[:, half, c, :]) for c in range(FC)])
                elif kind == "Z":
                    logits_read(pe)
                    name, chunks, hh, hl = ("0", FC, k.hh, k.hl) if e == 0 else ("1b", 2, k.t1h, k.t1l)
                    done(pe, s_wss, 4 * i + list(at).index(name) + 1)
                    done(pe, s_lo, LOWS * i + low["U" if e == 0 else "A", e, half])
                    wh, wl = spec[name]
                    for tt in range(4):
                        n = 16 * i + 4 * zs.index(job) + tt
                        done(pe, s_za, n - 1)
                        tok = slice(tt * P, (tt + 1) * P)
                        split_product(nc, k.ps[:, 6 + tt % 2, :],
                                      [(hh[:, half, c, tok], hl[:, half, c, tok],
                                        wh[:, c * F:(c + 1) * F], wl[:, c * F:(c + 1) * F]) for c in range(chunks)])\
                            .then_inc(s_z, 1)
                elif kind == "R":
                    z = zs.index(("Z", e, half))
                    done(pe, s_zn, 16 * i + 4 * z + 4)
                    for f in range(FC):
                        done(pe, s_h, PER * i + before_bank[job + (f,)] + 1)
                        for tt in range(4):
                            mm = pe_.transpose(k.ps[:, f, tt * P:(tt + 1) * P], k.z[:, half, tt, f * P:(f + 1) * P],
                                               const(k, "ident"))
                        mm.then_inc(s_up, 1)
                else:
                    d = downs.index(job)
                    src = index[({0: "R", 1: "R", 2: "S", 3: "U"}[e], e, half, FC - 1)]
                    h = k.h if e == 3 else k.h2
                    done(pe, s_acc, HALF * (8 * i + d - 1))
                    done(pe, s_h, PER * i + src + 1)
                    down_product(k, pe, lambda f: wf(F, f), h, half, s_dn)

    @k.block.scalar
    def _(act):
        a = nc.scalar.activation
        with act.Fori(0, GROUPS) as i:
            load_table(k, ACT.Gelu)
            for job in jobs:
                kind, e, half = job
                if kind not in banks:
                    continue
                v = lambda name, per, f: k.vecs[:, bass.ds(VEC[name][0] + per * i + f, 1)]
                for f in range(banks[kind]):
                    done(act, s_up, PER * i + index[job + (f,)] + 1, k.turn_act)
                    src = k.ps[:, f, :]
                    if kind == "U":
                        m = a(k.h[:, half, f, :], src, ACT.Gelu, bias=v("up_b", 4 * FC, e * FC + f), scale=1.0)
                    elif kind == "A":
                        m = a(k.t1[:, half, f, :], src, ACT.Gelu, bias=v("s1a_b", 2, f), scale=1.0)
                    elif kind == "S":
                        m = a(k.h2[:, half, f, :], src, ACT.Gelu, bias=v("s2_b", FC, f), scale=1.0)
                    elif e == 0:
                        m = a(k.h2[:, half, f, :], src, ACT.Gelu, bias=v("ln0_b", FC, f), scale=v("ln0_g", FC, f))
                    else:
                        m = a(k.h2[:, half, f, :], src, ACT.Identity, bias=v("ln1_b", FC, f), scale=v("ln1_g", FC, f))
                    m.then_inc(s_h, 1)

    @k.block.vector
    def _(dve):
        v = nc.vector
        dve.wait_ge(k.s_rows, 16)
        with dve.Fori(0, GROUPS) as i:
            def stats(job):
                z = zs.index(job)
                _, e, half = job
                name = "s0_b" if e == 0 else "s1b_b"
                for tt in range(4):
                    n = 16 * i + 4 * z + tt
                    done(dve, s_z, n + 1)
                    v.tensor_tensor(k.z[:, half, tt, :], k.ps[:, 6 + tt % 2, :],
                                    k.rowv[:, bass.ds(ROW[name][0] + F * i, F)], ALU.add).then_inc(s_za, 1)
                for tt in range(4):
                    n = 16 * i + 4 * z + tt
                    done(dve, s_za, n + 1)
                    v.bn_stats(k.stat[:, tt, :], k.z[:, half, tt, :]).then_inc(s_st, 1)
                done(dve, s_st, 16 * i + 4 * z + 4, k.turn_dve)
                for tt in range(4):
                    v.bn_aggr(k.mv[:, 4 * half + tt, :], k.stat[:, tt, :]).then_inc(s_mv, 1)

            def norm(job):
                z = zs.index(job)
                half = job[2]
                done(dve, s_r, 4 * i + z + 1)
                for tt in range(4):
                    t = 4 * half + tt
                    v.tensor_scalar(k.z[:, half, tt, :], k.z[:, half, tt, :], k.mv[:, t, 0:1], k.r1[:, t:t + 1],
                                    ALU.subtract, ALU.mult).then_inc(s_zn, 1)

            def lows(kind, e, half):
                h, hl, hh = (k.h, k.hl, k.hh) if kind == "U" else (k.t1, k.t1l, k.t1h)
                n = banks[kind]
                first = LOWS * i + low[kind, e, half] - n
                for f in range(n + 1):
                    if f < n:
                        done(dve, s_h, PER * i + index[kind, e, half, f] + 1)
                        v.tensor_copy(hh[:, half, f, :], h[:, half, f, :]).then_inc(s_hi, 1)
                    if f == 0:
                        continue
                    f -= 1
                    done(dve, s_hi, first + f + 1)
                    v.tensor_tensor(hl[:, half, f, :], h[:, half, f, :], hh[:, half, f, :].bitcast(F32),
                                    ALU.subtract).then_inc(s_lo, 1)

            for e in range(4):
                if e == 1:
                    for half in range(2):
                        lows("A", 1, half)
                if e == 0:
                    for half in range(2):
                        lows("U", 0, half)
                if e < 2:
                    for half in range(2):
                        stats(("Z", e, half))
                    for half in range(2):
                        norm(("Z", e, half))
                if e < 2:
                    for half in range(2):
                        lows("U", e + 1, half)
                for half in range(2):
                    accumulate(k, dve, s_dn, s_acc, 8 * i + 2 * e + half, half, 4 * i + e)


    @k.block.gpsimd
    def _(pool):
        gp = nc.gpsimd
        count = [2]

        def split(high, x, low, counter):
            count[0] += 1
            split_step(k, pool, x, high, low, s_wh, count[0], counter)

        def expert(i, e):
            pool.wait_ge(s_w[e % 2], 32 * i + 16 * (e // 2 + 1))
            split(k.wh[:, e % 2, 0:F], k.wf[:, e % 2, 0:F], k.wfl[:, e % 2, 0:F], s_ws)

        def special(i, name):
            a, b = at[name]
            pool.wait_ge(s_sw[name], 16 * i + 16)
            split(k.ws2h[:, a:b], k.ws2[:, a:b], k.ws2l[:, a:b], s_wss)

        def rstd(i, e):
            for half in range(2):
                z = zs.index(("Z", e, half))
                r = k.r1[:, 4 * half:4 * half + 4]
                done(pool, s_mv, 16 * i + 4 * z + 4)
                gp.tensor_scalar(r, k.mv[:, 4 * half:4 * half + 4, 1], EPS, None, ALU.add).then_inc(s_rp, 1)
                done(pool, s_rp, 4 * i + z + 1)
                gp.tensor_tensor(r, r, k.mhalf[:, 0:4], ALU.pow).then_inc(s_r, 1)

        for i in range(GROUPS):
            expert(i, 1)
            rstd(i, 0)
            special(i, "1a")
            special(i, "1b")
            expert(i, 2)
            rstd(i, 1)
            special(i, "2")
            expert(i, 3)
            if i + 1 < GROUPS:
                special(i + 1, "0")
                expert(i + 1, 0)


    @k.block.sync
    def _(sp):
        give(k, sp)
        wf = k.d["wf2"]
        for n, (a, b) in at.items():
            sp.dma_start(k.ws2[:, a:b], k.d["ws2"][0, :, a:b]).then_inc(s_sw[n], 16)
        before(sp)
        for j in range(2):
            sp.dma_start(k.wf[:, j, 0:2 * F], wf[j, :, :]).then_inc(s_w[j], 16)
        for e in range(2, E):
            done(sp, s_dn, 2 * e - 2)
            sp.dma_start(k.wf[:, e % 2, 0:2 * F], wf[e, :, :]).then_inc(s_w[e % 2], 16)
            if e in (2, 3, 4):
                for n in {2: ("0",), 3: ("1a", "1b"), 4: ("2",)}[e]:
                    a, b = at[n]
                    sp.dma_start(k.ws2[:, a:b], k.d["ws2"][1, :, a:b]).then_inc(s_sw[n], 16)
    return expert_biases(k, k.bias2[:, D:2 * D], comb_ready, s_acc)


def ffn3(k, s_xT, before, first):
    nc, cs = k.nc, lambda n: k.csem(f"f3_{n}")
    s_dn = cs("down")
    s_up, s_g, s_h, s_acc = cs("up"), cs("gate"), cs("h"), cs("acc")
    s_w, s_ws = split_weights(k, first, 2 * F)
    x_split = split_input(k, s_xT)
    router(k, 3, s_xT)

    @k.block.tensor
    def _(pe):
        with pe.Fori(0, E // 2) as i:
            def up(j, half):
                u = 4 * i + 2 * j + half
                if j == 0:
                    x_split(pe, half)
                cols = slice(half * 512, (half + 1) * 512)
                if half == 0:
                    done(pe, s_ws, 2 * i + j + 1)
                for f in range(FC):
                    done(pe, s_h, 4 * u + f - 1)
                    for g in (1, 0):
                        w = slice(g * F + f * P, g * F + (f + 1) * P)
                        mm = split_product(nc, k.ps[:, 2 * (f % 2) + g, :],
                                           [(k.wh[:, j, w], k.wfl[:, j, w], k.xTh[:, cols], k.xTl[:, cols])])
                    mm.then_inc(s_up, 1)

            def down(j, half):
                u = 4 * i + 2 * j + half
                done(pe, s_acc, HALF * (u - 1))
                done(pe, s_h, 4 * u + FC)
                down_product(k, pe, lambda f: k.wf[:, j, 2 * F + f * P:2 * F + (f + 1) * P], k.h, half, s_dn)
            up(0, 0)
            up(0, 1)
            down(0, 0)
            up(1, 0)
            down(0, 1)
            up(1, 1)
            down(1, 0)
            down(1, 1)

    @k.block.scalar
    def _(act):
        with act.Fori(0, E // 2) as i:
            load_table(k, ACT.Silu)
            for ju in range(4):
                for f in range(FC):
                    n = 16 * i + 4 * ju + f
                    done(act, s_up, n + 1)
                    done(act, s_h, n - 1)
                    nc.scalar.activation(k.gate[:, f % 2, :], k.ps[:, 2 * (f % 2) + 1, :], ACT.Silu).then_inc(s_g, 1)

    @k.block.vector
    def _(dve):
        with dve.Fori(0, E // 2) as i:
            def hidden(ju):
                for f in range(FC):
                    n = 16 * i + 4 * ju + f
                    done(dve, s_g, n + 1)
                    nc.vector.tensor_tensor(k.h[:, ju % 2, f, :], k.ps[:, 2 * (f % 2), :], k.gate[:, f % 2, :],
                                            ALU.mult).then_inc(s_h, 1)

            def add(ju):
                accumulate(k, dve, s_dn, s_acc, 4 * i + ju, ju % 2, 2 * i + ju // 2)
            hidden(0)
            hidden(1)
            add(0)
            hidden(2)
            add(1)
            hidden(3)
            add(2)
            add(3)
    load_experts(k, k.d["wf3"], before, s_w, s_dn)
    return summed(s_acc)


def program(nc, d):
    with ExitStack() as ctx:
        k = State()
        k.nc, k.d, k.credited = nc, d, []
        sb = lambda name, shape, dt=F32: ctx.enter_context(nc.sbuf_tensor(name, shape, dt))

        def two(name, shape, shape_r=None, scope=ctx):
            with nc.sbuf_tensor(name, shape, F32) as a:
                pass
            return a, scope.enter_context(nc.sbuf_tensor(f"{name}_r", shape_r or shape, F32R))
        k.sem = lambda name: ctx.enter_context(nc.semaphore(name))

        def csem(name):
            s = k.sem(name)
            k.credited.append(s)
            return s
        k.csem = csem
        shared = {}

        def shared_sem(name, total):
            if name not in shared:
                shared[name] = [k.sem(name), 0]
            sem, base = shared[name]
            shared[name][1] += total
            return sem, base
        k.shared = shared_sem
        own = {}

        def steps(engine):
            key = "pool" if "GpSimd" in type(engine).__name__ or "Pool" in type(engine).__name__ else "dve"
            if key not in own:
                own[key] = Steps(k.sem(f"{key}_steps"))
            own[key].engine = engine
            return own[key]
        k.steps = steps

        k.ps = ctx.enter_context(nc.psum_tensor("ps", [P, 8, 512], F32))
        k.X = sb("x_res", [P, T, D])
        k.xh, k.xTh = two("xhat", [P, T, D], [P, T * P])
        k.xT = sb("xT", [P, T * P])
        k.ctx = sb("ctx_sb", [P, 2, D])
        k.consts = sb("consts_sb", [P, NCONST])
        k.vecs = sb("vecs_sb", [P, NVEC])
        k.rowv = sb("rows_sb", [P, NROW])
        k.bias2 = sb("bias2_sb", [E, 2 * D])
        k.wr = sb("wr_sb", [P, 4, E])
        k.wa0 = sb("wa0_sb", [P, 10, P])
        k.mask_u8 = sb("mask_u8", [1, B * N], U8)
        k.maskf = sb("maskf", [1, B * N])
        k.mask16 = sb("mask_sb", [1, B * N], BF16)
        k.ones16 = sb("ones16", [1, P], BF16)
        k.columns, k.column = sb("columns", [P, 16]), 0
        k.mhalf = sb("mhalf", [P, 8])
        k.ones = sb("ones", [1, 512])
        k.stat = sb("stat", [P, T, 6])
        k.mv = sb("mv", [P, T, 2])
        k.r1 = sb("r1", [P, T])
        k.r2 = sb("r2", [P, T])
        k.rms1 = sb("rms1", [P, 1])
        k.c1T, k.c2T, k.c3T, k.k3T = (sb(n, [P, B * N]) for n in ("c1T", "c2T", "c3T", "k3T"))
        k.v3 = sb("v3", [P, B, D])
        k.kbd3 = sb("kbd3", [P, B, H3, N])
        k.ctxT = sb("ctxT", [P, S])

        k.wa2, k.hh = two("wa_sb", [P, 32 * P], [P, 2, FC, 512])
        k.wa1 = k.wa2[:, 0:20 * P]
        k.ws2, k.ws2l = two("ws2_sb", [P, 12 * F])
        k.wf, k.wfl = two("wf_sb", [P, 2, 3 * F])
        k.lg, k.pr, k.comb, k.oh, k.mx = (sb(n, [P, T, E]) for n in ("r_lg", "r_pr", "r_comb", "r_oh", "r_mx"))
        k.ix = sb("r_ix", [P, T, 8], U32)
        k.ixf = sb("r_ixf", [P, T, 2])
        k.sm = sb("r_sm", [P, T])

        with ExitStack() as c0:
            s0 = lambda name, shape, dt=F32: c0.enter_context(nc.sbuf_tensor(name, shape, dt))
            k.sc = s0("a0_sc", [P, TB, H0, N])
            k.w = s0("a0_w", [P, TB, H0, N])
            k.ex = s0("a0_ex", [P, TB, H0, N])
            k.prob = s0("a0_prob", [P, TB, H0, N])
            k.probT = s0("a0_probT", [P, 8, S])
            k.vbd = s0("a0_vbd", [P, 8, D])
            k.top1 = s0("a0_top1", [P, TB, H0, 8])
            k.top = s0("a0_top", [P, H0, 8])
            k.nb = s0("a0_nb", [P, TB, H0])
            k.y = s0("a0_y", [P, TB, D])
            k.qT = s0("a0_qT", [P, S])
            k.rden = s0("a0_rden", [P, S])
            k.dup3 = s0("dup3", [P, B, 2, N])
            k.c0T, k.k0T, k.k3s = (s0(n, [P, B * N]) for n in ("c0T", "k0T", "k3s"))
            k.dup = s0("dup", [P, B, 2, N])
            k.v0 = s0("v0", [P, B, D])
            k.kbd0 = s0("kbd0", [P, B, H0, N])
        with ExitStack() as c1:
            s1 = lambda name, shape, dt=F32: c1.enter_context(nc.sbuf_tensor(name, shape, dt))
            k.h, k.hl = two("f_h", [P, 2, FC, 512], None, c1)
            k.xTl = s1("f_xT_low", [P, T * P], F32R)
            k.t1h = s1("f2_t1_high", [P, 2, 2, 512], F32R)
            k.h2 = s1("f2_h2", [P, 2, FC, 512])
            k.t1, k.t1l = two("f2_t1", [P, 2, 2, 512], None, c1)
            k.z = s1("f2_z", [P, 2, 4, F])
            k.ws2h = s1("f2_ws_high", [P, 12 * F], F32R)
            k.wh = s1("f_w_high", [P, 2, 2 * F], F32R)
            k.gate = k.z[:, 0, :, :]
            k.combT = k.z[0:E, 0, 0:2, :].rearrange("e a n -> e (a n)")
        with ExitStack() as c2:
            s2 = lambda name, shape, dt=F32: c2.enter_context(nc.sbuf_tensor(name, shape, dt))
            k.q3, k.q3s, k.ctxT3 = (s2(f"a3_{n}", [P, 2 * S]) for n in ("q", "qs", "ctxT"))
            k.p3 = s2("a3_p", [P, HALF, H3, N])
            k.p3T = s2("a3_pT", [P, 2, 2 * S])
            k.vbd3 = s2("a3_vbd", [P, 2, 2, D])
            k.m3 = s2("a3_m", [P, HALF, H3])
        with ExitStack() as c3:
            s3 = lambda name, shape, dt=F32: c3.enter_context(nc.sbuf_tensor(name, shape, dt))
            k.at = s3("a_in", [P, S + N])
            k.aq = s3("a_q", [P, 8, S])
            k.ak = s3("a_k", [P, 8, S + N])
            k.av = s3("a_v", [P, 3, 8 * P])
            k.ap = s3("a_probs", [P, 8, S + N])
            k.apt = s3("a_probsT", [P, 2, 2, 3, S])
            k.aot = s3("a_oT", [P, 8, S])
            k.arot = s3("a_rot", [P, 4, N])
            k.anm = s3("a_negmax", [P, 8])
            k.asm = s3("a_sums", [P, 8])
        k.block = ctx.enter_context(nc.Block())
        s_out = k.sem("out_stored")
        load_constants(k)
        context(k)
        s_xT = normalize(k, lambda e, t: e.wait_ge(k.s_x, 16))
        spread_keys(k)
        first = split_first_weights(k, 0, F)
        ready = attention0(k, s_xT)
        give_credits(k)
        s_xT = normalize(k, ready)
        ready = ready_ff = ffn(k, 0, s_xT, lambda e: None, first, ACT.Gelu, None)
        s_xT = normalize(k, ready, second=EPS, xT_scale=vec(k, "gl1"), xT_bias=vec(k, "bl1"))
        ready = attention12(k, 1, s_xT)
        @k.block.scalar
        def _(act, ready=ready):
            ready(act)
            act.dma_start(k.wa2[:, :], d["wa2"]).then_inc(k.s_wa[2], 16)
        first = split_first_weights(k, 1, F)
        s_xT = normalize(k, ready)
        ready = ready_ff = ffn(k, 1, s_xT, ready_ff, first, ACT.Relu, "b1_1")
        s_xT = normalize(k, ready, second=EPS, xT_scale=vec(k, "g2_2"), xT_bias=vec(k, "b2_2"))
        ready = attention12(k, 2, s_xT)
        first = ffn2_first_weights(k)
        s_xT = normalize(k, ready, second=EPS, xT_scale=vec(k, "ln_g"), xT_bias=vec(k, "ln_b"), keep_first=True)
        ready = ready_ff = ffn2(k, s_xT, ready_ff, first)
        s_xT = normalize(k, ready, second=1e-6, xT_scale=k.rms1[:, 0:1])
        ready = attention3(k, s_xT)
        first = split_first_weights(k, 3, 2 * F)
        s_xT = normalize(k, ready)
        ready = ffn3(k, s_xT, ready_ff, first)
        give_credits(k)

        @k.block.sync
        def _(sp):
            ready(sp)
            sp.dma_start(d["out"].rearrange("(t p) d -> p t d", p=P), k.X[:, :, :]).then_inc(s_out, 16)
            sp.wait_ge(s_out, 16)


def constants():
    p = np.arange(P)
    c = np.zeros((P, NCONST), np.float32)

    def put(name, a):
        c[:, CONST[name][0]:CONST[name][1]] = a
    put("ident", np.eye(P))
    col = np.arange(D)
    put("pair0", np.concatenate([(col[None] // HD0 == 2 * j + p[:, None] // N) for j in range(8)], 1))
    put("pair3", np.concatenate([(col[None] // HD3 == 2 * j + p[:, None] // N) for j in range(2)], 1))
    put("head0", p[:, None] // HD0 == np.arange(H0)[None])
    put("head3", p[:, None] // HD3 == np.arange(H3)[None])
    put("iota8", np.arange(E)[None])

    def rope(dim, freq, pos):
        half = dim // 2
        ang = (pos[None, :].astype(np.float32) * freq[(p % dim) % half][:, None]).astype(np.float32)
        sign = np.where(p % dim < half, -1.0, 1.0)[:, None]
        return np.cos(ang), np.sin(ang) * sign
    f1 = (1.0 / 10000.0 ** (np.arange(0, 64, 2, dtype=np.float32) / 64)).astype(np.float32)
    a, b = rope(64, f1, np.arange(N))
    put("cos1", a), put("sin1", b)
    f3 = (1.0 / 10000.0 ** (np.float32(2.0 / 32) * np.arange(16, dtype=np.float32))).astype(np.float32)
    a, b = rope(32, f3, np.arange(N, N + S))
    put("cosq3", a), put("sinq3", b)
    a, b = rope(32, f3, np.arange(N))
    put("cosk3", a), put("sink3", b)
    return c


def swap_halves(w, dim):
    a = w.reshape(w.shape[0], -1, 2, dim // 2)
    return np.ascontiguousarray(a[:, :, ::-1]).reshape(w.shape)


def layout(i):
    g = {n: np.asarray(a) for n, a in i.items()}
    c = constants()
    col = lambda a: a.reshape(-1, P).T
    vecs = {"bq0": g["L0_xattn_bq"], "bk0": g["L0_xattn_bk"], "gx1": g["L1_xattn_gamma_x"], "bx1": g["L1_xattn_beta_x"],
            "gl1": g["L1_xattn_gamma_l"], "bl1": g["L1_xattn_beta_l"], "b1_1": g["L1_ffn_b1"],
            "g1_2": g["L2_xattn_g1"], "b1_2": g["L2_xattn_b1"], "g2_2": g["L2_xattn_g2"], "b2_2": g["L2_xattn_b2"],
            "ln_g": g["L2_ffn_ln_g"], "ln_b": g["L2_ffn_ln_b"], "up_b": g["L2_ffn_up_b"],
            "ln0_g": g["L2_ffn_ln0_g"], "ln0_b": g["L2_ffn_ln0_b"], "s1a_b": g["L2_ffn_spec1a_b"],
            "ln1_g": g["L2_ffn_ln1_g"], "ln1_b": g["L2_ffn_ln1_b"], "s2_b": g["L2_ffn_spec2_b"],
            "rms": g["L3_xattn_rms_scale"]}
    rows_ = {"bv0": g["L0_xattn_bv"], "bo0": g["L0_xattn_bo"], "rb0": g["L0_ffn_router_b"], "br1": g["L1_ffn_br"],
             "s0_b": g["L2_ffn_spec0_b"], "s1b_b": g["L2_ffn_spec1b_b"]}
    kv = g["L3_xattn_kv_w"][:, 0]
    q3 = g["L3_xattn_q_w"].transpose(1, 0, 2).reshape(D, D)
    k3, v3 = np.tile(kv[0], (1, H3)), np.tile(kv[1], (1, H3))
    wa0 = np.stack([g["L0_xattn_Wq"].T, g["L0_xattn_Wk"].T, g["L0_xattn_Wv"].T, g["L0_xattn_Wo"].T,
                    q3, swap_halves(q3, HD3), k3, swap_halves(k3, HD3), v3, g["L3_xattn_out_w"].reshape(D, D)], 1)
    wr = np.stack([g["L0_ffn_router_w"], g["L1_ffn_Wr"].T, g["L2_ffn_router_w"], g["L3_ffn_Wr"]], 1)
    a = {"x": g["x"].reshape(B * S, D), "ctx": g["ctx_1024"].reshape(B * N, D),
         "mask": g["mask_BxS2_bk0"].reshape(1, B * N), "consts": c,
         "bias2": np.concatenate([g["L1_ffn_b2"], g["L2_ffn_down_b"]], 1),
         "vecs": np.concatenate([col(vecs[n]) for n in VEC], 1), "rows": np.concatenate([rows_[n].reshape(-1) for n in ROW]),
         "wa0": wa0, "wr": wr}
    up = lambda w: w
    down = lambda w: w.reshape(-1, w.shape[1] // P, P, w.shape[2]).transpose(0, 2, 1, 3).reshape(w.shape[0], P, -1)
    a["wf0"] = np.concatenate([up(g["L0_ffn_expert_up"].transpose(0, 2, 1)), down(g["L0_ffn_expert_down"].transpose(0, 2, 1))], 2)
    a["wf1"] = np.concatenate([up(g["L1_ffn_W1"].transpose(0, 2, 1)), down(g["L1_ffn_W2"].transpose(0, 2, 1))], 2)
    rows_of = lambda w: w.reshape(-1, P, w.shape[1]).transpose(1, 0, 2).reshape(P, -1)
    wkv1 = g["L1_xattn_Wkv"]
    a["wa1"] = np.concatenate([g["L1_xattn_Wq"], wkv1, swap_halves(wkv1[:, :512], 64), rows_of(g["L1_xattn_Wo"])], 1)
    a["wa2"] = np.concatenate([g["L2_xattn_Wq"], g["L2_xattn_Wkv"], rows_of(g["L2_xattn_Wout"])], 1)
    a["wf2"] = np.concatenate([g["L2_ffn_up_W"], down(g["L2_ffn_down_W"])], 2)
    a["ws2"] = np.concatenate([down(g["L2_ffn_spec0_W"]), down(g["L2_ffn_spec1a_W"]), down(g["L2_ffn_spec1b_W"]),
                               down(g["L2_ffn_spec2_W"])], 2)
    cat = lambda w, s: np.concatenate([w, s[None]], 0)
    a["wf3"] = np.concatenate([cat(g["L3_ffn_Wu"], g["L3_ffn_Wu_s"]), cat(g["L3_ffn_Wg"], g["L3_ffn_Wg_s"]),
                               down(cat(g["L3_ffn_Wd"], g["L3_ffn_Wd_s"]))], 2)
    return {n: np.ascontiguousarray(v) for n, v in a.items()}


def kernel(**inputs):
    import concourse.bacc as _bacc
    from concourse.bass_utils import run_bass_kernel_spmd as _run

    nc = _bacc.Bacc("TRN2", target_bir_lowering=False, num_devices=1)
    a = layout(inputs)
    arrays, d = {}, {}
    for n, v in a.items():
        arrays[f"{n}_dram"] = v
        d[n] = nc.dram_tensor(f"{n}_dram", v.shape, mybir.dt.from_np(v.dtype), kind="ExternalInput").ap()
    d["out"] = nc.dram_tensor("out_dram", (B * S, D), F32, kind="ExternalOutput").ap()
    program(nc, d)
    r = _run(nc, [arrays], core_ids=[0])
    return r.results[0]["out_dram"].reshape(B, S, D)
```
